# Optimizing a Trainium2 kernel written in Bass

```python
import numpy as np
import jax
import jax.numpy as jnp

def _softmax(x, axis=-1):
    return jax.nn.softmax(x, axis=axis)

def _gelu(x):
    return jax.nn.gelu(x, approximate=True)

def _silu(x):
    return jax.nn.silu(x)

def _sigmoid(x):
    return jax.nn.sigmoid(x)

def _layernorm(x, axis=-1, eps=1e-05):
    m = jnp.mean(x, axis=axis, keepdims=True)
    v = jnp.var(x, axis=axis, keepdims=True)
    return (x - m) / jnp.sqrt(v + eps)

def _scatter_add(tgt, idx, src, axis=0):
    return tgt.at[idx].add(src)

def _segment_sum(src, seg, n):
    return jax.ops.segment_sum(src, seg, n)
kernel_name = 'mk_adj_ffn_d1_adj_r2_4d13cf'

def setup_inputs(seed: int=0):
    np.random.seed(seed)
    _w = jnp.asarray

    def _rec_inputs():
        import jax
        import jax.numpy as jnp
        _gk = jax.random.key(seed)
        x = 7.22e-05 + 1 * jax.random.normal(jax.random.fold_in(_gk, 1), (16, 512, 128), jnp.float32)
        _w = (1.0 + jnp.arange(512, dtype=jnp.float32)) ** (-0.5)
        _w = _w / _w.mean()
        _pij = jnp.clip(0.0078125 * _w[:, None] * _w[None, :], 0.0, 1.0)
        _a = jax.random.uniform(jax.random.fold_in(_gk, 2), (512, 512)) < _pij
        _a = jnp.logical_or(_a, jnp.swapaxes(_a, -1, -2))
        _a = jnp.logical_or(_a, jnp.eye(512, dtype=bool))
        _af = _a.astype(jnp.float32)
        _af = _af * jax.random.uniform(jax.random.fold_in(_gk, 3), (512, 512), jnp.float32, 0.05, 0.000976562)
        adj = _af
        return (x, adj)
    x, adj = _rec_inputs()

    def _L0_gnn_setup():
        import jax, jax.numpy as jnp
        import numpy as np
        N_STEPS = 8
        SPATIAL_SCALE = 1.0
        key = jax.random.key(seed)
        ks = jax.random.split(key, 6)
        B, N, D = (32, 512, 128)
        x = jax.random.normal(ks[0], (B, N, D), dtype=jnp.float32)
        adj_mx = jax.random.uniform(ks[1], (N, N), dtype=jnp.float32) / N
        alpha_train = jnp.ones((N,), dtype=jnp.float32)
        w = jnp.eye(D, dtype=jnp.float32) + 0.01 * jax.random.normal(ks[2], (D, D), dtype=jnp.float32)
        d = jax.random.uniform(ks[3], (D,), dtype=jnp.float32)
        fc_in_w = jax.random.normal(ks[4], (D, D), dtype=jnp.float32) * (1.0 / np.sqrt(D))
        fc_in_b = jnp.zeros((D,), dtype=jnp.float32)
        return {'x': x, 'adj_mx': adj_mx, 'alpha_train': alpha_train, 'w': w, 'd': d, 'fc_in_w': fc_in_w, 'fc_in_b': fc_in_b, 'vt': 0}
    _L0_gnn_all = _L0_gnn_setup()
    _L0_gnn_in = {k: v for k, v in _L0_gnn_all.items() if k in ('alpha_train', 'w', 'd', 'fc_in_w', 'fc_in_b')}
    del _L0_gnn_all

    def _L0_ffn_setup():
        import jax, jax.numpy as jnp
        import numpy as np
        N_EXPERTS = 8
        TOP_K = 2
        key = jax.random.key(seed)
        ks = jax.random.split(key, 5)
        B, T, C, E, H = (8, 1024, 128, 8, 341)
        scale = 1.0 / np.sqrt(C)
        return {'x': jax.random.normal(ks[0], (B, T, C), dtype=jnp.float32), 'router_w': jax.random.normal(ks[1], (E, C), dtype=jnp.float32) * scale, 'w1': jax.random.normal(ks[2], (E, H, C), dtype=jnp.float32) * scale, 'w2': jax.random.normal(ks[3], (E, C, H), dtype=jnp.float32) * (1.0 / np.sqrt(H)), 'w3': jax.random.normal(ks[4], (E, H, C), dtype=jnp.float32) * scale}
    _L0_ffn_all = _L0_ffn_setup()
    _L0_ffn_in = {k: v for k, v in _L0_ffn_all.items() if k in ('router_w', 'w1', 'w2', 'w3')}
    del _L0_ffn_all
    return {'x': x, 'adj': adj, 'L0_gnn_alpha_train': _L0_gnn_in['alpha_train'], 'L0_gnn_w': _L0_gnn_in['w'], 'L0_gnn_d': _L0_gnn_in['d'], 'L0_gnn_fc_in_w': _L0_gnn_in['fc_in_w'], 'L0_gnn_fc_in_b': _L0_gnn_in['fc_in_b'], 'L0_ffn_router_w': _L0_ffn_in['router_w'], 'L0_ffn_w1': _L0_ffn_in['w1'], 'L0_ffn_w2': _L0_ffn_in['w2'], 'L0_ffn_w3': _L0_ffn_in['w3']}

def reference(x, adj, L0_gnn_alpha_train, L0_gnn_w, L0_gnn_d, L0_gnn_fc_in_w, L0_gnn_fc_in_b, L0_ffn_router_w, L0_ffn_w1, L0_ffn_w2, L0_ffn_w3):
    import jax
    import jax.numpy as jnp

    def _L0_gnn_ref(x, adj_mx, alpha_train, w, d, fc_in_w, fc_in_b, vt):
        import jax, jax.numpy as jnp
        import numpy as np
        N_STEPS = 8
        SPATIAL_SCALE = 1.0
        x0 = jax.lax.stop_gradient(x)
        h = jnp.einsum('bnd,ed->bne', x, fc_in_w) + fc_in_b
        alph = jax.nn.sigmoid(alpha_train)[:, None]
        d_clamped = jnp.clip(d, 0.0, 1.0)
        w_eff = w * d_clamped @ w.T
        dt = jnp.float32(SPATIAL_SCALE / N_STEPS)

        def euler_step(h, _):
            ax = jnp.einsum('nm,bmd->bnd', adj_mx, h)
            f = alph * 0.5 * (ax - h) + h @ w_eff - h + x0
            return (h + dt * f, None)
        h, _ = jax.lax.scan(euler_step, h, None, length=N_STEPS)
        return h

    def _L0_ffn_ref(x, router_w, w1, w2, w3):
        import jax, jax.numpy as jnp
        import numpy as np
        N_EXPERTS = 8
        TOP_K = 2
        B, T, C = x.shape
        flat = x.reshape(-1, C)
        logits = flat @ router_w.T
        probs = jax.nn.softmax(logits, axis=-1)
        topk_probs, topk_idx = jax.lax.top_k(probs, TOP_K)
        topk_probs = topk_probs / (jnp.sum(topk_probs, axis=-1, keepdims=True) + 1e-09)
        onehot = jax.nn.one_hot(topk_idx, N_EXPERTS, dtype=flat.dtype)
        gates = jnp.einsum('nk,nke->ne', topk_probs, onehot)
        h1 = jnp.einsum('nc,ehc->neh', flat, w1)
        h3 = jnp.einsum('nc,ehc->neh', flat, w3)
        h = jax.nn.silu(h1) * h3
        y = jnp.einsum('neh,ech->nec', h, w2)
        out = jnp.einsum('ne,nec->nc', gates, y)
        return out.reshape(B, T, C)
    x = x + _L0_gnn_ref(_layernorm(x, axis=-1), adj, L0_gnn_alpha_train, L0_gnn_w, L0_gnn_d, L0_gnn_fc_in_w, L0_gnn_fc_in_b, 0)
    x = x + _L0_ffn_ref(_layernorm(x, axis=-1), L0_ffn_router_w, L0_ffn_w1, L0_ffn_w2, L0_ffn_w3)
    return x

_drawn_inputs = setup_inputs


def setup_inputs(seed=0):
    import zlib

    import numpy as np

    out = dict(_drawn_inputs(seed))
    spreads = {'L0_gnn_alpha_train': (1.0, 0.2), 'L0_gnn_fc_in_b': (0.0, 0.1)}
    factors = {}
    for name, (base, spread) in spreads.items():
        noise = np.random.default_rng([zlib.crc32(name.encode()), seed]).standard_normal(out[name].shape)
        drawn = base * np.exp(spread * noise) if base else spread * noise
        out[name] = jnp.asarray(drawn.astype(out[name].dtype))
    for name, factor in factors.items():
        out[name] = (out[name] * factor).astype(out[name].dtype)
    return out
```

```python
from contextlib import ExitStack
from math import comb

import numpy as np

import concourse.bass as bass
from concourse import mybir

F32 = mybir.dt.float32
F16 = mybir.dt.float16
U32 = mybir.dt.uint32
I32 = mybir.dt.int32
ALU = mybir.AluOpType
ACT = mybir.ActivationFunctionType
AX = mybir.AxisListType.X

P = 128
D = 128
N = 512
NC = N // P
NB = 16
TOKENS = NB * N
STEPS = 8
DT = 1.0 / STEPS
EPS = 1e-5
GB = 4
NG = NB // GB
GT = GB * NC
E = 8
HID = 341
HC = 3
SLOT = 256
CAP = TOKENS + SLOT
DUMMY = E * CAP
ROWS = DUMMY + SLOT
NTILES = (2 * TOKENS + E * (SLOT - 1)) // SLOT
NTAB = 80
UNROLL = 4
FIRST = 16
ROW = D + 2

SA = [0, 10, 14, 12]
SV = [0, 6, 10]
SZ = 6
SW = 6
SU = 6


def p2(n):
    return float(2.0 ** n)


C_ID, C_IOM, C_EB, C_TOK, C_SCAN, C_BIN, C_TILE, C_ONE, C_END = np.cumsum(
    [0, P, E, E, GT, P, 9, NTAB, E]).tolist()


def shape_constants():
    c = np.zeros((P, C_END), np.float32)
    c[:, C_ID:C_ID + P] = np.eye(P)
    c[:, C_IOM:C_IOM + E] = np.arange(E) - E
    c[:, C_EB:C_EB + E] = np.arange(E) * CAP
    tt = np.arange(GT)
    c[:, C_TOK:C_TOK + GT] = ((tt % GB) * NC + tt // GB)[None] * P + np.arange(P)[:, None]
    c[:, C_SCAN:C_SCAN + P] = (np.arange(P) % GT != 0)[None]
    c[:, C_BIN:C_BIN + 9] = [comb(STEPS, j) / 2.0 ** SU for j in range(9)]
    c[:, C_TILE:C_TILE + NTAB] = np.arange(NTAB)
    c[:, C_ONE:C_ONE + E] = 1.0
    h = np.zeros((P, 3 * P), np.float16)
    h[:, 0:P] = np.eye(P)
    h[:, P:2 * P] = np.triu(np.ones((P, P)), 1)
    h[:, 2 * P:] = 1.0
    pad = np.zeros((SLOT, ROW), np.uint32)
    pad[:, D] = TOKENS + np.arange(SLOT)
    return c, h, pad


def wait_apart(eng, sem, value, tiny):
    eng.wait_ge(sem, value)
    tiny()


class Steps:

    def __init__(self, eng, sem, index, per):
        self.eng, self.sem, self.base, self.per, self.n = eng, sem, index * per, per, 0

    def done(self, ins):
        self.n += 1
        return ins.then_inc(self.sem, 1)

    def wait(self):
        self.eng.wait_ge(self.sem, self.base + self.n)

    def wait_apart(self, tiny):
        wait_apart(self.eng, self.sem, self.base + self.n, tiny)

    def end(self):
        assert self.n == self.per, (self.n, self.per)


def gnn_moe_kernel(nc, x, adj, adj_t, alpha, w_t, d, fc_w, fc_b, router_t, w1_t, w3_t, w2_t, c32, c16, pad, out):
    with ExitStack() as ctx:
        def sb(name, shape, dt):
            return ctx.enter_context(nc.sbuf_tensor(name, shape, dt))

        def sem(name):
            return ctx.enter_context(nc.semaphore(name))

        slots = nc.dram_tensor("slots", (ROWS, ROW), U32, kind="Internal").ap()

        k32 = sb("k32", [P, C_END], F32)
        k16 = sb("k16", [P, 3 * P], F16)
        ident16, tri16, ones16 = k16[:, 0:P], k16[:, P:2 * P], k16[:, 2 * P:3 * P]
        ident32 = k32[:, C_ID:C_ID + P]
        X = sb("X", [P, (NB + 1) * NC, D], F32)
        stage = sb("stage", [P, 4096], F32)
        adjT = stage[:, 0:2048].rearrange("p (k n) -> p k n", k=NC)
        adjN = stage[:, 2048:4096].rearrange("p (k n) -> p k n", k=NC)
        B = sb("B", [P, 3, 2, NC, N], F16)
        sigc = sb("sigc", [P, NC], F32)
        alfc = sb("alfc", [P, NC], F32)
        G16 = sb("G16", [P, 2, 3, 3, D], F16)
        W1 = sb("W1", [P, 2, E, HC * P], F16)
        W3 = sb("W3", [P, 2, E, HC * P], F16)
        W2 = sb("W2", [P, 2, E, HC, D], F16)
        wr32 = sb("wr32", [P, E], F32)
        wr16 = sb("wr16", [P, 2, E], F16)
        xn = sb("xn", [P, 2, NC, D], F32)
        Xh = sb("Xh", [P, 2, 2, NC, D], F16)
        XT = sb("XT", [P, 2, 2, N], F16)
        V = sb("V", [P, 2, 2, 2, N], F16)
        Z2 = sb("Z2", [P, 2, NC, GB, D], F16)
        An = Z2[:].rearrange("p a k b d -> p a k (b d)")
        Z1 = sb("Z1", [P, NC, GB, D], F32)
        Uf = sb("Uf", [P, 2, GB * D], F32)
        U = sb("U", [P, 2, NC, GB * D], F16)
        stats = sb("stats", [P, 2, NC, 6], F32)
        mv = sb("mv", [P, 2, NC, 2], F32)
        var = sb("var", [P, 2, NC], F32)
        rstd = sb("rstd", [P, 2, NC], F32)
        stats2 = sb("stats2", [P, 2, NC, 6], F32)
        mv2 = sb("mv2", [P, 2, NC, 2], F32)
        var2 = sb("var2", [P, 2, NC], F32)
        rstd2 = sb("rstd2", [P, 2, NC], F32)
        xn2 = sb("xn2", [P, 2, NC, D], F32)
        spare = sb("spare", [P, 3], F32)
        mhalf = sb("mhalf", [P, NC], F32)
        pay = sb("pay", [P, 2, GT, ROW], U32)
        payh = pay[:].bitcast(F16)
        payf = pay[:].bitcast(F32)
        XR = sb("XR", [P, 2, 2, NC, P], F16)
        biasf = sb("biasf", [P, NC, D], F32)
        uall = sb("uall", [P, NC, 9], F32)
        u16 = sb("u16", [P, 2, NC, 9], F16)
        bt = sb("bt", [P, 9], F32)
        btT = sb("btT", [9, D], F32)
        bcol = sb("bcol", [P, 1], F32)
        dcol = sb("dcol", [P, 2], F32)
        mx = sb("mx", [P, GT], F32)
        dl = sb("dl", [P, GT, E], F32)
        ex = sb("ex", [P, GT, E], F32)
        ssum = sb("ssum", [P, GT], F32)
        key = sb("key", [P, GT, E], F32)
        first = sb("first", [P, GT], F32)
        oh = sb("oh", [P, 2, GT, E], F32)
        rest = sb("rest", [P, GT, E], F32)
        m2 = sb("m2", [P, GT], F32)
        den = sb("den", [P, GT], F32)
        gate = sb("gate", [P, 2, GT], F32)
        M16 = sb("M16", [P, E, GT], F16)
        incl = sb("incl", [P, E, GT], F32)
        pos = sb("pos", [P, E, GT], F32)
        prod = sb("prod", [P, 2, GT, E], F32)
        slotf = sb("slotf", [P, 2, GT], F32)
        idx = sb("idx", [P, 2, GT], U32)
        run = sb("run", [P, E], F32)
        tok = sb("tok", [P, GT], F32)
        cnt = sb("cnt", [P, 4, E], F32)
        cnti = sb("cnti", [P, 2, E], I32)
        padrow = sb("padrow", [P, E], I32)

        z1w = Z1[:].rearrange("p k b d -> p (k b d)")
        uw = U[:].rearrange("p h k n -> p (h k n)").bitcast(F32)
        Gf = z1w[:, 0:9 * D].rearrange("p (r i d) -> p r i d", r=3, i=3)
        sig = z1w[:, 9 * D:9 * D + N]
        Wp = uw[:, 0:9 * D].rearrange("p (a d) -> p a d", a=9)
        fcw, wt, wd, idt = (uw[:, (9 + n) * D:(10 + n) * D] for n in range(4))
        alf = Uf[:, 1, :]
        ut = xn2[0:9].rearrange("p a k d -> p (a k d)")[:, 0:N]
        ind = stage[:, 0:3 * NTAB * E].rearrange("p (a t e) -> p a t e", a=3, t=NTAB)
        tabf = stage[:, 3 * NTAB * E:3 * NTAB * E + 6 * NTAB].rearrange("p (a t) -> p a t", a=6)
        tabi = stage[:, 3 * NTAB * E + 6 * NTAB:3 * NTAB * E + 12 * NTAB].bitcast(I32).rearrange("p (a t) -> p a t", a=6)

        Bw = B[:].rearrange("p a b k n -> p (a b k n)")
        at = [0]

        def carve(words16, dt, pattern, **k):
            a = Bw[:, at[0]:at[0] + words16]
            at[0] += words16
            if dt != F16:
                a = a.bitcast(dt)
            return a.rearrange(pattern, **k)

        XS = carve(4 * 2 * 2 * ROW, U32, "p (r a w) -> p r a w", r=4, a=2)
        XSh, XSf = XS.bitcast(F16), XS.bitcast(F32)
        XTf = carve(2 * 2 * SLOT, F16, "p (r h s) -> p r h s", r=2, h=2)
        sil = carve(2 * 2 * HC * SLOT, F32, "p (r c s) -> p r c s", r=2, c=HC)
        hf = carve(2 * HC * SLOT, F32, "p (c s) -> p c s", c=HC)
        Hh = carve(2 * 2 * HC * SLOT, F16, "p (r h c s) -> p r h c s", r=2, h=2, c=HC)
        Y = carve(2 * 2 * 2 * D, F32, "p (r a d) -> p r a d", r=2, a=2)
        assert at[0] <= 3 * 2 * NC * N

        ps = ctx.enter_context(nc.psum_tensor("ps", [P, 8, 512], F32))
        psT = ps[:, 0, :].bitcast(F16).rearrange("p (h n) -> p h n", h=2)
        psR = ps[:, 7, :]

        S = {}

        def s(name):
            if name not in S:
                S[name] = sem(name)
            return S[name]

        x_rows = x.rearrange("b (k p) d -> p (b k) d", p=P)
        out_rows = out[0:TOKENS, :].rearrange("(t p) d -> p t d", p=P)

        def y_free(t, u):
            return FIRST + (32 * (t // 2) if isinstance(t, int) else 16 * t - 16 * (u % 2))

        def tiles_loop(eng, front, back):
            front(0, 0)
            whole = (NTILES - 1) // UNROLL
            peel = 1
            for u in range(UNROLL):
                front(u + 1, (u + 1) % UNROLL)
                back(u, u)
            with eng.Fori(peel, whole) as i:
                for u in range(UNROLL):
                    front(i * UNROLL + u + 1, (u + 1) % UNROLL)
                    back(i * UNROLL + u, u)
            for t in range(whole * UNROLL, NTILES):
                if t + 1 < NTILES:
                    front(t + 1, (t + 1) % UNROLL)
                back(t, t % UNROLL)

        block = ctx.enter_context(nc.Block())

        @block.sync
        def _(sp):
            sp.dma_start(k32[:], c32).then_inc(s("in_w"), 16)
            sp.dma_start(wt, w_t).then_inc(s("in_w"), 16)
            sp.dma_start(dcol[:, 0:1], d).then_inc(s("in_w"), 16)
            sp.dma_start(fcw, fc_w).then_inc(s("in_w"), 16)
            sp.dma_start(bcol[:], fc_b).then_inc(s("in_w"), 16)
            sp.dma_start(alf, alpha.to_broadcast([P, N])).then_inc(s("in_a"), 16)
            sp.dma_start(adjT, adj_t.rearrange("(k p) n -> p k n", p=P)).then_inc(s("in_a"), 16)
            sp.dma_start(X[:, 0:GT, :], x_rows[:, 0:GT, :]).then_inc(s("in_x"), 16)
            sp.dma_start(adjN, adj.rearrange("(k p) n -> p k n", p=P)).then_inc(s("in_n"), 16)
            with nc.allow_non_contiguous_dma(reason="512 numbers"):
                sp.dma_start(alfc[:], alpha.rearrange("a (k p) -> p (a k)", p=P)).then_inc(s("in_n"), 16)
            sp.dma_start(k16[:], c16).then_inc(s("in_c"), 16)
            sp.dma_start(wr32[:], router_t).then_inc(s("in_c"), 16)
            for g in range(1, NG):
                sp.wait_ge(s("in_x"), 16 * g)
                sp.dma_start(X[:, g * GT:(g + 1) * GT, :], x_rows[:, g * GT:(g + 1) * GT, :]).then_inc(s("in_x"), 16)
            sp.wait_ge(s("a_split"), 2)
            sp.dma_start(stage[:, 0:E * HID], w1_t).then_inc(s("in_f"), 16)
            sp.wait_ge(s("f_split"), 1)
            sp.dma_start(stage[:, 0:E * HID], w3_t).then_inc(s("in_f"), 16)
            sp.wait_ge(s("f_split"), 2)
            for c in range(HC):
                n = min(P, HID - c * P)
                sp.dma_start(stage[0:n, c * E * D:(c + 1) * E * D], w2_t[c * P:c * P + n, :]).then_inc(s("in_f"), 16)
            with sp.Fori(0, NG) as g:
                sp.wait_ge(s("x2_steps"), NC * (g + 1))
                sp.dma_start(out_rows[:, bass.ds(g * GT, GT), :], X[:, bass.ds(g * GT, GT), :]).then_inc(s("out_st"), 16)
            sp.wait_ge(s("out_st"), 16 * NG)
            sp.wait_ge(s("table"), 1)
            for e in range(E):
                r = sp.value_load(padrow[0:1, e:e + 1], min_val=0, max_val=DUMMY - SLOT)
                sp.dma_start(slots[bass.ds(r, SLOT), :], pad).then_inc(s("pad_st"), 16)
            sp.wait_ge(s("pad_st"), 16 * E)
            sp.wait_ge(s("added1"), FIRST)
            sp.wait_ge(s("scatter"), FIRST + 16 * 2 * GT * NG)

            for t in range(4):
                r = sp.value_load(tabi[0:1, 0, t:t + 1], min_val=0, max_val=DUMMY)
                sp.dma_start(XS[:, t], slots[bass.ds(r, SLOT), :].rearrange("(p a) w -> p a w", a=2)).then_inc(s(f"xs{t}"), 16)
            with sp.Fori(1, NTILES // UNROLL) as i:
                for u in range(UNROLL):
                    sp.wait_ge(s(f"added{u % 2}"), FIRST + 64 * i - 32 + 32 * (u // 2))
                    r = sp.value_load(tabi[0:1, 0, bass.ds(i * UNROLL + u, 1)], min_val=0, max_val=DUMMY)
                    sp.dma_start(XS[:, u], slots[bass.ds(r, SLOT), :].rearrange("(p a) w -> p a w", a=2)).then_inc(s(f"xs{u}"), 16)
            for t in range(NTILES // UNROLL * UNROLL, NTILES):
                u = t % UNROLL
                sp.wait_ge(s(f"added{u % 2}"), FIRST + 32 * ((t - 4) // 2 + 1))
                r = sp.value_load(tabi[0:1, 0, t:t + 1], min_val=0, max_val=DUMMY)
                sp.dma_start(XS[:, u], slots[bass.ds(r, SLOT), :].rearrange("(p a) w -> p a w", a=2)).then_inc(s(f"xs{u}"), 16)
            sp.wait_ge(s("added0"), FIRST + 32 * ((NTILES + 1) // 2))
            sp.wait_ge(s("added1"), FIRST + 32 * (NTILES // 2))

        @block.gpsimd
        def _(pool):
            tiny = lambda: nc.gpsimd.tensor_tensor(spare[:, 2:3], mhalf[:, 0:1], mhalf[:, 0:1], ALU.add).then_inc(s("tick"), 1)
            nc.gpsimd.memset(mhalf[:], -0.5).then_inc(s("mhalf"), 1)
            nc.gpsimd.memset(Uf[:, 0, :], 0.0).then_inc(s("zero_out"), 1)
            nc.gpsimd.memset(X[:, NB * NC:, :], 0.0).then_inc(s("zero_x"), 1)
            nc.gpsimd.memset(W1[:, :, :, HID:], 0.0)
            nc.gpsimd.memset(W3[:, :, :, HID:], 0.0)
            nc.gpsimd.memset(W2[:, :, :, HC - 1, :], 0.0).then_inc(s("zero_w"), 1)
            nc.gpsimd.memset(uall[:, :, 0:1], p2(SU)).then_inc(s("u0"), 1)
            pool.wait_ge(s("zero_out"), 1)
            nc.gpsimd.dma_start(out[TOKENS:TOKENS + SLOT, :].rearrange("(a p) d -> p a d", p=P),
                                Uf[:, 0, 0:2 * D].rearrange("p (a d) -> p a d", a=2)).then_inc(s("added0"), 16)
            nc.gpsimd.dma_start(slots[DUMMY:DUMMY + P, :], pad[0:P, :]).then_inc(s("added1"), 16)
            nc.gpsimd.dma_start(slots[DUMMY + P:DUMMY + SLOT, :], pad[P:SLOT, :]).then_inc(s("scatter"), 16)
            pool.wait_ge(s("mhalf"), 1)

            def ln1_rstd(b, q):
                pool.wait_ge(s("var"), b + 1)
                nc.gpsimd.tensor_tensor(rstd[:, q], var[:, q], mhalf[:], ALU.pow).then_inc(s("rstd"), 1)

            def ln1_lo(b, q):
                pool.wait_ge(s("xn_hi"), b + 1)
                nc.gpsimd.tensor_tensor(Xh[:, q, 1], xn[:, q], Xh[:, q, 0], ALU.subtract).then_inc(s("xn_split"), 1)

            def scatters(g):
                wait_apart(pool, s("route"), g + 2, tiny)
                for k in range(2):
                    for tt in range(GT):
                        nc.gpsimd.indirect_dma_start(
                            out=slots, out_offset=bass.IndirectOffsetOnAxis(ap=idx[:, k, tt:tt + 1], axis=0),
                            in_=pay[:, k, tt, :], in_offset=None).then_inc(s("scatter"), 16)

            def ln2_rstd(g):
                for q in range(NC):
                    pool.wait_ge(s("var2"), NC * g + q + 1)
                    nc.gpsimd.tensor_tensor(rstd2[:, q % 2], var2[:, q % 2], mhalf[:], ALU.pow).then_inc(s("rstd2"), 1)

            def bias_add(b):
                pool.wait_ge(s("xn_ready"), b + 1)
                nc.gpsimd.tensor_tensor(X[:, bass.ds(b * NC, NC), :], X[:, bass.ds(b * NC, NC), :], biasf[:],
                                        ALU.add).then_inc(s("x_bias"), 1)

            ln1_rstd(0, 0)
            ln1_lo(0, 0)
            pool.wait_ge(s("bias"), 1)

            def body(g, tail):
                for j in range(GB):
                    b = g * GB + j
                    bias_add(b)
                    ln1_rstd(b + 1, (j + 1) % 2)
                    ln1_lo(b + 1, (j + 1) % 2)
                    if tail and j == 1:
                        ln2_rstd(g - 1)
                if tail:
                    scatters(g - 1)

            body(0, False)
            with pool.Fori(1, NG) as g:
                body(g, True)
            ln2_rstd(NG - 1)
            scatters(NG - 1)

            pool.wait_ge(s("table"), 1)
            pool.wait_ge(s("out_st"), 16 * NG)

            def add_tile(t, u, col):
                w0 = pool.value_load(tabi[0:1, 2, col], min_val=FIRST, max_val=32 * NTAB)
                w1 = pool.value_load(tabi[0:1, 3, col], min_val=FIRST, max_val=32 * NTAB)
                pool.wait_ge(s("added0"), w0)
                pool.wait_ge(s("added1"), w1)
                pool.wait_ge(s("tick"), NG + t)
                wait_apart(pool, s("y_ready"), t + 1, tiny)
                for a in range(2):
                    nc.gpsimd.indirect_dma_start(
                        out=out, out_offset=bass.IndirectOffsetOnAxis(ap=XS[:, u, a, D:D + 1], axis=0),
                        in_=Y[:, u % 2, a, :], in_offset=None, compute_op=ALU.add).then_inc(s(f"added{u % 2}"), 16)

            with pool.Fori(0, NTILES // UNROLL) as i:
                for u in range(UNROLL):
                    add_tile(i * UNROLL + u, u, bass.ds(i * UNROLL + u, 1))
            for t in range(NTILES // UNROLL * UNROLL, NTILES):
                add_tile(t, t % UNROLL, slice(t, t + 1))

        @block.scalar
        def _(act):
            copy = lambda o, i, sc=1.0: nc.scalar.activation(o, i, ACT.Copy, scale=sc)
            act.wait_ge(s("in_a"), 32)
            nc.scalar.activation(sig, alf, ACT.Sigmoid).then_inc(s("sig"), 1)
            act.wait_ge(s("in_n"), 32)
            nc.scalar.activation(sigc[:], alfc[:], ACT.Sigmoid).then_inc(s("sig"), 1)

            def ln1_hi(b, q):
                act.wait_ge(s("xn_ready"), b + 1)
                copy(Xh[:, q, 0], xn[:, q]).then_inc(s("xn_hi"), 1)

            ln1_hi(0, 0)
            act.wait_ge(s("a_full"), 1)
            copy(B[:, 0, 0], adjT).then_inc(s("a_hi"), 1)
            act.wait_ge(s("a_full"), 2)
            copy(An[:, 0], adjN).then_inc(s("a_hi"), 1)
            for j in (1, 2):
                for i in range(NC):
                    act.wait_ge(s("pow_done"), (j - 1) * NC + i + 1)
                    copy(B[:, j, 0, i], ps[:, 4 + i, :], p2(SA[j + 1] - SA[1] - SA[j])).then_inc(s("pow_hi"), 1)

            def xt_evac(b, q):
                act.wait_ge(s("xt_done"), b + 1)
                copy(XT[:, q], psT).then_inc(s("xt_ready"), 1)

            def v_hi(b, q):
                for r in range(2):
                    act.wait_ge(s("v_done"), 2 * b + r + 1)
                    copy(V[:, q, 0, r], ps[:, 1 + r, :], p2(SV[r + 1] - SA[r + 1])).then_inc(s("v_hi"), 1)

            def z_hi(b, j, cs):
                for c in cs:
                    act.wait_ge(s("z_done"), NC * b + c + 1)
                    z = ps[:, 3 + c % 2, 0:3 * D]
                    copy(Z2[:, 0, c, j, :], z[:, 0:D], p2(-SZ))
                    copy(Z1[:, c, j, :], z[:, D:2 * D], p2(-SZ)).then_inc(s("z_hi"), 1)

            def u_hi(g):
                for i in range(NC):
                    act.wait_ge(s("u_full"), NC * g + i + 1)
                    copy(U[:, 0, i], Uf[:, i % 2]).then_inc(s("u_hi"), 1)

            def ln2_hi(g):
                for q in range(NC):
                    act.wait_ge(s("xn2_ready"), NC * g + q + 1)
                    copy(payh[:, 0, q * GB:(q + 1) * GB, 0:D], xn2[:, q % 2]).then_inc(s("xn2_hi"), 1)
                    act.wait_ge(s("xn2_lo"), NC * g + q + 1)
                    copy(payh[:, 1, q * GB:(q + 1) * GB, 0:2 * D],
                         payh[:, 0, q * GB:(q + 1) * GB, 0:2 * D]).then_inc(s("pay_x"), 1)

            def rt_evac(g, q):
                act.wait_ge(s("rt_done"), NC * g + q + 1)
                copy(XR[:, q % 2].rearrange("p h t n -> p (h t n)"), ps[:, 5 + q % 2, :].bitcast(F16)).then_inc(s("rt_ready"), 1)

            def expo(g):
                act.wait_ge(s("dl_ready"), g + 1)
                nc.scalar.activation(ex[:], dl[:], ACT.Exp, scale=p2(-SW)).then_inc(s("ex_ready"), 1)

            def weights(k):
                if k < 2:
                    act.wait_ge(s("in_f"), 16 * (k + 1))
                    src = stage[:, 0:E * HID].rearrange("p (e h) -> p e h", e=E)
                    copy((W1, W3)[k][:, 0, :, 0:HID], src, p2(SW)).then_inc(s("f_hi"), 1)
                else:
                    act.wait_ge(s("in_f"), 16 * (2 + HC))
                    act.wait_ge(s("zero_w"), 1)
                    for c in range(HC):
                        n = min(P, HID - c * P)
                        src = stage[0:n, c * E * D:(c + 1) * E * D].rearrange("p (e d) -> p e d", e=E)
                        ins = copy(W2[0:n, 0, :, c, :], src, p2(SW))
                    ins.then_inc(s("f_hi"), 1)

            def body(g, tail):
                for j in range(GB):
                    b = g * GB + j
                    if tail and j == 2:
                        ln2_hi(g - 1)
                    xt_evac(b, j % 2)
                    v_hi(b, j % 2)
                    if tail and j == 2:
                        rt_evac(g - 1, 0)
                        rt_evac(g - 1, 1)
                    if tail and j == 0:
                        u_hi(g - 1)
                    if j:
                        z_hi(b - 1, j - 1, (0, 1))
                    ln1_hi(b + 1, (j + 1) % 2)
                    if j:
                        z_hi(b - 1, j - 1, (2, 3))
                    if tail and j == 2:
                        rt_evac(g - 1, 2)
                        rt_evac(g - 1, 3)
                    if tail and j == 3:
                        expo(g - 1)
                    if not tail and j < 3:
                        weights(j)
                z_hi(g * GB + 3, 3, range(NC))

            body(0, False)
            with act.Fori(1, NG) as g:
                body(g, True)
            u_hi(NG - 1)
            ln2_hi(NG - 1)
            for q in range(NC):
                rt_evac(NG - 1, q)
            expo(NG - 1)

            def xt(t, q):
                act.wait_ge(s("fx_done"), t + 1)
                copy(XTf[:, q], ps[:, 6, 0:SLOT].bitcast(F16).rearrange("p (h s) -> p h s", h=2)).then_inc(s("fx_ready"), 1)

            def silu(t, q):
                for c in range(HC):
                    act.wait_ge(s("h_done"), HC * t + c + 1)
                    nc.scalar.activation(sil[:, q, c], ps[:, HC * q + c, 0:SLOT], ACT.Silu,
                                         scale=p2(-SW)).then_inc(s("sil"), 1)

            def y_out(t, u):
                act.wait_ge(s("y_done"), t + 1)
                if not (isinstance(t, int) and t < 2):
                    act.wait_ge(s(f"added{u % 2}"), y_free(t, u))
                for a in range(2):
                    ins = nc.scalar.activation(Y[:, u % 2, a], ps[:, 7, a * D:(a + 1) * D], ACT.Identity,
                                               scale=XSf[:, u, a, D + 1:D + 2])
                ins.then_inc(s("y_ready"), 1)

            tiles_loop(act, lambda t, u: (xt(t, u % 2), silu(t, u % 2)), y_out)

        @block.vector
        def _(dve):
            v = nc.vector
            tiny = lambda: v.tensor_copy(spare[:, 0:1], spare[:, 1:2])
            v.memset(spare[:, 0:2], 0.0).then_inc(s("spare"), 1)
            dve.wait_ge(s("spare"), 1)

            def ln_stats(rows, q, name, index, st, m, va, out_sem):
                st_, m_, va_ = st[:, q], m[:, q], va[:, q]
                steps = Steps(dve, s(name), index, 2)
                tiny()
                for c in range(NC):
                    ins = v.bn_stats(st_[:, c, :], rows(c))
                steps.done(ins)
                steps.wait_apart(tiny)
                for c in range(NC):
                    ins = v.bn_aggr(m_[:, c, :], st_[:, c, :])
                steps.done(ins)
                steps.wait()
                v.tensor_scalar(va_, m_[:, :, 1], EPS, None, ALU.add).then_inc(s(out_sem), 1)
                steps.end()

            def ln1_stats(b, q):
                ln_stats(lambda c: X[:, b * NC + c, :] if isinstance(b, int) else X[:, bass.ds(b * NC + c, 1), :].rearrange("p a d -> p (a d)"),
                         q, "ln1_st", b, stats, mv, var, "var")

            def ln1_norm(b, q):
                dve.wait_ge(s("rstd"), b + 1)
                for c in range(NC):
                    row = X[:, b * NC + c, :] if isinstance(b, int) else X[:, bass.ds(b * NC + c, 1), :].rearrange("p a d -> p (a d)")
                    ins = v.tensor_scalar(xn[:, q, c], row, mv[:, q, c, 0:1], rstd[:, q, c:c + 1], ALU.subtract, ALU.mult)
                ins.then_inc(s("xn_ready"), 1)

            w = Steps(dve, s("w_steps"), 0, 18)
            dve.wait_ge(s("in_w"), 80)
            w.done(v.tensor_scalar(dcol[:, 1:2], dcol[:, 0:1], 0.0, 1.0, ALU.max, ALU.min))
            v.tensor_scalar(idt, ident32, 1.0 - DT, None, ALU.mult)
            w.done(v.tensor_copy(Wp[:, 0], ident32))
            w.wait()
            v.tensor_scalar(wd, wt, dcol[:, 1:2], None, ALU.mult).then_inc(s("wd"), 1)
            dve.wait_ge(s("wp_done"), 1)
            v.scalar_tensor_tensor(Wp[:, 1], ps[:, 7, 0:D], DT, idt, ALU.mult, ALU.add).then_inc(s("wp"), 1)
            dve.wait_ge(s("wp_done"), 2)
            v.tensor_copy(Wp[:, 2], ps[:, 6, 0:D]).then_inc(s("wp"), 1)
            dve.wait_ge(s("in_x"), 16)
            dve.wait_ge(s("wp_done"), 3)
            v.tensor_copy(Wp[:, 3:5], ps[:, 5, 0:2 * D].rearrange("p (a d) -> p a d", a=2)).then_inc(s("wp"), 1)
            ln1_stats(0, 0)
            dve.wait_ge(s("wp_done"), 4)
            v.tensor_copy(Wp[:, 5:9], ps[:, 4, 0:4 * D].rearrange("p (a d) -> p a d", a=4)).then_inc(s("wp"), 1)
            ln1_norm(0, 0)
            a = Steps(dve, s("a_steps"), 0, 2)
            dve.wait_ge(s("sig"), 1)
            for k in range(NC):
                blk = adjT[:, k, k * P:(k + 1) * P]
                ins = v.tensor_tensor(blk, blk, ident32, ALU.subtract)
            a.done(ins)
            a.wait()
            v.scalar_tensor_tensor(adjT, adjT, DT * 0.5 * p2(SA[1]), sig.unsqueeze(1).to_broadcast([P, NC, N]),
                                   ALU.mult, ALU.mult).then_inc(s("a_full"), 1)
            dve.wait_ge(s("sig"), 2)
            for k in range(NC):
                blk = adjN[:, k, k * P:(k + 1) * P]
                ins = v.tensor_tensor(blk, blk, ident32, ALU.subtract)
            a.done(ins)
            a.wait()
            for k in range(NC):
                ins = v.tensor_scalar(adjN[:, k, :], adjN[:, k, :], sigc[:, k:k + 1], DT * 0.5 * p2(SA[1]), ALU.mult, ALU.mult)
            ins.then_inc(s("a_full"), 1)
            dve.wait_ge(s("a_hi"), 1)
            v.tensor_tensor(B[:, 0, 1], adjT, B[:, 0, 0], ALU.subtract).then_inc(s("a_split"), 1)
            dve.wait_ge(s("a_hi"), 2)
            v.tensor_tensor(An[:, 1], adjN, An[:, 0], ALU.subtract).then_inc(s("a_split"), 1)
            dve.wait_ge(s("in_c"), 32)
            w.done(v.tensor_scalar(wr16[:, 0], wr32[:], p2(SW), None, ALU.mult))
            w.wait()
            v.scalar_tensor_tensor(wr16[:, 1], wr32[:], p2(SW), wr16[:, 0], ALU.mult, ALU.subtract).then_inc(s("router"), 1)
            dve.wait_ge(s("fw_done"), 3)
            for p in range(9):
                i, r = divmod(8 - p, 3)
                ins = v.tensor_scalar(Gf[:, r, 2 - i], ps[:, 1 + p // 3, (p % 3) * D:(p % 3 + 1) * D],
                                      comb(STEPS, p) * p2(SZ - SV[r]), None, ALU.mult)
            ins.then_inc(s("g_psum"), 1)
            dve.wait_ge(s("g_psum"), 1)
            for p in range(STEPS):
                for j in range(STEPS - p):
                    i, r = divmod(j, 3)
                    ins = v.scalar_tensor_tensor(Gf[:, r, 2 - i], Wp[:, p], DT * comb(p + j, j) * p2(SZ - SV[r]),
                                                 Gf[:, r, 2 - i], ALU.mult, ALU.add)
                w.done(ins)
                w.wait()
            w.done(v.tensor_copy(G16[:, 0], Gf))
            w.wait()
            v.tensor_tensor(G16[:, 1], Gf, G16[:, 0], ALU.subtract).then_inc(s("g_split"), 1)
            for j in (1, 2):
                for i in range(NC):
                    dve.wait_ge(s("pow_hi"), (j - 1) * NC + i + 1)
                    v.scalar_tensor_tensor(B[:, j, 1, i], ps[:, 4 + i, :], p2(SA[j + 1] - SA[1] - SA[j]), B[:, j, 0, i],
                                           ALU.mult, ALU.subtract).then_inc(s("pow_split"), 1)
            def u_split(a0, a1):
                w.done(v.tensor_copy(u16[:, 0, :, a0:a1], uall[:, :, a0:a1]))
                w.wait()
                v.tensor_tensor(u16[:, 1, :, a0:a1], uall[:, :, a0:a1], u16[:, 0, :, a0:a1], ALU.subtract).then_inc(s("u_split"), 1)

            dve.wait_ge(s("u0"), 1)
            dve.wait_ge(s("us_done"), 1)
            for r in range(2):
                ins = v.tensor_scalar(uall[:, :, r + 1:r + 2], ps[:, 0, 0:8].rearrange("p (i r) -> p i r", r=2)[:, :, r:r + 1],
                                      p2(SU - SA[r + 1]), None, ALU.mult)
            w.done(ins)
            w.wait()
            u_split(0, 3)
            for n in (1, 2):
                dve.wait_ge(s("us_done"), 1 + n)
                w.done(v.tensor_scalar(uall[:, :, 3 * n:3 * n + 3], ps[:, 0, 12 * n:12 * n + 12].rearrange("p (i r) -> p i r", r=3),
                                       p2(-SA[3]), None, ALU.mult))
                w.wait()
                if n == 1:
                    u_split(3, 6)
            dve.wait_ge(s("bw_done"), 1)
            v.tensor_tensor(bt[:], ps[:, 0, 64:73], k32[:, C_BIN:C_BIN + 9], ALU.mult).then_inc(s("ub"), 1)
            dve.wait_ge(s("ut_done"), 1)
            w.done(v.tensor_copy(ut, ps[0:9, 4, :]))
            v.tensor_copy(btT[:], ps[0:9, 5, 0:D]).then_inc(s("ub"), 1)
            dve.wait_ge(s("bias_done"), 1)
            v.tensor_copy(biasf[:], ps[:, 6, :].rearrange("p (k d) -> p k d", k=NC)).then_inc(s("bias"), 1)
            v.tensor_copy(run[:], k32[:, C_EB:C_EB + E]).then_inc(s("route"), 1)
            w.done(v.tensor_copy(tok[:], k32[:, C_TOK:C_TOK + GT]))
            w.wait()
            dve.wait_ge(s("zero_x"), 1)
            dve.wait_ge(s("zero_out"), 1)
            dve.wait_ge(s("added0"), FIRST)

            def v_lo(b, q):
                for r in range(2):
                    dve.wait_ge(s("v_hi"), 2 * b + r + 1)
                    v.scalar_tensor_tensor(V[:, q, 1, r], ps[:, 1 + r, :], p2(SV[r + 1] - SA[r + 1]), V[:, q, 0, r],
                                           ALU.mult, ALU.subtract).then_inc(s("v_split"), 1)

            def z_lo(b, j, cs):
                for c in cs:
                    if c == 0:
                        dve.wait_ge(s("x_bias"), b + 1)
                    dve.wait_ge(s("z_hi"), NC * b + c + 1)
                    z = ps[:, 3 + c % 2, 0:3 * D]
                    if isinstance(b, int):
                        row = X[:, b * NC + c, :]
                    else:
                        row = X[:, bass.ds(b * NC + c, 1), :].rearrange("p a d -> p (a d)")
                    v.scalar_tensor_tensor(row, z[:, 2 * D:3 * D], p2(-SZ), row, ALU.mult, ALU.add)
                    v.scalar_tensor_tensor(Z2[:, 1, c, j, :], z[:, 0:D], p2(-SZ), Z2[:, 0, c, j, :],
                                           ALU.mult, ALU.subtract).then_inc(s("z_split"), 1)

            def u_all(g):
                def lo(i):
                    dve.wait_ge(s("u_hi"), NC * g + i + 1)
                    v.tensor_tensor(U[:, 1, i], Uf[:, i % 2], U[:, 0, i], ALU.subtract).then_inc(s("u_lo"), 1)
                for i in range(NC):
                    dve.wait_ge(s("s2_done"), 2 * NC * g + i + 1)
                    if i >= 2:
                        dve.wait_ge(s("u_lo"), NC * g + i - 1)
                    v.scalar_tensor_tensor(Uf[:, i % 2], ps[:, 5 + i % 2, :], p2(-SA[3]), Z1[:, i].rearrange("p b d -> p (b d)"),
                                           ALU.mult, ALU.add).then_inc(s("u_full"), 1)
                    if i:
                        lo(i - 1)
                lo(NC - 1)

            def x2_chunk(g, q):
                st = Steps(dve, s("x2_steps"), g * NC + q, 1)
                dve.wait_ge(s("s2_done"), 2 * NC * g + NC + q + 1)
                rows = X[:, bass.ds(g * GT, GT), :].rearrange("p (b k) d -> p b k d", k=NC)[:, :, q, :]
                st.done(v.scalar_tensor_tensor(rows, ps[:, 5 + q % 2, :].rearrange("p (b d) -> p b d", b=GB), p2(-SA[3]), rows,
                                               ALU.mult, ALU.add))
                st.wait()
                row = lambda c: rows[:, c, :]
                ln_stats(row, q % 2, "ln2_st", g * NC + q, stats2, mv2, var2, "var2")

            def ln2_norm(g, q):
                rows = X[:, bass.ds(g * GT, GT), :].rearrange("p (b k) d -> p b k d", k=NC)[:, :, q, :]
                dve.wait_ge(s("rstd2"), NC * g + q + 1)
                for c in range(GB):
                    ins = v.tensor_scalar(xn2[:, q % 2, c], rows[:, c, :], mv2[:, q % 2, c, 0:1], rstd2[:, q % 2, c:c + 1],
                                          ALU.subtract, ALU.mult)
                ins.then_inc(s("xn2_ready"), 1)

            def ln2_lo(g, q):
                dve.wait_ge(s("xn2_hi"), NC * g + q + 1)
                v.tensor_tensor(payh[:, 0, q * GB:(q + 1) * GB, D:2 * D], xn2[:, q % 2], payh[:, 0, q * GB:(q + 1) * GB, 0:D],
                                ALU.subtract).then_inc(s("xn2_lo"), 1)

            def x2_all(g):
                for q in range(NC):
                    x2_chunk(g, q)
                    if q:
                        ln2_norm(g, q - 1)
                        ln2_lo(g, q - 1)
                ln2_norm(g, NC - 1)
                ln2_lo(g, NC - 1)

            def top2(g):
                st = Steps(dve, s("top2"), g, 15)
                dve.wait_ge(s("logits"), g + 1)
                lg = psR[:, 0:P].rearrange("p (t e) -> p t e", e=E)
                iom = k32[:, C_IOM:C_IOM + E].unsqueeze(1).to_broadcast([P, GT, E])
                wide = lambda a: a.unsqueeze(2).to_broadcast([P, GT, E])
                st.done(v.tensor_reduce(mx[:], lg, AX, ALU.max))
                st.wait()
                v.tensor_tensor(dl[:], lg, wide(mx[:]), ALU.subtract).then_inc(s("dl_ready"), 1)
                dve.wait_ge(s("dl_ready"), g + 1)
                st.done(v.scalar_tensor_tensor(key[:], dl[:], 0.0, iom, ALU.is_equal, ALU.mult))
                st.wait()
                st.done(v.tensor_reduce(first[:], key[:], AX, ALU.min))
                st.wait()
                st.done(v.tensor_tensor(oh[:, 0], key[:], wide(first[:]), ALU.is_equal))
                dve.wait_ge(s("ex_ready"), g + 1)
                v.tensor_reduce(ssum[:], ex[:], AX, ALU.add)
                st.wait()
                st.done(v.scalar_tensor_tensor(rest[:], oh[:, 0], -2.0, ex[:], ALU.mult, ALU.add))
                st.wait()
                st.done(v.tensor_reduce(m2[:], rest[:], AX, ALU.max))
                st.wait()
                st.done(v.tensor_tensor(key[:], rest[:], wide(m2[:]), ALU.is_equal))
                v.tensor_scalar(den[:], m2[:], 1.0, None, ALU.add)
                st.wait()
                st.done(v.tensor_tensor(key[:], key[:], iom, ALU.mult))
                st.wait()
                st.done(v.tensor_reduce(first[:], key[:], AX, ALU.min))
                st.wait()
                st.done(v.tensor_tensor(oh[:, 1], key[:], wide(first[:]), ALU.is_equal))
                st.wait()
                v.tensor_tensor(M16[:].rearrange("p e t -> p t e"), oh[:, 0], oh[:, 1], ALU.add).then_inc(s("mask"), 1)
                st.done(v.scalar_tensor_tensor(den[:], ssum[:], 1e-9, den[:], ALU.mult, ALU.add))
                st.wait()
                st.done(v.tensor_scalar(den[:], den[:], p2(SW), None, ALU.mult))
                st.wait()
                st.done(v.reciprocal(gate[:, 0], den[:]))
                st.wait()
                st.done(v.tensor_tensor(gate[:, 1], gate[:, 0], m2[:], ALU.mult))
                st.wait()
                v.tensor_copy(payf[:, :, :, D + 1], gate[:])
                for k in range(2):
                    v.tensor_copy(pay[:, k, :, D], tok[:])
                st.done(v.tensor_scalar(tok[:], tok[:], float(GT * P), None, ALU.add))
                st.end()

            def place(g):
                st = Steps(dve, s("place"), g, 6)
                dve.wait_ge(s("prefix"), g + 1)
                total = psR[:, 2 * P:3 * P]
                before = psR[:, P:2 * P].rearrange("p (e t) -> p e t", e=E)
                st.done(v.tensor_tensor_scan(incl[:].rearrange("p e t -> p (e t)"), k32[:, C_SCAN:C_SCAN + P], total, 0.0,
                                             ALU.mult, ALU.add))
                st.wait()
                st.done(v.tensor_tensor(pos[:], incl[:], total.rearrange("p (e t) -> p e t", e=E), ALU.subtract))
                st.wait()
                st.done(v.tensor_tensor(pos[:], pos[:], before, ALU.add))
                st.wait()
                st.done(v.tensor_tensor(pos[:], pos[:], run[:].unsqueeze(2).to_broadcast([P, E, GT]), ALU.add))
                st.wait()
                v.tensor_tensor(run[:], run[:], incl[:, :, GT - 1], ALU.add)
                for k in range(2):
                    ins = v.tensor_tensor(prod[:, k], oh[:, k], pos[:].rearrange("p e t -> p t e"), ALU.mult)
                st.done(ins)
                st.wait()
                st.done(v.tensor_reduce(slotf[:].rearrange("p k t -> p (k t)"), prod[:].rearrange("p k t e -> p (k t) e"),
                                        AX, ALU.add))
                st.wait()
                v.tensor_copy(idx[:], slotf[:]).then_inc(s("route"), 1)
                st.end()

            def weights(k):
                dve.wait_ge(s("f_hi"), k + 1)
                if k < 2:
                    src = stage[:, 0:E * HID].rearrange("p (e h) -> p e h", e=E)
                    t = (W1, W3)[k]
                    ins = v.scalar_tensor_tensor(t[:, 1, :, 0:HID], src, p2(SW), t[:, 0, :, 0:HID], ALU.mult, ALU.subtract)
                else:
                    dve.wait_ge(s("zero_w"), 1)
                    for c in range(HC):
                        n = min(P, HID - c * P)
                        src = stage[0:n, c * E * D:(c + 1) * E * D].rearrange("p (e d) -> p e d", e=E)
                        ins = v.scalar_tensor_tensor(W2[0:n, 1, :, c, :], src, p2(SW), W2[0:n, 0, :, c, :],
                                                     ALU.mult, ALU.subtract)
                ins.then_inc(s("f_split"), 1)

            def body(g, tail):
                for j in range(GB):
                    b = g * GB + j
                    v_lo(b, j % 2)
                    if tail and j == 0:
                        u_all(g - 1)
                    if j == GB - 1:
                        if isinstance(g, int):
                            dve.wait_ge(s("in_x"), 16 * min(g + 2, NG))
                        else:
                            dve.wait_ge(s("in_x"), 16 * NG)
                    ln1_stats(b + 1, (j + 1) % 2)
                    if j:
                        z_lo(b - 1, j - 1, (0, 1))
                    ln1_norm(b + 1, (j + 1) % 2)
                    if j:
                        z_lo(b - 1, j - 1, (2, 3))
                    if tail and j == 1:
                        if tail == "loop":
                            dve.wait_ge(s("scatter"), 16 * 2 * GT * (g - 1) + FIRST)
                        x2_all(g - 1)
                    if tail and j == 3:
                        top2(g - 1)
                    if not tail and j < 3:
                        weights(j)
                if tail:
                    place(g - 1)
                z_lo(g * GB + 3, 3, (0, 1, 2, 3))

            body(0, None)
            with dve.Fori(1, NG) as g:
                body(g, "loop")
            u_all(NG - 1)
            dve.wait_ge(s("scatter"), 16 * 2 * GT * (NG - 1) + FIRST)
            x2_all(NG - 1)
            top2(NG - 1)
            place(NG - 1)

            st = Steps(dve, s("tab_steps"), 0, 14)
            first_row = k32[:, C_EB:C_EB + E]
            dve.wait_ge(s("route"), NG + 1)
            st.done(v.tensor_tensor(cnt[:, 0], run[:], first_row, ALU.subtract))
            v.tensor_copy(padrow[:], run[:])
            st.wait()
            st.done(v.tensor_scalar(cnti[:, 0], cnt[:, 0], float(SLOT - 1), None, ALU.add))
            st.wait()
            st.done(v.tensor_scalar(cnti[:, 1], cnti[:, 0], SLOT.bit_length() - 1, None, ALU.logical_shift_right))
            st.wait()
            st.done(v.tensor_copy(cnt[:, 1], cnti[:, 1]))
            st.wait()
            st.done(v.tensor_tensor_scan(cnt[:, 2], k32[:, C_ONE:C_ONE + E], cnt[:, 1], 0.0, ALU.mult, ALU.add))
            st.done(v.tensor_scalar(cnt[:, 3], cnt[:, 1], -float(SLOT), float(CAP), ALU.mult, ALU.add))
            st.wait()
            over = lambda a: a.unsqueeze(1).to_broadcast([P, NTAB, E])
            tile_no = k32[:, C_TILE:C_TILE + NTAB]
            st.done(v.tensor_tensor(ind[:, 0], tile_no.unsqueeze(2).to_broadcast([P, NTAB, E]), over(cnt[:, 2]), ALU.is_ge))
            st.wait()
            v.tensor_tensor(ind[:, 1], ind[:, 0], over(cnt[:, 3]), ALU.mult)
            st.done(v.tensor_tensor(ind[:, 2], ind[:, 0], over(cnt[:, 1]), ALU.mult))
            st.wait()
            st.done(v.tensor_reduce(tabf[:, 0:3].rearrange("p a t -> p (a t)"), ind[:].rearrange("p a t e -> p (a t) e"),
                                    AX, ALU.add))
            st.wait()
            v.tensor_scalar(tabf[:, 5], tile_no, cnt[:, 2, E - 1:E], 0.0, ALU.subtract, ALU.max).then_inc(s("unneeded"), 1)
            dve.wait_ge(s("unneeded"), 1)
            st.done(v.tensor_tensor(tabf[:, 2], tabf[:, 2], tabf[:, 5], ALU.add))
            st.wait()
            st.done(v.scalar_tensor_tensor(tabf[:, 3], tile_no, float(SLOT), tabf[:, 1], ALU.mult, ALU.add))
            v.tensor_scalar(tabi[:, 1], tabf[:, 0], float(E - 1), None, ALU.min)
            v.tensor_scalar(tabf[:, 4], tabf[:, 2], 1.0, None, ALU.add)
            st.done(v.tensor_copy(tabi[:, 4], tabf[:, 2]))
            st.wait()
            v.tensor_scalar(tabi[:, 0], tabf[:, 3], float(DUMMY), None, ALU.min)
            st.done(v.tensor_copy(tabi[:, 5], tabf[:, 4]))
            st.wait()
            st.done(v.tensor_scalar(tabi[:, 4:6], tabi[:, 4:6], 1, 5, ALU.logical_shift_right, ALU.logical_shift_left))
            st.wait()
            v.tensor_scalar(tabi[:, 2], tabi[:, 5], FIRST, None, ALU.add)
            v.tensor_scalar(tabi[:, 3], tabi[:, 4], FIRST, None, ALU.add).then_inc(s("table"), 1)
            st.end()

            def hidden(t, q):
                st = Steps(dve, s("hid"), t, 3 * HC)

                def whole(c):
                    dve.wait_ge(s("sil"), HC * t + c + 1)
                    st.done(v.scalar_tensor_tensor(hf[:, c], ps[:, HC * q + c, SLOT:2 * SLOT], p2(-SW), sil[:, q, c],
                                                   ALU.mult, ALU.mult))

                def hi(c, n):
                    dve.wait_ge(s("hid"), st.base + n)
                    st.done(v.tensor_copy(Hh[:, q, 0, c], hf[:, c]))

                def lo(c, n):
                    dve.wait_ge(s("hid"), st.base + n)
                    st.done(v.tensor_tensor(Hh[:, q, 1, c], hf[:, c], Hh[:, q, 0, c], ALU.subtract))

                whole(0); hi(0, 1); whole(1); lo(0, 2); hi(1, 3); whole(2); lo(1, 5); hi(2, 6); lo(2, 8)
                st.end()

            tiles_loop(dve, lambda t, u: hidden(t, u % 2), lambda t, u: None)

        @block.tensor
        def _(pe):
            mm = nc.tensor.matmul

            def passes(out_ap, lhs, rhs, first, last):
                mm(out_ap, lhs(0), rhs(0), start=first, stop=False)
                mm(out_ap, lhs(0), rhs(1), start=False, stop=False)
                return mm(out_ap, lhs(1), rhs(0), start=False, stop=last)

            pe.wait_ge(s("in_w"), 80)
            pe.wait_ge(s("wd"), 1)
            mm(ps[:, 7, 0:D], wd, wt, start=True, stop=True).then_inc(s("wp_done"), 1)
            pe.wait_ge(s("wp"), 1)
            mm(ps[:, 6, 0:D], Wp[:, 1], Wp[:, 1], start=True, stop=True).then_inc(s("wp_done"), 1)
            pe.wait_ge(s("wp"), 2)
            mm(ps[:, 5, 0:2 * D], Wp[:, 2], Wp[:, 1:3].rearrange("p a d -> p (a d)"), start=True, stop=True).then_inc(s("wp_done"), 1)
            pe.wait_ge(s("wp"), 3)
            mm(ps[:, 4, :], Wp[:, 4], Wp[:, 1:5].rearrange("p a d -> p (a d)"), start=True, stop=True).then_inc(s("wp_done"), 1)
            pe.wait_ge(s("wp"), 4)
            for n in range(3):
                mm(ps[:, 1 + n, 0:3 * D], fcw, Wp[:, 3 * n:3 * n + 3].rearrange("p a d -> p (a d)"),
                   start=True, stop=True).then_inc(s("fw_done"), 1)
            for j in range(9):
                ins = mm(ps[:, 0, 64 + j:65 + j], Wp[:, 8 - j], bcol[:], start=True, stop=True)
            ins.then_inc(s("bw_done"), 1)
            pe.wait_ge(s("a_split"), 2)
            for j in (1, 2):
                for i in range(NC):
                    if j == 2:
                        pe.wait_ge(s("pow_split"), NC)
                    for k in range(NC):
                        ins = passes(ps[:, 4 + i, :], lambda h: An[:, h, k, i * P:(i + 1) * P], lambda h: B[:, j - 1, h, k],
                                     k == 0, k == NC - 1)
                    ins.then_inc(s("pow_done"), 1)
            pe.wait_ge(s("in_c"), 32)
            for i in range(NC):
                for r in range(2):
                    for k in range(NC):
                        for h in range(2):
                            ins = mm(ps[:, 0, 2 * i + r:2 * i + r + 1], B[:, r, h, k, i * P:(i + 1) * P], ones16[:, 0:1],
                                     start=(k == 0 and h == 0), stop=(k == NC - 1 and h == 1))
            ins.then_inc(s("us_done"), 1)
            pe.wait_ge(s("pow_split"), 2 * NC)
            for n in (1, 2):
                pe.wait_ge(s("u_split"), n)
                for i in range(NC):
                    for k in range(NC):
                        ins = passes(ps[:, 0, 12 * n + 3 * i:12 * n + 3 * i + 3], lambda h: B[:, 2, h, k, i * P:(i + 1) * P],
                                     lambda h: u16[:, h, k, 3 * n - 3:3 * n], k == 0, k == NC - 1)
                ins.then_inc(s("us_done"), 1)
            pe.wait_ge(s("ub"), 1)
            for i in range(NC):
                nc.tensor.transpose(ps[0:9, 4, i * P:(i + 1) * P], uall[:, i, :], ident32)
            nc.tensor.transpose(ps[0:9, 5, 0:D], bt[:], ident32).then_inc(s("ut_done"), 1)
            pe.wait_ge(s("ub"), 2)
            for i in range(NC):
                ins = mm(ps[:, 6, i * D:(i + 1) * D], ut[:, i * P:(i + 1) * P], btT[:], start=True, stop=True)
            ins.then_inc(s("bias_done"), 1)
            pe.wait_ge(s("bias"), 1)
            pe.wait_ge(s("g_split"), 1)

            def xt(b, q):
                pe.wait_ge(s("xn_split"), b + 1)
                if not (isinstance(b, int) and b < 1):
                    pe.wait_ge(s("xt_ready"), b)
                for h in range(2):
                    for c in range(NC):
                        ins = nc.tensor.transpose(psT[:, h, c * P:(c + 1) * P], Xh[:, q, h, c, :], ident16)
                ins.then_inc(s("xt_done"), 1)

            def vv(b, q):
                if not (isinstance(b, int) and b < 1):
                    pe.wait_ge(s("v_split"), 2 * b)
                for r in range(2):
                    for k in range(NC):
                        ins = passes(ps[:, 1 + r, :], lambda h: Xh[:, q, h, k, :], lambda h: B[:, r, h, k], k == 0, k == NC - 1)
                    ins.then_inc(s("v_done"), 1)

            def zz(b, q):
                pe.wait_ge(s("xt_ready"), b + 1)
                pe.wait_ge(s("v_split"), 2 * b + 2)
                for c in range(NC):
                    if not (isinstance(b, int) and b < 1 and c < 2):
                        pe.wait_ge(s("z_split"), NC * b + c - 1)
                    n = slice(c * P, (c + 1) * P)
                    for r in range(3):
                        ins = passes(ps[:, 3 + c % 2, 0:3 * D], lambda h: XT[:, q, h, n] if r == 0 else V[:, q, h, r - 1, n],
                                     lambda h: G16[:, h, r].rearrange("p i d -> p (i d)"), r == 0, r == 2)
                    ins.then_inc(s("z_done"), 1)

            def s2(g, second):
                if second:
                    src = lambda h, k: U[:, h, k]
                    pe.wait_ge(s("u_lo"), NC * (g + 1))
                else:
                    src = lambda h, k: Z2[:, h, k].rearrange("p b d -> p (b d)")
                    pe.wait_ge(s("z_split"), NC * GB * (g + 1))
                for i in range(NC):
                    if second:
                        if i < 2:
                            pe.wait_ge(s("u_full"), NC * g + i + 3)
                        else:
                            pe.wait_ge(s("x2_steps"), NC * g + i - 1)
                    elif i >= 2:
                        pe.wait_ge(s("u_full"), NC * g + i - 1)
                    for k in range(NC):
                        ins = passes(ps[:, 5 + i % 2, :], lambda h: B[:, 2, h, k, i * P:(i + 1) * P], lambda h: src(h, k),
                                     k == 0, k == NC - 1)
                    ins.then_inc(s("s2_done"), 1)

            def rt(g, q):
                pe.wait_ge(s("xn2_lo"), NC * g + q + 1)
                if q < 2:
                    pe.wait_ge(s("x2_steps"), NC * g + q + 3)
                else:
                    pe.wait_ge(s("rt_ready"), NC * g + q - 1)
                bank = ps[:, 5 + q % 2, :].bitcast(F16)
                for h in range(2):
                    for t in range(GB):
                        ins = nc.tensor.transpose(bank[:, (h * GB + t) * P:(h * GB + t + 1) * P],
                                                  payh[:, 0, q * GB + t, h * D:(h + 1) * D], ident16)
                ins.then_inc(s("rt_done"), 1)

            def logits(g, q):
                pe.wait_ge(s("rt_ready"), NC * g + q + 1)
                if q == 0:
                    pe.wait_ge(s("route"), g + 1)
                for t in range(GB):
                    tt = q * GB + t
                    ins = passes(psR[:, tt * E:(tt + 1) * E], lambda h: XR[:, q % 2, h, t], lambda h: wr16[:, h], True, True)
                if q == NC - 1:
                    ins.then_inc(s("logits"), 1)

            def prefix(g):
                pe.wait_ge(s("mask"), g + 1)
                m = M16[:].rearrange("p e t -> p (e t)")
                mm(psR[:, P:2 * P], tri16, m, start=True, stop=True)
                mm(psR[:, 2 * P:3 * P], ones16, m, start=True, stop=True).then_inc(s("prefix"), 1)

            def body(g, tail):
                for j in range(GB):
                    b = g * GB + j
                    xt(b, j % 2)
                    vv(b, j % 2)
                    if tail and j == 0:
                        s2(g - 1, False)
                    if tail and j == 2:
                        rt(g - 1, 0)
                        rt(g - 1, 1)
                    if tail and j == 3:
                        logits(g - 1, 2)
                        logits(g - 1, 3)
                    if j:
                        zz(b - 1, (j - 1) % 2)
                    if tail and j == 1:
                        s2(g - 1, True)
                    if tail and j == 2:
                        logits(g - 1, 0)
                        logits(g - 1, 1)
                        rt(g - 1, 2)
                        rt(g - 1, 3)
                if tail:
                    prefix(g - 1)
                zz(g * GB + 3, 1)

            body(0, False)
            pe.wait_ge(s("router"), 1)
            with pe.Fori(1, NG) as g:
                body(g, True)
            s2(NG - 1, False)
            s2(NG - 1, True)
            for q in range(NC):
                rt(NG - 1, q)
                if q >= 1:
                    logits(NG - 1, q - 1)
            logits(NG - 1, NC - 1)
            prefix(NG - 1)

            pe.wait_ge(s("table"), 1)
            pe.wait_ge(s("f_split"), 3)

            def front(t, u):
                q = u % 2
                if isinstance(t, int):
                    pe.wait_ge(s(f"xs{u}"), 16 * (t // UNROLL + 1))
                    e = pe.value_load(tabi[0:1, 1, t:t + 1], min_val=0, max_val=E - 1)
                else:
                    pe.wait_ge(s(f"xs{u}"), 4 * (t - u) + 16)
                    e = pe.value_load(tabi[0:1, 1, bass.ds(t, 1)], min_val=0, max_val=E - 1)
                if not (isinstance(t, int) and t < 1):
                    pe.wait_ge(s("fx_ready"), t)
                bank = ps[:, 6, 0:SLOT].bitcast(F16)
                for h in range(2):
                    for a in range(2):
                        n = (h * 2 + a) * P
                        ins = nc.tensor.transpose(bank[:, n:n + P], XSh[:, u, a, h * D:(h + 1) * D], ident16)
                ins.then_inc(s("fx_done"), 1)
                pe.wait_ge(s("fx_ready"), t + 1)
                for c in range(HC):
                    if not (isinstance(t, int) and t < 2):
                        pe.wait_ge(s("hid"), 9 * (t - 2) + (1, 3, 6)[c])
                    for n, W in enumerate((W1, W3)):
                        wp = lambda h: W[:, h, bass.ds(e, 1), c * P:(c + 1) * P].rearrange("p a h -> p (a h)")
                        o = ps[:, HC * q + c, n * SLOT:(n + 1) * SLOT]
                        hi, lo = wp(0), wp(1)
                        mm(o, hi, XTf[:, q, 0], start=True, stop=False)
                        mm(o, hi, XTf[:, q, 1], start=False, stop=False)
                        ins = mm(o, lo, XTf[:, q, 0], start=False, stop=True)
                    ins.then_inc(s("h_done"), 1)

            def back(t, u):
                q = u % 2
                if isinstance(t, int):
                    e = pe.value_load(tabi[0:1, 1, t:t + 1], min_val=0, max_val=E - 1)
                else:
                    e = pe.value_load(tabi[0:1, 1, bass.ds(t, 1)], min_val=0, max_val=E - 1)
                pe.wait_ge(s("hid"), 9 * (t + 1))
                if not (isinstance(t, int) and t < 1):
                    pe.wait_ge(s("y_ready"), t)
                for a in range(2):
                    o = ps[:, 7, a * D:(a + 1) * D]
                    for c in range(HC):
                        wp = lambda h: W2[:, h, bass.ds(e, 1), c, :].rearrange("p a d -> p (a d)")
                        ins = passes(o, lambda h: Hh[:, q, h, c, a * P:(a + 1) * P], wp, c == 0, c == HC - 1)
                ins.then_inc(s("y_done"), 1)

            tiles_loop(pe, front, back)


def kernel(x, adj, L0_gnn_alpha_train, L0_gnn_w, L0_gnn_d, L0_gnn_fc_in_w, L0_gnn_fc_in_b, L0_ffn_router_w,
           L0_ffn_w1, L0_ffn_w2, L0_ffn_w3):
    import concourse.bacc as _bacc
    from concourse.bass_utils import run_bass_kernel_spmd as _run

    f = np.ascontiguousarray
    c32, c16, pad = shape_constants()
    w1, w2, w3 = np.asarray(L0_ffn_w1), np.asarray(L0_ffn_w2), np.asarray(L0_ffn_w3)
    arrays = {
        "in_x": f(np.asarray(x)),
        "in_adj": f(np.asarray(adj)),
        "in_adj_t": f(np.asarray(adj).T),
        "in_alpha": f(np.asarray(L0_gnn_alpha_train).reshape(1, N)),
        "in_w_t": f(np.asarray(L0_gnn_w).T),
        "in_d": f(np.asarray(L0_gnn_d).reshape(D, 1)),
        "in_fc_w": f(np.asarray(L0_gnn_fc_in_w)),
        "in_fc_b": f(np.asarray(L0_gnn_fc_in_b).reshape(D, 1)),
        "in_router_t": f(np.asarray(L0_ffn_router_w).T),
        "in_w1_t": f(w1.transpose(2, 0, 1).reshape(D, E * HID)),
        "in_w3_t": f(w3.transpose(2, 0, 1).reshape(D, E * HID)),
        "in_w2_t": f(w2.transpose(2, 0, 1).reshape(HID, E * D)),
        "in_c32": c32,
        "in_c16": c16,
        "in_pad": pad,
    }
    nc = _bacc.Bacc("TRN2", target_bir_lowering=False, num_devices=1)
    args = [nc.dram_tensor(n, a.shape, mybir.dt.from_np(a.dtype), kind="ExternalInput").ap() for n, a in arrays.items()]
    out = nc.dram_tensor("out_rows", (TOKENS + SLOT, D), F32, kind="ExternalOutput").ap()
    gnn_moe_kernel(nc, *args, out)
    r = _run(nc, [arrays], core_ids=[0])
    return np.asarray(r.results[0]["out_rows"])[0:TOKENS].reshape(NB, N, D)
```

```python
from contextlib import ExitStack
from math import comb

import numpy as np

import concourse.bass as bass
from concourse import mybir

F32 = mybir.dt.float32
F16 = mybir.dt.float16
U32 = mybir.dt.uint32
I32 = mybir.dt.int32
ALU = mybir.AluOpType
ACT = mybir.ActivationFunctionType
AX = mybir.AxisListType.X

P = 128
D = 128
N = 512
NC = N // P
NB = 16
TOKENS = NB * N
STEPS = 8
DT = 1.0 / STEPS
EPS = 1e-5
GB = 4
NG = NB // GB
GT = GB * NC
E = 8
HID = 341
HC = 3
SLOT = 256
CAP = TOKENS + SLOT
DUMMY = E * CAP
ROWS = DUMMY + SLOT
NTILES = (2 * TOKENS + E * (SLOT - 1)) // SLOT
NTAB = 80
UNROLL = 8
NY = 4
FIRST = 16
ROW = D + 1 + E

MOVED = 16 * 2 * GB

SA = [0, 10, 14, 12]
SV = [0, 6, 10]
SZ = 6
SW = 6
SU = 6


def p2(n):
    return float(2.0 ** n)


C_ID, C_IOM, C_EB, C_TOK, C_SCAN, C_BIN, C_TILE, C_ONE, C_END = np.cumsum(
    [0, P, E, E, GT, P, 9, NTAB, E]).tolist()


def shape_constants():
    c = np.zeros((P, C_END), np.float32)
    c[:, C_ID:C_ID + P] = np.eye(P)
    c[:, C_IOM:C_IOM + E] = np.arange(E) - E
    c[:, C_EB:C_EB + E] = np.arange(E) * CAP
    tt = np.arange(GT)
    c[:, C_TOK:C_TOK + GT] = ((tt % GB) * NC + tt // GB)[None] * P + np.arange(P)[:, None]
    c[:, C_SCAN:C_SCAN + P] = (np.arange(P) % GT != 0)[None]
    c[:, C_BIN:C_BIN + 9] = [comb(STEPS, j) / 2.0 ** SU for j in range(9)]
    c[:, C_TILE:C_TILE + NTAB] = np.arange(NTAB)
    c[:, C_ONE:C_ONE + E] = 1.0
    h = np.zeros((P, 3 * P), np.float16)
    h[:, 0:P] = np.eye(P)
    h[:, P:2 * P] = np.triu(np.ones((P, P)), 1)
    h[:, 2 * P:] = 1.0
    pad = np.zeros((SLOT, ROW), np.uint32)
    pad[:, D] = TOKENS + np.arange(SLOT)
    return c, h, pad


def wait_apart(eng, sem, value, tiny):
    eng.wait_ge(sem, value)
    tiny()


class Steps:

    def __init__(self, eng, sem, index, per):
        self.eng, self.sem, self.base, self.per, self.n = eng, sem, index * per, per, 0

    def done(self, ins):
        self.n += 1
        return ins.then_inc(self.sem, 1)

    def wait(self):
        self.eng.wait_ge(self.sem, self.base + self.n)

    def wait_apart(self, tiny):
        wait_apart(self.eng, self.sem, self.base + self.n, tiny)

    def end(self):
        assert self.n == self.per, (self.n, self.per)


def gnn_moe_kernel(nc, x, adj, adj_t, alpha, w_t, d, fc_w, fc_b, router_t, w1_t, w3_t, w2_t, c32, c16, pad, out):
    with ExitStack() as ctx:
        def sb(name, shape, dt):
            return ctx.enter_context(nc.sbuf_tensor(name, shape, dt))

        def sem(name):
            return ctx.enter_context(nc.semaphore(name))

        slots = nc.dram_tensor("slots", (ROWS, ROW), U32, kind="Internal").ap()

        k32 = sb("k32", [P, C_END], F32)
        k16 = sb("k16", [P, 3 * P], F16)
        ident16, tri16, ones16 = k16[:, 0:P], k16[:, P:2 * P], k16[:, 2 * P:3 * P]
        ident32 = k32[:, C_ID:C_ID + P]
        X = sb("X", [P, (NB + 2) * NC, D], F32)
        stage = sb("stage", [P, 4096], F32)
        adjT = stage[:, 0:2048].rearrange("p (k n) -> p k n", k=NC)
        adjN = stage[:, 2048:4096].rearrange("p (k n) -> p k n", k=NC)
        B = sb("B", [P, 3, 2, NC, N], F16)
        sigc = sb("sigc", [P, NC], F32)
        alfc = sb("alfc", [P, NC], F32)
        G16 = sb("G16", [P, 2, 3, 3, D], F16)
        W1 = sb("W1", [P, 2, E, HC * P], F16)
        W3 = sb("W3", [P, 2, E, HC * P], F16)
        W2 = sb("W2", [P, 2, E, HC, D], F16)
        wr32 = sb("wr32", [P, E], F32)
        wr16 = sb("wr16", [P, 2, E], F16)
        xn = sb("xn", [P, 2, NC, D], F32)
        Xh = sb("Xh", [P, 2, 2, NC, D], F16)
        XT = sb("XT", [P, 2, 2, N], F16)
        V = sb("V", [P, 2, 2, 2, N], F16)
        Z2 = sb("Z2", [P, 2, NC, GB, D], F16)
        An = Z2[:].rearrange("p a k b d -> p a k (b d)")
        Z1 = sb("Z1", [P, NC, GB, D], F32)
        Uf = sb("Uf", [P, 2, GB * D], F32)
        U = sb("U", [P, 2, NC, GB * D], F16)
        stats = sb("stats", [P, 2, NC, 6], F32)
        mv = sb("mv", [P, 2, NC, 2], F32)
        var = sb("var", [P, 2, NC], F32)
        rstd = sb("rstd", [P, 2, NC], F32)
        stats2 = sb("stats2", [P, 2, NC, 6], F32)
        mv2 = sb("mv2", [P, 2, NC, 2], F32)
        var2 = sb("var2", [P, 2, NC], F32)
        rstd2 = sb("rstd2", [P, 2, NC], F32)
        xn2 = sb("xn2", [P, 2, NC, D], F32)
        spare = sb("spare", [P, 3], F32)
        mhalf = sb("mhalf", [P, NC], F32)
        pay = sb("pay", [P, GT, ROW], U32)
        payh = pay[:].bitcast(F16)
        payf = pay[:].bitcast(F32)
        XR = sb("XR", [P, 2, 2, NC, P], F16)
        biasf = sb("biasf", [P, NC, D], F32)
        uall = sb("uall", [P, NC, 9], F32)
        u16 = sb("u16", [P, 2, NC, 9], F16)
        bt = sb("bt", [P, 9], F32)
        btT = sb("btT", [9, D], F32)
        bcol = sb("bcol", [P, 1], F32)
        dcol = sb("dcol", [P, 2], F32)
        mx = sb("mx", [P, GT], F32)
        dl = sb("dl", [P, GT, E], F32)
        ex = sb("ex", [P, GT, E], F32)
        ssum = sb("ssum", [P, GT], F32)
        key = sb("key", [P, GT, E], F32)
        first = sb("first", [P, GT], F32)
        oh = sb("oh", [P, 2, GT, E], F32)
        rest = sb("rest", [P, GT, E], F32)
        m2 = sb("m2", [P, GT], F32)
        den = sb("den", [P, GT], F32)
        rden = sb("rden", [P, GT], F32)
        M16 = sb("M16", [P, E, GT], F16)
        incl = sb("incl", [P, E, GT], F32)
        pos = sb("pos", [P, E, GT], F32)
        prod = sb("prod", [P, 2, GT, E], F32)
        slotf = sb("slotf", [P, 2, GT], F32)
        idx = sb("idx", [P, 2, GT], U32)
        run = sb("run", [P, E], F32)
        run3 = sb("run3", [P, E], F32)
        tok = sb("tok", [P, GT], F32)
        cnt = sb("cnt", [P, 4, E], F32)
        cnti = sb("cnti", [P, 2, E], I32)
        padrow = sb("padrow", [P, E], I32)

        z1w = Z1[:].rearrange("p k b d -> p (k b d)")
        uw = U[:].rearrange("p h k n -> p (h k n)").bitcast(F32)
        Gf = z1w[:, 0:9 * D].rearrange("p (r i d) -> p r i d", r=3, i=3)
        sig = z1w[:, 9 * D:9 * D + N]
        Wp = uw[:, 0:9 * D].rearrange("p (a d) -> p a d", a=9)
        fcw, wt, wd, idt = (uw[:, (9 + n) * D:(10 + n) * D] for n in range(4))
        alf = Uf[:, 1, :]
        ut = xn2[0:9].rearrange("p a k d -> p (a k d)")[:, 0:N]
        ind = stage[:, 0:3 * NTAB * E].rearrange("p (a t e) -> p a t e", a=3, t=NTAB)
        tabf = stage[:, 3 * NTAB * E:3 * NTAB * E + 6 * NTAB].rearrange("p (a t) -> p a t", a=6)
        tabi = stage[:, 3 * NTAB * E + 6 * NTAB:3 * NTAB * E + (9 + NY) * NTAB].bitcast(I32).rearrange("p (a t) -> p a t", a=3 + NY)

        Bw = B[:].rearrange("p a b k n -> p (a b k n)")
        at = [0]

        def carve(words16, dt, pattern, **k):
            a = Bw[:, at[0]:at[0] + words16]
            at[0] += words16
            if dt != F16:
                a = a.bitcast(dt)
            return a.rearrange(pattern, **k)

        XS = carve(UNROLL * 2 * 2 * ROW, U32, "p (r a w) -> p r a w", r=UNROLL, a=2)
        XSh, XSf = XS.bitcast(F16), XS.bitcast(F32)
        XTf = carve(2 * 2 * SLOT, F16, "p (r h s) -> p r h s", r=2, h=2)
        sil = carve(2 * 2 * HC * SLOT, F32, "p (r c s) -> p r c s", r=2, c=HC)
        hf = xn2[:].rearrange("p a k d -> p (a k d)")[:, 0:HC * SLOT].rearrange("p (c s) -> p c s", c=HC)
        Hh = carve(2 * 2 * HC * SLOT, F16, "p (r h c s) -> p r h c s", r=2, h=2, c=HC)
        Y = xn[:].rearrange("p q (r a) d -> p (q r) a d", a=2)
        assert at[0] <= 3 * 2 * NC * N

        ps = ctx.enter_context(nc.psum_tensor("ps", [P, 8, 512], F32))
        psT = ps[:, 0, :].bitcast(F16).rearrange("p (h n) -> p h n", h=2)
        psR = ps[:, 7, :]

        S = {}

        def s(name):
            if name not in S:
                S[name] = sem(name)
            return S[name]

        x_rows = x.rearrange("b (k p) d -> p (b k) d", p=P)
        out_rows = out[0:TOKENS, :].rearrange("(t p) d -> p t d", p=P)

        def y_free(t, u):
            return FIRST + (32 * (t // NY) if isinstance(t, int) else 32 // NY * (t - u % NY))

        def tiles_loop(eng, early, front, back):
            def step(t, u):
                if not isinstance(t, int) or t + 2 < NTILES:
                    early(t + 2, (u + 2) % UNROLL)
                if not isinstance(t, int) or t + 1 < NTILES:
                    front(t + 1, (u + 1) % UNROLL)
                back(t, u)

            early(0, 0)
            early(1, 1)
            front(0, 0)
            whole = (NTILES - 2) // UNROLL
            for u in range(UNROLL):
                step(u, u)
            with eng.Fori(1, whole) as i:
                for u in range(UNROLL):
                    step(i * UNROLL + u, u)
            for t in range(whole * UNROLL, NTILES):
                step(t, t % UNROLL)

        block = ctx.enter_context(nc.Block())

        @block.sync
        def _(sp):
            sp.dma_start(k32[:], c32).then_inc(s("in_w"), 16)
            sp.dma_start(wt, w_t).then_inc(s("in_w"), 16)
            sp.dma_start(dcol[:, 0:1], d).then_inc(s("in_w"), 16)
            sp.dma_start(fcw, fc_w).then_inc(s("in_w"), 16)
            sp.dma_start(bcol[:], fc_b).then_inc(s("in_w"), 16)
            sp.dma_start(alf, alpha.to_broadcast([P, N])).then_inc(s("in_a"), 16)
            sp.dma_start(adjT, adj_t.rearrange("(k p) n -> p k n", p=P)).then_inc(s("in_a"), 16)
            sp.dma_start(X[:, 0:GT, :], x_rows[:, 0:GT, :]).then_inc(s("in_x"), 16)
            sp.dma_start(adjN, adj.rearrange("(k p) n -> p k n", p=P)).then_inc(s("in_n"), 16)
            with nc.allow_non_contiguous_dma(reason="512 numbers"):
                sp.dma_start(alfc[:], alpha.rearrange("a (k p) -> p (a k)", p=P)).then_inc(s("in_n"), 16)
            sp.dma_start(k16[:], c16).then_inc(s("in_c"), 16)
            sp.dma_start(wr32[:], router_t).then_inc(s("in_c"), 16)
            for g in range(1, NG):
                sp.wait_ge(s("in_x"), 16 * g)
                sp.dma_start(X[:, g * GT:(g + 1) * GT, :], x_rows[:, g * GT:(g + 1) * GT, :]).then_inc(s("in_x"), 16)
            sp.wait_ge(s("a_split"), 2)
            sp.dma_start(stage[:, 0:E * HID], w1_t).then_inc(s("in_f"), 16)
            sp.wait_ge(s("f_split"), 1)
            sp.dma_start(stage[:, 0:E * HID], w3_t).then_inc(s("in_f"), 16)
            sp.wait_ge(s("f_split"), 2)
            for c in range(HC):
                n = min(P, HID - c * P)
                sp.dma_start(stage[0:n, c * E * D:(c + 1) * E * D], w2_t[c * P:c * P + n, :]).then_inc(s("in_f"), 16)
            with sp.Fori(0, NG) as g:
                sp.wait_ge(s("x2_steps"), NC * (g + 1))
                sp.dma_start(out_rows[:, bass.ds(g * GT, GT), :], X[:, bass.ds(g * GT, GT), :]).then_inc(s("out_st"), 16)
            sp.wait_ge(s("out_st"), 16 * NG)
            sp.wait_ge(s("table"), 1)
            for e in range(E):
                r = sp.value_load(padrow[0:1, e:e + 1], min_val=0, max_val=DUMMY - SLOT)
                sp.dma_start(slots[bass.ds(r, SLOT), :], pad).then_inc(s("pad_st"), 16)
            sp.wait_ge(s("pad_st"), 16 * E)
            for n in (2, 3):
                sp.wait_ge(s(f"added{n}"), FIRST)


            def load_tile(col, u, u_free=None):
                r = sp.value_load(tabi[0:1, 0, col], min_val=0, max_val=DUMMY)
                moved = sp.value_load(tabi[0:1, 2, col], min_val=MOVED, max_val=NG * MOVED)
                if u_free is not None:
                    sp.wait_ge(s(f"added{u % NY}"), u_free)
                for q in range(NC):
                    sp.wait_ge(s(f"moved{q}"), moved)
                sp.dma_start(XS[:, u], slots[bass.ds(r, SLOT), :].rearrange("(p a) w -> p a w", a=2)).then_inc(s(f"xs{u}"), 16)

            for t in range(UNROLL):
                load_tile(slice(t, t + 1), t)
            with sp.Fori(1, NTILES // UNROLL) as i:
                for u in range(UNROLL):
                    load_tile(bass.ds(i * UNROLL + u, 1), u, FIRST + 32 * (UNROLL // NY * (i - 1) + u // NY + 1))
            for t in range(NTILES // UNROLL * UNROLL, NTILES):
                load_tile(slice(t, t + 1), t % UNROLL, FIRST + 32 * ((t - UNROLL) // NY + 1))
            for n in range(NY):
                sp.wait_ge(s(f"added{n}"), FIRST + 32 * ((NTILES + NY - 1 - n) // NY))

        @block.gpsimd
        def _(pool):
            tiny = lambda: nc.gpsimd.tensor_tensor(spare[:, 2:3], mhalf[:, 0:1], mhalf[:, 0:1], ALU.add).then_inc(s("tick"), 1)
            nc.gpsimd.memset(mhalf[:], -0.5).then_inc(s("mhalf"), 1)
            nc.gpsimd.memset(Uf[:, 0, :], 0.0).then_inc(s("zero_out"), 1)
            nc.gpsimd.memset(X[:, NB * NC:, :], 0.0).then_inc(s("zero_x"), 1)
            nc.gpsimd.memset(W1[:, :, :, HID:], 0.0)
            nc.gpsimd.memset(W3[:, :, :, HID:], 0.0)
            nc.gpsimd.memset(W2[:, :, :, HC - 1, :], 0.0).then_inc(s("zero_w"), 1)
            nc.gpsimd.memset(uall[:, :, 0:1], p2(SU)).then_inc(s("u0"), 1)
            pool.wait_ge(s("zero_out"), 1)
            for a in range(2):
                nc.gpsimd.dma_start(out[TOKENS + a * P:TOKENS + (a + 1) * P, :], Uf[:, 0, 0:D]).then_inc(s(f"added{a}"), 16)
                nc.gpsimd.dma_start(slots[DUMMY + a * P:DUMMY + (a + 1) * P, :], pad[a * P:(a + 1) * P, :]).then_inc(
                    s(f"added{2 + a}"), 16)
            pool.wait_ge(s("mhalf"), 1)

            def ln1_rstd(b, q):
                pool.wait_ge(s("var"), b + 1)
                nc.gpsimd.tensor_tensor(rstd[:, q], var[:, q], mhalf[:], ALU.pow).then_inc(s("rstd"), 1)

            def ln1_lo(b, q):
                pool.wait_ge(s("xn_hi"), b + 1)
                nc.gpsimd.tensor_tensor(Xh[:, q, 1], xn[:, q], Xh[:, q, 0], ALU.subtract).then_inc(s("xn_split"), 1)

            def route(g):
                wait_apart(pool, s("route"), g + 2, tiny)

            def scatters(tiles):
                for tt in tiles:
                    for k in range(2):
                        nc.gpsimd.indirect_dma_start(
                            out=slots, out_offset=bass.IndirectOffsetOnAxis(ap=idx[:, k, tt:tt + 1], axis=0),
                            in_=pay[:, tt, :], in_offset=None).then_inc(s(f"moved{tt // GB}"), 16)

            def ln2_rstd(g, q):
                pool.wait_ge(s("var2"), NC * g + q + 1)
                nc.gpsimd.tensor_tensor(rstd2[:, q % 2], var2[:, q % 2], mhalf[:], ALU.pow).then_inc(s("rstd2"), 1)

            def bias_add(b):
                pool.wait_ge(s("xn_ready"), b + 1)
                nc.gpsimd.tensor_tensor(X[:, bass.ds(b * NC, NC), :], X[:, bass.ds(b * NC, NC), :], biasf[:],
                                        ALU.add).then_inc(s("x_bias"), 1)

            ln1_rstd(0, 0)
            ln1_lo(0, 0)
            ln1_rstd(1, 1)
            pool.wait_ge(s("bias"), 1)

            def body(g, tail, moves):
                if moves:
                    route(g - 2)
                for j in range(GB):
                    b = g * GB + j
                    ln1_lo(b + 1, (j + 1) % 2)
                    ln1_rstd(b + 2, j % 2)
                    if moves and j == 0:
                        scatters(range(0, 3))
                    if moves and j == 1:
                        scatters(range(6, 8))
                    bias_add(b)
                    if moves and j == 0:
                        scatters(range(3, 6))
                    if moves and j == 1:
                        scatters(range(8, 10))
                    if tail and j == 1:
                        ln2_rstds(g - 1, moves)

            def ln2_rstds(g, moves):
                for q in range(NC):
                    ln2_rstd(g, q)
                    if moves:
                        scatters(((10,), (11,), (12, 13), (14, 15))[q])

            body(0, False, False)
            body(1, True, False)
            with pool.Fori(2, NG) as g:
                body(g, True, True)
            route(NG - 2)
            scatters(range(0, 10))
            ln2_rstds(NG - 1, True)
            route(NG - 1)
            scatters(range(GT))

            pool.wait_ge(s("table"), 1)
            pool.wait_ge(s("out_st"), 16 * NG)

            def add_tile(t, u, col):
                before = [pool.value_load(tabi[0:1, 3 + n, col], min_val=FIRST, max_val=32 * NTAB) for n in range(NY)]
                for n in range(NY):
                    pool.wait_ge(s(f"added{n}"), before[n])
                pool.wait_ge(s("tick"), NG + t)
                wait_apart(pool, s("y_ready"), t + 1, tiny)
                for a in range(2):
                    nc.gpsimd.indirect_dma_start(
                        out=out, out_offset=bass.IndirectOffsetOnAxis(ap=XS[:, u, a, D:D + 1], axis=0),
                        in_=Y[:, u % NY, a, :], in_offset=None, compute_op=ALU.add).then_inc(s(f"added{u % NY}"), 16)

            with pool.Fori(0, NTILES // UNROLL) as i:
                for u in range(UNROLL):
                    add_tile(i * UNROLL + u, u, bass.ds(i * UNROLL + u, 1))
            for t in range(NTILES // UNROLL * UNROLL, NTILES):
                add_tile(t, t % UNROLL, slice(t, t + 1))

        @block.scalar
        def _(act):
            copy = lambda o, i, sc=1.0: nc.scalar.activation(o, i, ACT.Copy, scale=sc)
            act.wait_ge(s("in_a"), 32)
            nc.scalar.activation(sig, alf, ACT.Sigmoid).then_inc(s("sig"), 1)
            act.wait_ge(s("in_n"), 32)
            nc.scalar.activation(sigc[:], alfc[:], ACT.Sigmoid).then_inc(s("sig"), 1)

            def ln1_hi(b, q):
                act.wait_ge(s("xn_ready"), b + 1)
                copy(Xh[:, q, 0], xn[:, q]).then_inc(s("xn_hi"), 1)

            ln1_hi(0, 0)
            act.wait_ge(s("a_full"), 1)
            copy(B[:, 0, 0], adjT).then_inc(s("a_hi"), 1)
            act.wait_ge(s("a_full"), 2)
            copy(An[:, 0], adjN).then_inc(s("a_hi"), 1)
            for j in (1, 2):
                for i in range(NC):
                    act.wait_ge(s("pow_done"), (j - 1) * NC + i + 1)
                    copy(B[:, j, 0, i], ps[:, 4 + i, :], p2(SA[j + 1] - SA[1] - SA[j])).then_inc(s("pow_hi"), 1)

            def xt_evac(b, q):
                act.wait_ge(s("xt_done"), b + 1)
                copy(XT[:, q], psT).then_inc(s("xt_ready"), 1)

            def v_hi(b, q, r):
                act.wait_ge(s("v_done"), 2 * b + r + 1)
                copy(V[:, q, 0, r], ps[:, 1 + r, :], p2(SV[r + 1] - SA[r + 1])).then_inc(s("v_hi"), 1)

            def z_hi(b, j, cs):
                for c in cs:
                    act.wait_ge(s("z_done"), NC * b + c + 1)
                    z = ps[:, 3 + c % 2, 0:3 * D]
                    copy(Z2[:, 0, c, j, :], z[:, 0:D], p2(-SZ))
                    copy(Z1[:, c, j, :], z[:, D:2 * D], p2(-SZ)).then_inc(s("z_hi"), 1)

            def u_hi(g):
                for i in range(NC):
                    act.wait_ge(s("u_full"), NC * g + i + 1)
                    copy(U[:, 0, i], Uf[:, i % 2]).then_inc(s("u_hi"), 1)

            def ln2_hi(g, q, moved):
                act.wait_ge(s("xn2_ready"), NC * g + q + 1)
                if moved:
                    act.wait_ge(s(f"moved{q}"), MOVED * g)
                copy(payh[:, q * GB:(q + 1) * GB, 0:D], xn2[:, q % 2]).then_inc(s("xn2_hi"), 1)

            def rt_evac(g, q):
                act.wait_ge(s("rt_done"), NC * g + q + 1)
                copy(XR[:, q % 2].rearrange("p h t n -> p (h t n)"), ps[:, 5 + q % 2, :].bitcast(F16)).then_inc(s("rt_ready"), 1)

            def expo(g):
                act.wait_ge(s("dl_ready"), g + 1)
                nc.scalar.activation(ex[:], dl[:], ACT.Exp, scale=p2(-SW)).then_inc(s("ex_ready"), 1)

            def weights(k):
                if k < 2:
                    act.wait_ge(s("in_f"), 16 * (k + 1))
                    src = stage[:, 0:E * HID].rearrange("p (e h) -> p e h", e=E)
                    copy((W1, W3)[k][:, 0, :, 0:HID], src, p2(SW)).then_inc(s("f_hi"), 1)
                else:
                    act.wait_ge(s("in_f"), 16 * (2 + HC))
                    act.wait_ge(s("zero_w"), 1)
                    for c in range(HC):
                        n = min(P, HID - c * P)
                        src = stage[0:n, c * E * D:(c + 1) * E * D].rearrange("p (e d) -> p e d", e=E)
                        ins = copy(W2[0:n, 0, :, c, :], src, p2(SW))
                    ins.then_inc(s("f_hi"), 1)

            def body(g, tail, moved):
                for j in range(GB):
                    b = g * GB + j
                    xt_evac(b, j % 2)
                    if tail and j == 3:
                        rt_evac(g - 1, 2)
                        rt_evac(g - 1, 3)
                    if tail and j == 2:
                        ln2_hi(g - 1, 2, moved)
                    ln1_hi(b + 1, (j + 1) % 2)
                    v_hi(b, j % 2, 0)
                    v_hi(b, j % 2, 1)
                    if tail and j == 2:
                        ln2_hi(g - 1, 3, moved)
                    if tail and j == 0:
                        u_hi(g - 1)
                    if j:
                        z_hi(b - 1, j - 1, (0, 1))
                    if tail and j == 3:
                        expo(g - 1)
                    if j:
                        z_hi(b - 1, j - 1, (2, 3))
                    if tail and j == 1:
                        for q in range(2):
                            ln2_hi(g - 1, q, moved)
                    if tail and j == 2:
                        rt_evac(g - 1, 0)
                        rt_evac(g - 1, 1)
                    if not tail and j < 3:
                        weights(j)
                z_hi(g * GB + 3, 3, range(NC))

            body(0, False, False)
            body(1, True, False)
            with act.Fori(2, NG) as g:
                body(g, True, True)
            u_hi(NG - 1)
            for q in range(NC):
                ln2_hi(NG - 1, q, True)
            for q in range(NC):
                rt_evac(NG - 1, q)
            expo(NG - 1)

            def xt(t, u):
                q = u % 2
                act.reg_load(expert[u], tabi[0:1, 1, t:t + 1] if isinstance(t, int) else tabi[0:1, 1, bass.ds(t, 1)])
                act.wait_ge(s("fx_done"), t + 1)
                copy(XTf[:, q], ps[:, 6, 0:SLOT].bitcast(F16).rearrange("p (h s) -> p h s", h=2)).then_inc(s("fx_ready"), 1)

            def silu(t, q):
                for c in range(HC):
                    act.wait_ge(s("h_done"), HC * t + c + 1)
                    nc.scalar.activation(sil[:, q, c], ps[:, HC * q + c, 0:SLOT], ACT.Silu,
                                         scale=p2(-SW)).then_inc(s("sil"), 1)

            expert = [act.alloc_register(f"act_expert{u}") for u in range(UNROLL)]

            def y_out(t, u):
                e = act.snap(expert[u], min_val=0, max_val=E - 1)
                act.wait_ge(s("y_done"), t + 1)
                if not (isinstance(t, int) and t < NY):
                    act.wait_ge(s(f"added{u % NY}"), y_free(t, u))
                for a in range(2):
                    ins = nc.scalar.activation(Y[:, u % NY, a], ps[:, 7, a * D:(a + 1) * D], ACT.Identity,
                                               scale=XSf[:, u, a, bass.ds(e + (D + 1), 1)])
                ins.then_inc(s("y_ready"), 1)

            act.wait_ge(s("table"), 1)
            tiles_loop(act, xt, lambda t, u: silu(t, u % 2), y_out)

        @block.vector
        def _(dve):
            v = nc.vector
            tiny = lambda: v.tensor_copy(spare[:, 0:1], spare[:, 1:2])
            v.memset(spare[:, 0:2], 0.0).then_inc(s("spare"), 1)
            dve.wait_ge(s("spare"), 1)

            def ln_stats(rows, q, name, index, st, m, va, out_sem):
                st_, m_, va_ = st[:, q], m[:, q], va[:, q]
                steps = Steps(dve, s(name), index, 2)
                tiny()
                for c in range(NC):
                    ins = v.bn_stats(st_[:, c, :], rows(c))
                steps.done(ins)
                steps.wait_apart(tiny)
                for c in range(NC):
                    ins = v.bn_aggr(m_[:, c, :], st_[:, c, :])
                steps.done(ins)
                steps.wait()
                v.tensor_scalar(va_, m_[:, :, 1], EPS, None, ALU.add).then_inc(s(out_sem), 1)
                steps.end()

            def ln1_stats(b, q):
                ln_stats(lambda c: X[:, b * NC + c, :] if isinstance(b, int) else X[:, bass.ds(b * NC + c, 1), :].rearrange("p a d -> p (a d)"),
                         q, "ln1_st", b, stats, mv, var, "var")

            def ln1_norm(b, q):
                dve.wait_ge(s("rstd"), b + 1)
                for c in range(NC):
                    row = X[:, b * NC + c, :] if isinstance(b, int) else X[:, bass.ds(b * NC + c, 1), :].rearrange("p a d -> p (a d)")
                    ins = v.tensor_scalar(xn[:, q, c], row, mv[:, q, c, 0:1], rstd[:, q, c:c + 1], ALU.subtract, ALU.mult)
                ins.then_inc(s("xn_ready"), 1)

            w = Steps(dve, s("w_steps"), 0, 18)
            dve.wait_ge(s("in_w"), 80)
            w.done(v.tensor_scalar(dcol[:, 1:2], dcol[:, 0:1], 0.0, 1.0, ALU.max, ALU.min))
            v.tensor_scalar(idt, ident32, 1.0 - DT, None, ALU.mult)
            w.done(v.tensor_copy(Wp[:, 0], ident32))
            w.wait()
            v.tensor_scalar(wd, wt, dcol[:, 1:2], None, ALU.mult).then_inc(s("wd"), 1)
            dve.wait_ge(s("wp_done"), 1)
            v.scalar_tensor_tensor(Wp[:, 1], ps[:, 7, 0:D], DT, idt, ALU.mult, ALU.add).then_inc(s("wp"), 1)
            dve.wait_ge(s("wp_done"), 2)
            v.tensor_copy(Wp[:, 2], ps[:, 6, 0:D]).then_inc(s("wp"), 1)
            dve.wait_ge(s("in_x"), 16)
            dve.wait_ge(s("wp_done"), 3)
            v.tensor_copy(Wp[:, 3:5], ps[:, 5, 0:2 * D].rearrange("p (a d) -> p a d", a=2)).then_inc(s("wp"), 1)
            ln1_stats(0, 0)
            dve.wait_ge(s("wp_done"), 4)
            v.tensor_copy(Wp[:, 5:9], ps[:, 4, 0:4 * D].rearrange("p (a d) -> p a d", a=4)).then_inc(s("wp"), 1)
            ln1_norm(0, 0)
            ln1_stats(1, 1)
            a = Steps(dve, s("a_steps"), 0, 2)
            dve.wait_ge(s("sig"), 1)
            for k in range(NC):
                blk = adjT[:, k, k * P:(k + 1) * P]
                ins = v.tensor_tensor(blk, blk, ident32, ALU.subtract)
            a.done(ins)
            a.wait()
            v.scalar_tensor_tensor(adjT, adjT, DT * 0.5 * p2(SA[1]), sig.unsqueeze(1).to_broadcast([P, NC, N]),
                                   ALU.mult, ALU.mult).then_inc(s("a_full"), 1)
            dve.wait_ge(s("sig"), 2)
            for k in range(NC):
                blk = adjN[:, k, k * P:(k + 1) * P]
                ins = v.tensor_tensor(blk, blk, ident32, ALU.subtract)
            a.done(ins)
            a.wait()
            for k in range(NC):
                ins = v.tensor_scalar(adjN[:, k, :], adjN[:, k, :], sigc[:, k:k + 1], DT * 0.5 * p2(SA[1]), ALU.mult, ALU.mult)
            ins.then_inc(s("a_full"), 1)
            dve.wait_ge(s("a_hi"), 1)
            v.tensor_tensor(B[:, 0, 1], adjT, B[:, 0, 0], ALU.subtract).then_inc(s("a_split"), 1)
            dve.wait_ge(s("a_hi"), 2)
            v.tensor_tensor(An[:, 1], adjN, An[:, 0], ALU.subtract).then_inc(s("a_split"), 1)
            dve.wait_ge(s("in_c"), 32)
            w.done(v.tensor_scalar(wr16[:, 0], wr32[:], p2(SW), None, ALU.mult))
            w.wait()
            v.scalar_tensor_tensor(wr16[:, 1], wr32[:], p2(SW), wr16[:, 0], ALU.mult, ALU.subtract).then_inc(s("router"), 1)
            dve.wait_ge(s("fw_done"), 3)
            for p in range(9):
                i, r = divmod(8 - p, 3)
                ins = v.tensor_scalar(Gf[:, r, 2 - i], ps[:, 1 + p // 3, (p % 3) * D:(p % 3 + 1) * D],
                                      comb(STEPS, p) * p2(SZ - SV[r]), None, ALU.mult)
            ins.then_inc(s("g_psum"), 1)
            dve.wait_ge(s("g_psum"), 1)
            for p in range(STEPS):
                for j in range(STEPS - p):
                    i, r = divmod(j, 3)
                    ins = v.scalar_tensor_tensor(Gf[:, r, 2 - i], Wp[:, p], DT * comb(p + j, j) * p2(SZ - SV[r]),
                                                 Gf[:, r, 2 - i], ALU.mult, ALU.add)
                w.done(ins)
                w.wait()
            w.done(v.tensor_copy(G16[:, 0], Gf))
            w.wait()
            v.tensor_tensor(G16[:, 1], Gf, G16[:, 0], ALU.subtract).then_inc(s("g_split"), 1)
            for j in (1, 2):
                for i in range(NC):
                    dve.wait_ge(s("pow_hi"), (j - 1) * NC + i + 1)
                    v.scalar_tensor_tensor(B[:, j, 1, i], ps[:, 4 + i, :], p2(SA[j + 1] - SA[1] - SA[j]), B[:, j, 0, i],
                                           ALU.mult, ALU.subtract).then_inc(s("pow_split"), 1)
            def u_split(a0, a1):
                w.done(v.tensor_copy(u16[:, 0, :, a0:a1], uall[:, :, a0:a1]))
                w.wait()
                v.tensor_tensor(u16[:, 1, :, a0:a1], uall[:, :, a0:a1], u16[:, 0, :, a0:a1], ALU.subtract).then_inc(s("u_split"), 1)

            dve.wait_ge(s("u0"), 1)
            dve.wait_ge(s("us_done"), 1)
            for r in range(2):
                ins = v.tensor_scalar(uall[:, :, r + 1:r + 2], ps[:, 0, 0:8].rearrange("p (i r) -> p i r", r=2)[:, :, r:r + 1],
                                      p2(SU - SA[r + 1]), None, ALU.mult)
            w.done(ins)
            w.wait()
            u_split(0, 3)
            for n in (1, 2):
                dve.wait_ge(s("us_done"), 1 + n)
                w.done(v.tensor_scalar(uall[:, :, 3 * n:3 * n + 3], ps[:, 0, 12 * n:12 * n + 12].rearrange("p (i r) -> p i r", r=3),
                                       p2(-SA[3]), None, ALU.mult))
                w.wait()
                if n == 1:
                    u_split(3, 6)
            dve.wait_ge(s("bw_done"), 1)
            v.tensor_tensor(bt[:], ps[:, 0, 64:73], k32[:, C_BIN:C_BIN + 9], ALU.mult).then_inc(s("ub"), 1)
            dve.wait_ge(s("ut_done"), 1)
            w.done(v.tensor_copy(ut, ps[0:9, 4, :]))
            v.tensor_copy(btT[:], ps[0:9, 5, 0:D]).then_inc(s("ub"), 1)
            dve.wait_ge(s("bias_done"), 1)
            v.tensor_copy(biasf[:], ps[:, 6, :].rearrange("p (k d) -> p k d", k=NC)).then_inc(s("bias"), 1)
            v.tensor_copy(run[:], k32[:, C_EB:C_EB + E]).then_inc(s("route"), 1)
            w.done(v.tensor_copy(tok[:], k32[:, C_TOK:C_TOK + GT]))
            w.wait()
            dve.wait_ge(s("zero_x"), 1)
            dve.wait_ge(s("zero_out"), 1)
            for a in range(2):
                dve.wait_ge(s(f"added{a}"), FIRST)

            def v_lo(b, q, r):
                dve.wait_ge(s("v_hi"), 2 * b + r + 1)
                v.scalar_tensor_tensor(V[:, q, 1, r], ps[:, 1 + r, :], p2(SV[r + 1] - SA[r + 1]), V[:, q, 0, r],
                                       ALU.mult, ALU.subtract).then_inc(s("v_split"), 1)

            def z_lo(b, j, cs):
                for c in cs:
                    if c == 0:
                        dve.wait_ge(s("x_bias"), b + 1)
                    dve.wait_ge(s("z_hi"), NC * b + c + 1)
                    z = ps[:, 3 + c % 2, 0:3 * D]
                    if isinstance(b, int):
                        row = X[:, b * NC + c, :]
                    else:
                        row = X[:, bass.ds(b * NC + c, 1), :].rearrange("p a d -> p (a d)")
                    v.scalar_tensor_tensor(row, z[:, 2 * D:3 * D], p2(-SZ), row, ALU.mult, ALU.add)
                    v.scalar_tensor_tensor(Z2[:, 1, c, j, :], z[:, 0:D], p2(-SZ), Z2[:, 0, c, j, :],
                                           ALU.mult, ALU.subtract).then_inc(s("z_split"), 1)

            def u_all(g):
                def lo(i):
                    dve.wait_ge(s("u_hi"), NC * g + i + 1)
                    v.tensor_tensor(U[:, 1, i], Uf[:, i % 2], U[:, 0, i], ALU.subtract).then_inc(s("u_lo"), 1)
                for i in range(NC):
                    dve.wait_ge(s("s2_done"), 2 * NC * g + i + 1)
                    if i >= 2:
                        dve.wait_ge(s("u_lo"), NC * g + i - 1)
                    v.scalar_tensor_tensor(Uf[:, i % 2], ps[:, 5 + i % 2, :], p2(-SA[3]), Z1[:, i].rearrange("p b d -> p (b d)"),
                                           ALU.mult, ALU.add).then_inc(s("u_full"), 1)
                    if i:
                        lo(i - 1)
                lo(NC - 1)

            def x2_chunk(g, q):
                st = Steps(dve, s("x2_steps"), g * NC + q, 1)
                dve.wait_ge(s("s2_done"), 2 * NC * g + NC + q + 1)
                rows = X[:, bass.ds(g * GT, GT), :].rearrange("p (b k) d -> p b k d", k=NC)[:, :, q, :]
                st.done(v.scalar_tensor_tensor(rows, ps[:, 5 + q % 2, :].rearrange("p (b d) -> p b d", b=GB), p2(-SA[3]), rows,
                                               ALU.mult, ALU.add))
                st.wait()
                row = lambda c: rows[:, c, :]
                ln_stats(row, q % 2, "ln2_st", g * NC + q, stats2, mv2, var2, "var2")

            def ln2_norm(g, q):
                rows = X[:, bass.ds(g * GT, GT), :].rearrange("p (b k) d -> p b k d", k=NC)[:, :, q, :]
                dve.wait_ge(s("rstd2"), NC * g + q + 1)
                for c in range(GB):
                    ins = v.tensor_scalar(xn2[:, q % 2, c], rows[:, c, :], mv2[:, q % 2, c, 0:1], rstd2[:, q % 2, c:c + 1],
                                          ALU.subtract, ALU.mult)
                ins.then_inc(s("xn2_ready"), 1)

            def ln2_lo(g, q):
                dve.wait_ge(s("xn2_hi"), NC * g + q + 1)
                v.tensor_tensor(payh[:, q * GB:(q + 1) * GB, D:2 * D], xn2[:, q % 2], payh[:, q * GB:(q + 1) * GB, 0:D],
                                ALU.subtract).then_inc(s("xn2_lo"), 1)

            lg = psR[:, 0:P].rearrange("p (t e) -> p t e", e=E)
            iom = k32[:, C_IOM:C_IOM + E].unsqueeze(1).to_broadcast([P, GT, E])
            wide = lambda a: a.unsqueeze(2).to_broadcast([P, GT, E])

            def first_choice(g):
                st = Steps(dve, s("first"), g, 4)
                dve.wait_ge(s("logits"), g + 1)
                st.done(v.tensor_reduce(mx[:], lg, AX, ALU.max))
                st.wait()
                v.tensor_tensor(dl[:], lg, wide(mx[:]), ALU.subtract).then_inc(s("dl_ready"), 1)
                dve.wait_ge(s("dl_ready"), g + 1)
                st.done(v.scalar_tensor_tensor(key[:], dl[:], 0.0, iom, ALU.is_equal, ALU.mult))
                st.wait()
                st.done(v.tensor_reduce(first[:], key[:], AX, ALU.min))
                st.wait()
                st.done(v.tensor_tensor(oh[:, 0], key[:], wide(first[:]), ALU.is_equal))
                st.end()

            def second_choice(g):
                st = Steps(dve, s("second"), g, 6)
                dve.wait_ge(s("ex_ready"), g + 1)
                dve.wait_ge(s("first"), 4 * (g + 1))
                st.done(v.scalar_tensor_tensor(rest[:], oh[:, 0], -2.0, ex[:], ALU.mult, ALU.add))
                st.wait()
                st.done(v.tensor_reduce(m2[:], rest[:], AX, ALU.max))
                v.tensor_reduce(ssum[:], ex[:], AX, ALU.add)
                st.wait()
                st.done(v.tensor_tensor(key[:], rest[:], wide(m2[:]), ALU.is_equal))
                st.wait()
                st.done(v.tensor_tensor(key[:], key[:], iom, ALU.mult))
                st.wait()
                st.done(v.tensor_reduce(first[:], key[:], AX, ALU.min))
                st.wait()
                st.done(v.tensor_tensor(oh[:, 1], key[:], wide(first[:]), ALU.is_equal))
                st.wait()
                v.tensor_tensor(M16[:].rearrange("p e t -> p t e"), oh[:, 0], oh[:, 1], ALU.add).then_inc(s("mask"), 1)
                st.end()

            def gates(g):
                st = Steps(dve, s("gates"), g, 5)
                dve.wait_ge(s("mask"), g + 1)
                st.done(v.scalar_tensor_tensor(den[:], ssum[:], 1e-9, m2[:], ALU.mult, ALU.add))
                v.tensor_tensor(rest[:], M16[:].rearrange("p e t -> p t e"), ex[:], ALU.mult)
                st.wait()
                st.done(v.tensor_scalar(den[:], den[:], 1.0, p2(SW), ALU.add, ALU.mult))
                v.tensor_copy(pay[:, :, D], tok[:])
                st.wait()
                st.done(v.reciprocal(rden[:], den[:]))
                st.done(v.tensor_scalar(tok[:], tok[:], float(GT * P), None, ALU.add))
                st.wait()
                st.done(v.tensor_tensor(payf[:, :, D + 1:], rest[:], wide(rden[:]), ALU.mult))
                st.end()

            def place(g):
                st = Steps(dve, s("place"), g, 6)
                dve.wait_ge(s("prefix"), g + 1)
                total = psR[:, 2 * P:3 * P]
                before = psR[:, P:2 * P].rearrange("p (e t) -> p e t", e=E)
                st.done(v.tensor_tensor_scan(incl[:].rearrange("p e t -> p (e t)"), k32[:, C_SCAN:C_SCAN + P], total, 0.0,
                                             ALU.mult, ALU.add))
                st.wait()
                st.done(v.tensor_tensor(pos[:], incl[:], total.rearrange("p (e t) -> p e t", e=E), ALU.subtract))
                st.wait()
                st.done(v.tensor_tensor(pos[:], pos[:], before, ALU.add))
                st.wait()
                st.done(v.tensor_tensor(pos[:], pos[:], run[:].unsqueeze(2).to_broadcast([P, E, GT]), ALU.add))
                st.wait()
                v.tensor_tensor(run[:], run[:], incl[:, :, GT - 1], ALU.add)
                for k in range(2):
                    ins = v.tensor_tensor(prod[:, k], oh[:, k], pos[:].rearrange("p e t -> p t e"), ALU.mult)
                st.done(ins)
                st.wait()
                st.done(v.tensor_reduce(slotf[:].rearrange("p k t -> p (k t)"), prod[:].rearrange("p k t e -> p (k t) e"),
                                        AX, ALU.add))
                st.wait()
                dve.wait_ge(s("gates"), 5 * (g + 1))
                v.tensor_copy(idx[:], slotf[:]).then_inc(s("route"), 1)
                st.end()

            def weights(k):
                dve.wait_ge(s("f_hi"), k + 1)
                if k < 2:
                    src = stage[:, 0:E * HID].rearrange("p (e h) -> p e h", e=E)
                    t = (W1, W3)[k]
                    ins = v.scalar_tensor_tensor(t[:, 1, :, 0:HID], src, p2(SW), t[:, 0, :, 0:HID], ALU.mult, ALU.subtract)
                else:
                    dve.wait_ge(s("zero_w"), 1)
                    for c in range(HC):
                        n = min(P, HID - c * P)
                        src = stage[0:n, c * E * D:(c + 1) * E * D].rearrange("p (e d) -> p e d", e=E)
                        ins = v.scalar_tensor_tensor(W2[0:n, 1, :, c, :], src, p2(SW), W2[0:n, 0, :, c, :],
                                                     ALU.mult, ALU.subtract)
                ins.then_inc(s("f_split"), 1)

            def body(g, tail):
                for j in range(GB):
                    b = g * GB + j
                    q, n = j % 2, (j + 1) % 2
                    if tail and j == 2:
                        ln2_norm(g - 1, 2)
                        ln1_norm(b + 1, n)
                        ln2_lo(g - 1, 2)
                    else:
                        ln1_norm(b + 1, n)
                    v_lo(b, q, 0)
                    if j == 2:
                        dve.wait_ge(s("in_x"), 16 * (min(g + 2, NG) if isinstance(g, int) else NG))
                    ln1_stats(b + 2, q)
                    if tail and j == 2:
                        ln2_norm(g - 1, 3)
                    v_lo(b, q, 1)
                    if tail and j == 0:
                        u_all(g - 1)
                    if j:
                        z_lo(b - 1, j - 1, (0,))
                    if tail and j == 2:
                        ln2_lo(g - 1, 3)
                    if tail and j == 3:
                        first_choice(g - 1)
                    if j:
                        z_lo(b - 1, j - 1, (1, 2, 3))
                    if tail and j == 3:
                        second_choice(g - 1)
                    if tail and j == 1:
                        x2_chunk(g - 1, 0)
                        x2_chunk(g - 1, 1)
                        ln2_norm(g - 1, 0)
                        ln2_lo(g - 1, 0)
                        x2_chunk(g - 1, 2)
                        ln2_norm(g - 1, 1)
                        ln2_lo(g - 1, 1)
                        x2_chunk(g - 1, 3)
                    if not tail and j < 3:
                        weights(j)
                z_lo(g * GB + 3, 3, (0,))
                if tail:
                    gates(g - 1)
                z_lo(g * GB + 3, 3, (1, 2, 3))
                if tail:
                    place(g - 1)

            body(0, False)
            with dve.Fori(1, NG) as g:
                body(g, True)
            u_all(NG - 1)
            x2_chunk(NG - 1, 0)
            x2_chunk(NG - 1, 1)
            ln2_norm(NG - 1, 0)
            ln2_lo(NG - 1, 0)
            x2_chunk(NG - 1, 2)
            ln2_norm(NG - 1, 1)
            ln2_lo(NG - 1, 1)
            x2_chunk(NG - 1, 3)
            for q in (2, 3):
                ln2_norm(NG - 1, q)
                ln2_lo(NG - 1, q)
            st = Steps(dve, s("saved"), 0, 1)
            st.done(v.tensor_copy(run3[:], run[:]))
            st.wait()
            first_choice(NG - 1)
            second_choice(NG - 1)
            gates(NG - 1)
            place(NG - 1)

            st = Steps(dve, s("tab_steps"), 0, 19)
            first_row = k32[:, C_EB:C_EB + E]
            dve.wait_ge(s("route"), NG + 1)
            st.done(v.tensor_tensor(cnt[:, 0], run[:], first_row, ALU.subtract))
            v.tensor_copy(padrow[:], run[:])
            st.wait()
            st.done(v.tensor_scalar(cnti[:, 0], cnt[:, 0], float(SLOT - 1), None, ALU.add))
            st.wait()
            st.done(v.tensor_scalar(cnti[:, 1], cnti[:, 0], SLOT.bit_length() - 1, None, ALU.logical_shift_right))
            st.wait()
            st.done(v.tensor_copy(cnt[:, 1], cnti[:, 1]))
            st.wait()
            st.done(v.tensor_tensor_scan(cnt[:, 2], k32[:, C_ONE:C_ONE + E], cnt[:, 1], 0.0, ALU.mult, ALU.add))
            st.done(v.tensor_scalar(cnt[:, 3], cnt[:, 1], -float(SLOT), float(CAP), ALU.mult, ALU.add))
            st.wait()
            over = lambda a: a.unsqueeze(1).to_broadcast([P, NTAB, E])
            tile_no = k32[:, C_TILE:C_TILE + NTAB]
            st.done(v.tensor_tensor(ind[:, 0], tile_no.unsqueeze(2).to_broadcast([P, NTAB, E]), over(cnt[:, 2]), ALU.is_ge))
            st.wait()
            v.tensor_tensor(ind[:, 1], ind[:, 0], over(cnt[:, 3]), ALU.mult)
            st.done(v.tensor_tensor(ind[:, 2], ind[:, 0], over(cnt[:, 1]), ALU.mult))
            st.wait()
            st.done(v.tensor_reduce(tabf[:, 0:3].rearrange("p a t -> p (a t)"), ind[:].rearrange("p a t e -> p (a t) e"),
                                    AX, ALU.add))
            st.wait()
            v.tensor_scalar(tabf[:, 5], tile_no, cnt[:, 2, E - 1:E], 0.0, ALU.subtract, ALU.max).then_inc(s("unneeded"), 1)
            dve.wait_ge(s("unneeded"), 1)
            st.done(v.tensor_tensor(tabf[:, 2], tabf[:, 2], tabf[:, 5], ALU.add))
            st.wait()
            st.done(v.scalar_tensor_tensor(tabf[:, 3], tile_no, float(SLOT), tabf[:, 1], ALU.mult, ALU.add))
            st.wait()
            v.tensor_scalar(tabi[:, 1], tabf[:, 0], float(E - 1), None, ALU.min)
            v.tensor_scalar(tabi[:, 0], tabf[:, 3], float(DUMMY), None, ALU.min)
            for n in range(NY):
                ins = v.tensor_scalar(tabi[:, 3 + n], tabf[:, 2], float(NY - 1 - n), None, ALU.add)
            st.done(ins)
            st.wait()
            waits = tabi[:, 3:3 + NY]
            st.done(v.tensor_scalar(waits, waits, NY.bit_length() - 1, 5, ALU.logical_shift_right, ALU.logical_shift_left))
            st.done(v.tensor_scalar(tabf[:, 3], tabf[:, 3], float(SLOT), None, ALU.add))
            st.wait()
            st.done(v.tensor_scalar(waits, waits, FIRST, None, ALU.add))
            st.done(v.tensor_tensor(ind[:, 0], tabf[:, 3].unsqueeze(2).to_broadcast([P, NTAB, E]), over(run3[:]), ALU.is_le))
            st.wait()
            st.done(v.tensor_reduce(tabf[:, 5], ind[:, 0], AX, ALU.add))
            st.wait()
            st.done(v.tensor_tensor(tabf[:, 5], tabf[:, 5], tabf[:, 0], ALU.add))
            st.wait()
            st.done(v.tensor_scalar(tabf[:, 5], tabf[:, 5], float(E - 1), 0.0, ALU.subtract, ALU.max))
            st.wait()
            v.tensor_scalar(tabi[:, 2], tabf[:, 5], -float(MOVED), float(NG * MOVED), ALU.mult, ALU.add).then_inc(s("table"), 1)
            st.end()

            def hidden(t, q):
                st = Steps(dve, s("hid"), t, 3 * HC)

                def whole(c):
                    dve.wait_ge(s("sil"), HC * t + c + 1)
                    st.done(v.scalar_tensor_tensor(hf[:, c], ps[:, HC * q + c, SLOT:2 * SLOT], p2(-SW), sil[:, q, c],
                                                   ALU.mult, ALU.mult))

                def hi(c, n):
                    dve.wait_ge(s("hid"), st.base + n)
                    st.done(v.tensor_copy(Hh[:, q, 0, c], hf[:, c]))

                def lo(c, n):
                    dve.wait_ge(s("hid"), st.base + n)
                    st.done(v.tensor_tensor(Hh[:, q, 1, c], hf[:, c], Hh[:, q, 0, c], ALU.subtract))

                whole(0); hi(0, 1); whole(1); lo(0, 2); hi(1, 3); whole(2); lo(1, 5); hi(2, 6); lo(2, 8)
                st.end()

            tiles_loop(dve, lambda t, u: None, lambda t, u: hidden(t, u % 2), lambda t, u: None)

        @block.tensor
        def _(pe):
            mm = nc.tensor.matmul

            def passes(out_ap, lhs, rhs, first, last):
                mm(out_ap, lhs(0), rhs(0), start=first, stop=False)
                mm(out_ap, lhs(0), rhs(1), start=False, stop=False)
                return mm(out_ap, lhs(1), rhs(0), start=False, stop=last)

            pe.wait_ge(s("in_w"), 80)
            pe.wait_ge(s("wd"), 1)
            mm(ps[:, 7, 0:D], wd, wt, start=True, stop=True).then_inc(s("wp_done"), 1)
            pe.wait_ge(s("wp"), 1)
            mm(ps[:, 6, 0:D], Wp[:, 1], Wp[:, 1], start=True, stop=True).then_inc(s("wp_done"), 1)
            pe.wait_ge(s("wp"), 2)
            mm(ps[:, 5, 0:2 * D], Wp[:, 2], Wp[:, 1:3].rearrange("p a d -> p (a d)"), start=True, stop=True).then_inc(s("wp_done"), 1)
            pe.wait_ge(s("wp"), 3)
            mm(ps[:, 4, :], Wp[:, 4], Wp[:, 1:5].rearrange("p a d -> p (a d)"), start=True, stop=True).then_inc(s("wp_done"), 1)
            pe.wait_ge(s("wp"), 4)
            for n in range(3):
                mm(ps[:, 1 + n, 0:3 * D], fcw, Wp[:, 3 * n:3 * n + 3].rearrange("p a d -> p (a d)"),
                   start=True, stop=True).then_inc(s("fw_done"), 1)
            for j in range(9):
                ins = mm(ps[:, 0, 64 + j:65 + j], Wp[:, 8 - j], bcol[:], start=True, stop=True)
            ins.then_inc(s("bw_done"), 1)
            pe.wait_ge(s("a_split"), 2)
            for j in (1, 2):
                for i in range(NC):
                    if j == 2:
                        pe.wait_ge(s("pow_split"), NC)
                    for k in range(NC):
                        ins = passes(ps[:, 4 + i, :], lambda h: An[:, h, k, i * P:(i + 1) * P], lambda h: B[:, j - 1, h, k],
                                     k == 0, k == NC - 1)
                    ins.then_inc(s("pow_done"), 1)
            pe.wait_ge(s("in_c"), 32)
            for i in range(NC):
                for r in range(2):
                    for k in range(NC):
                        for h in range(2):
                            ins = mm(ps[:, 0, 2 * i + r:2 * i + r + 1], B[:, r, h, k, i * P:(i + 1) * P], ones16[:, 0:1],
                                     start=(k == 0 and h == 0), stop=(k == NC - 1 and h == 1))
            ins.then_inc(s("us_done"), 1)
            pe.wait_ge(s("pow_split"), 2 * NC)
            for n in (1, 2):
                pe.wait_ge(s("u_split"), n)
                for i in range(NC):
                    for k in range(NC):
                        ins = passes(ps[:, 0, 12 * n + 3 * i:12 * n + 3 * i + 3], lambda h: B[:, 2, h, k, i * P:(i + 1) * P],
                                     lambda h: u16[:, h, k, 3 * n - 3:3 * n], k == 0, k == NC - 1)
                ins.then_inc(s("us_done"), 1)
            pe.wait_ge(s("ub"), 1)
            for i in range(NC):
                nc.tensor.transpose(ps[0:9, 4, i * P:(i + 1) * P], uall[:, i, :], ident32)
            nc.tensor.transpose(ps[0:9, 5, 0:D], bt[:], ident32).then_inc(s("ut_done"), 1)
            pe.wait_ge(s("ub"), 2)
            for i in range(NC):
                ins = mm(ps[:, 6, i * D:(i + 1) * D], ut[:, i * P:(i + 1) * P], btT[:], start=True, stop=True)
            ins.then_inc(s("bias_done"), 1)
            pe.wait_ge(s("bias"), 1)
            pe.wait_ge(s("g_split"), 1)

            def xt(b, q):
                pe.wait_ge(s("xn_split"), b + 1)
                if not (isinstance(b, int) and b < 1):
                    pe.wait_ge(s("xt_ready"), b)
                for h in range(2):
                    for c in range(NC):
                        ins = nc.tensor.transpose(psT[:, h, c * P:(c + 1) * P], Xh[:, q, h, c, :], ident16)
                ins.then_inc(s("xt_done"), 1)

            def vv(b, q):
                if not (isinstance(b, int) and b < 1):
                    pe.wait_ge(s("v_split"), 2 * b)
                for r in range(2):
                    for k in range(NC):
                        ins = passes(ps[:, 1 + r, :], lambda h: Xh[:, q, h, k, :], lambda h: B[:, r, h, k], k == 0, k == NC - 1)
                    ins.then_inc(s("v_done"), 1)

            def zz(b, q, cs=range(NC)):
                pe.wait_ge(s("xt_ready"), b + 1)
                pe.wait_ge(s("v_split"), 2 * b + 2)
                for c in cs:
                    if not (isinstance(b, int) and b < 1 and c < 2):
                        pe.wait_ge(s("z_split"), NC * b + c - 1)
                    n = slice(c * P, (c + 1) * P)
                    for r in range(3):
                        ins = passes(ps[:, 3 + c % 2, 0:3 * D], lambda h: XT[:, q, h, n] if r == 0 else V[:, q, h, r - 1, n],
                                     lambda h: G16[:, h, r].rearrange("p i d -> p (i d)"), r == 0, r == 2)
                    ins.then_inc(s("z_done"), 1)

            def s2(g, second):
                if second:
                    src = lambda h, k: U[:, h, k]
                    pe.wait_ge(s("u_lo"), NC * (g + 1))
                else:
                    src = lambda h, k: Z2[:, h, k].rearrange("p b d -> p (b d)")
                    pe.wait_ge(s("z_split"), NC * GB * (g + 1))
                for i in range(NC):
                    if second:
                        if i < 2:
                            pe.wait_ge(s("u_full"), NC * g + i + 3)
                        else:
                            pe.wait_ge(s("x2_steps"), NC * g + i - 1)
                    elif i >= 2:
                        pe.wait_ge(s("u_full"), NC * g + i - 1)
                    for k in range(NC):
                        ins = passes(ps[:, 5 + i % 2, :], lambda h: B[:, 2, h, k, i * P:(i + 1) * P], lambda h: src(h, k),
                                     k == 0, k == NC - 1)
                    ins.then_inc(s("s2_done"), 1)

            def rt(g, q):
                pe.wait_ge(s("xn2_lo"), NC * g + q + 1)
                if q < 2:
                    pe.wait_ge(s("x2_steps"), NC * g + q + 3)
                else:
                    pe.wait_ge(s("rt_ready"), NC * g + q - 1)
                bank = ps[:, 5 + q % 2, :].bitcast(F16)
                for h in range(2):
                    for t in range(GB):
                        ins = nc.tensor.transpose(bank[:, (h * GB + t) * P:(h * GB + t + 1) * P],
                                                  payh[:, q * GB + t, h * D:(h + 1) * D], ident16)
                ins.then_inc(s("rt_done"), 1)

            def logits(g, q):
                pe.wait_ge(s("rt_ready"), NC * g + q + 1)
                if q == 0:
                    pe.wait_ge(s("route"), g + 1)
                for t in range(GB):
                    tt = q * GB + t
                    ins = passes(psR[:, tt * E:(tt + 1) * E], lambda h: XR[:, q % 2, h, t], lambda h: wr16[:, h], True, True)
                if q == NC - 1:
                    ins.then_inc(s("logits"), 1)

            def prefix(g):
                pe.wait_ge(s("mask"), g + 1)
                m = M16[:].rearrange("p e t -> p (e t)")
                mm(psR[:, P:2 * P], tri16, m, start=True, stop=True)
                mm(psR[:, 2 * P:3 * P], ones16, m, start=True, stop=True).then_inc(s("prefix"), 1)

            def body(g, tail):
                for j in range(GB):
                    b = g * GB + j
                    xt(b, j % 2)
                    if tail and j == 3:
                        logits(g - 1, 0)
                        logits(g - 1, 1)
                        rt(g - 1, 2)
                        rt(g - 1, 3)
                    vv(b, j % 2)
                    if tail and j == 0:
                        s2(g - 1, False)
                    if tail and j == 3:
                        logits(g - 1, 2)
                        logits(g - 1, 3)
                    if j:
                        zz(b - 1, (j - 1) % 2)
                    if tail and j == 1:
                        s2(g - 1, True)
                    if tail and j == 2:
                        rt(g - 1, 0)
                        rt(g - 1, 1)
                zz(g * GB + 3, 1, (0, 1, 2))
                if tail:
                    prefix(g - 1)
                zz(g * GB + 3, 1, (3,))

            body(0, False)
            pe.wait_ge(s("router"), 1)
            with pe.Fori(1, NG) as g:
                body(g, True)
            s2(NG - 1, False)
            s2(NG - 1, True)
            for q in range(NC):
                rt(NG - 1, q)
                if q >= 1:
                    logits(NG - 1, q - 1)
            logits(NG - 1, NC - 1)
            prefix(NG - 1)

            pe.wait_ge(s("table"), 1)
            pe.wait_ge(s("f_split"), 3)

            expert = [pe.alloc_register(f"expert{u}") for u in range(UNROLL)]

            def early(t, u):
                q = u % 2
                if isinstance(t, int):
                    pe.reg_load(expert[u], tabi[0:1, 1, t:t + 1])
                    pe.wait_ge(s(f"xs{u}"), 16 * (t // UNROLL + 1))
                else:
                    pe.reg_load(expert[u], tabi[0:1, 1, bass.ds(t, 1)])
                    pe.wait_ge(s(f"xs{u}"), 16 // UNROLL * (t - u) + 16)
                if not (isinstance(t, int) and t < 1):
                    pe.wait_ge(s("fx_ready"), t)
                bank = ps[:, 6, 0:SLOT].bitcast(F16)
                for h in range(2):
                    for a in range(2):
                        n = (h * 2 + a) * P
                        ins = nc.tensor.transpose(bank[:, n:n + P], XSh[:, u, a, h * D:(h + 1) * D], ident16)
                ins.then_inc(s("fx_done"), 1)

            def front(t, u):
                q = u % 2
                e = pe.snap(expert[u], min_val=0, max_val=E - 1)
                pe.wait_ge(s("fx_ready"), t + 1)
                for c in range(HC):
                    if not (isinstance(t, int) and t < 2):
                        pe.wait_ge(s("hid"), 9 * (t - 2) + (1, 3, 6)[c])
                    for n, W in enumerate((W1, W3)):
                        wp = lambda h: W[:, h, bass.ds(e, 1), c * P:(c + 1) * P].rearrange("p a h -> p (a h)")
                        o = ps[:, HC * q + c, n * SLOT:(n + 1) * SLOT]
                        hi, lo = wp(0), wp(1)
                        mm(o, hi, XTf[:, q, 0], start=True, stop=False)
                        mm(o, hi, XTf[:, q, 1], start=False, stop=False)
                        ins = mm(o, lo, XTf[:, q, 0], start=False, stop=True)
                    ins.then_inc(s("h_done"), 1)

            def back(t, u):
                q = u % 2
                e = pe.snap(expert[u], min_val=0, max_val=E - 1)
                pe.wait_ge(s("hid"), 9 * (t + 1))
                if not (isinstance(t, int) and t < 1):
                    pe.wait_ge(s("y_ready"), t)
                for a in range(2):
                    o = ps[:, 7, a * D:(a + 1) * D]
                    for c in range(HC):
                        wp = lambda h: W2[:, h, bass.ds(e, 1), c, :].rearrange("p a d -> p (a d)")
                        ins = passes(o, lambda h: Hh[:, q, h, c, a * P:(a + 1) * P], wp, c == 0, c == HC - 1)
                ins.then_inc(s("y_done"), 1)

            tiles_loop(pe, early, front, back)


def kernel(x, adj, L0_gnn_alpha_train, L0_gnn_w, L0_gnn_d, L0_gnn_fc_in_w, L0_gnn_fc_in_b, L0_ffn_router_w,
           L0_ffn_w1, L0_ffn_w2, L0_ffn_w3):
    import concourse.bacc as _bacc
    from concourse.bass_utils import run_bass_kernel_spmd as _run

    f = np.ascontiguousarray
    c32, c16, pad = shape_constants()
    w1, w2, w3 = np.asarray(L0_ffn_w1), np.asarray(L0_ffn_w2), np.asarray(L0_ffn_w3)
    arrays = {
        "in_x": f(np.asarray(x)),
        "in_adj": f(np.asarray(adj)),
        "in_adj_t": f(np.asarray(adj).T),
        "in_alpha": f(np.asarray(L0_gnn_alpha_train).reshape(1, N)),
        "in_w_t": f(np.asarray(L0_gnn_w).T),
        "in_d": f(np.asarray(L0_gnn_d).reshape(D, 1)),
        "in_fc_w": f(np.asarray(L0_gnn_fc_in_w)),
        "in_fc_b": f(np.asarray(L0_gnn_fc_in_b).reshape(D, 1)),
        "in_router_t": f(np.asarray(L0_ffn_router_w).T),
        "in_w1_t": f(w1.transpose(2, 0, 1).reshape(D, E * HID)),
        "in_w3_t": f(w3.transpose(2, 0, 1).reshape(D, E * HID)),
        "in_w2_t": f(w2.transpose(2, 0, 1).reshape(HID, E * D)),
        "in_c32": c32,
        "in_c16": c16,
        "in_pad": pad,
    }
    nc = _bacc.Bacc("TRN2", target_bir_lowering=False, num_devices=1)
    args = [nc.dram_tensor(n, a.shape, mybir.dt.from_np(a.dtype), kind="ExternalInput").ap() for n, a in arrays.items()]
    out = nc.dram_tensor("out_rows", (TOKENS + SLOT, D), F32, kind="ExternalOutput").ap()
    gnn_moe_kernel(nc, *args, out)
    r = _run(nc, [arrays], core_ids=[0])
    return np.asarray(r.results[0]["out_rows"])[0:TOKENS].reshape(NB, N, D)
```

```python
from contextlib import ExitStack
from math import comb

import numpy as np

import concourse.bass as bass
from concourse import mybir

F32 = mybir.dt.float32
F16 = mybir.dt.float16
U32 = mybir.dt.uint32
I32 = mybir.dt.int32
ALU = mybir.AluOpType
ACT = mybir.ActivationFunctionType
AX = mybir.AxisListType.X

P = 128
D = 128
N = 512
NC = N // P
NB = 16
TOKENS = NB * N
STEPS = 8
DT = 1.0 / STEPS
EPS = 1e-5
GB = 4
NG = NB // GB
GT = GB * NC
E = 8
HID = 341
HC = 3
SLOT = 256
CAP = TOKENS + SLOT
DUMMY = E * CAP
ROWS = DUMMY + SLOT
NTILES = (2 * TOKENS + E * (SLOT - 1)) // SLOT

UNROLL = 8


def whole_tiles(groups):
    return (groups * 2 * TOKENS // NG - E * (SLOT - 1)) // SLOT // UNROLL * UNROLL


STARTS = (0, whole_tiles(NG - 2), whole_tiles(NG - 1), NTILES)
COLS = 6
NY = 4
FIRST = 16
ROW = D + 1 + E

MOVED = 16 * 2 * GB

SA = [0, 10, 14, 12]
SV = [0, 6, 10]
SZ = 6
SW = 6
SU = 6


def p2(n):
    return float(2.0 ** n)


C_ID, C_IOM, C_EB, C_TOK, C_SCAN, C_BIN, C_TILE, C_BACK, C_ONE, C_END = np.cumsum(
    [0, P, E, E, GT, P, 9, 2, NY, E]).tolist()


def shape_constants():
    c = np.zeros((P, C_END), np.float32)
    c[:, C_ID:C_ID + P] = np.eye(P)
    c[:, C_IOM:C_IOM + E] = np.arange(E) - E
    c[:, C_EB:C_EB + E] = np.arange(E) * CAP
    tt = np.arange(GT)
    c[:, C_TOK:C_TOK + GT] = ((tt % GB) * NC + tt // GB)[None] * P + np.arange(P)[:, None]
    c[:, C_SCAN:C_SCAN + P] = (np.arange(P) % GT != 0)[None]
    c[:, C_BIN:C_BIN + 9] = [comb(STEPS, j) / 2.0 ** SU for j in range(9)]
    c[:, C_TILE] = np.arange(P)
    c[:, C_TILE + 1] = SLOT * np.arange(P)
    c[:, C_BACK:C_BACK + NY] = NY - 1 - np.arange(NY)
    c[:, C_ONE:C_ONE + E] = 1.0
    h = np.zeros((P, 3 * P), np.float16)
    h[:, 0:P] = np.eye(P)
    h[:, P:2 * P] = np.triu(np.ones((P, P)), 1)
    h[:, 2 * P:] = 1.0
    pad = np.zeros((SLOT, ROW), np.uint32)
    pad[:, D] = TOKENS + np.arange(SLOT)
    return c, h, pad


def wait_apart(eng, sem, value, tiny):
    eng.wait_ge(sem, value)
    tiny()


class Steps:

    def __init__(self, eng, sem, index, per):
        self.eng, self.sem, self.base, self.per, self.n = eng, sem, index * per, per, 0

    def done(self, ins):
        self.n += 1
        return ins.then_inc(self.sem, 1)

    def wait(self):
        self.eng.wait_ge(self.sem, self.base + self.n)

    def wait_apart(self, tiny):
        wait_apart(self.eng, self.sem, self.base + self.n, tiny)

    def end(self):
        assert self.n == self.per, (self.n, self.per)


def gnn_moe_kernel(nc, x, adj, adj_t, alpha, w_t, d, fc_w, fc_b, router_t, w1_t, w3_t, w2_t, c32, c16, pad, out):
    with ExitStack() as ctx:
        def sb(name, shape, dt):
            return ctx.enter_context(nc.sbuf_tensor(name, shape, dt))

        def sem(name):
            return ctx.enter_context(nc.semaphore(name))

        slots = nc.dram_tensor("slots", (ROWS, ROW), U32, kind="Internal").ap()

        k32 = sb("k32", [P, C_END], F32)
        k16 = sb("k16", [P, 3 * P], F16)
        ident16, tri16, ones16 = k16[:, 0:P], k16[:, P:2 * P], k16[:, 2 * P:3 * P]
        ident32 = k32[:, C_ID:C_ID + P]
        X = sb("X", [P, (NB + 2) * NC, D], F32)
        stage = sb("stage", [P, 4096], F32)
        adjT = stage[:, 0:2048].rearrange("p (k n) -> p k n", k=NC)
        adjN = stage[:, 2048:4096].rearrange("p (k n) -> p k n", k=NC)
        B = sb("B", [P, 3, 2, NC, N], F16)
        sigc = sb("sigc", [P, NC], F32)
        alfc = sb("alfc", [P, NC], F32)
        G16 = sb("G16", [P, 2, 3, 3, D], F16)
        W1 = sb("W1", [P, 2, E, HC * P], F16)
        W3 = sb("W3", [P, 2, E, HC * P], F16)
        W2 = sb("W2", [P, 2, E, HC, D], F16)
        wr32 = sb("wr32", [P, E], F32)
        wr16 = sb("wr16", [P, 2, E], F16)
        xn = sb("xn", [P, 2, NC, D], F32)
        Xh = sb("Xh", [P, 2, 2, NC, D], F16)
        XT = sb("XT", [P, 2, 2, N], F16)
        Vw = sb("Vw", [P, GT * ROW], F32)
        V = Vw[:, 0:4 * N].bitcast(F16).rearrange("p (q h r n) -> p q h r n", q=2, h=2, r=2)
        Z2 = sb("Z2", [P, 2, NC, GB, D], F16)
        An = Z2[:].rearrange("p a k b d -> p a k (b d)")
        Z1 = sb("Z1", [P, NC, GB, D], F32)
        Uf = sb("Uf", [P, 2, GB * D], F32)
        U = sb("U", [P, 2, NC, GB * D], F16)
        stats = sb("stats", [P, 2, NC, 6], F32)
        mv = sb("mv", [P, 2, NC, 2], F32)
        var = sb("var", [P, 2, NC], F32)
        rstd = sb("rstd", [P, 2, NC], F32)
        negm = sb("negm", [P, 2, NC], F32)
        shift = sb("shift", [P, 2, NC], F32)
        negm2 = sb("negm2", [P, NC, NC], F32)
        shift2 = sb("shift2", [P, NC, NC], F32)
        stats2 = sb("stats2", [P, NC, NC, 6], F32)
        mv2 = sb("mv2", [P, NC, NC, 2], F32)
        var2 = sb("var2", [P, NC, NC], F32)
        rstd2 = sb("rstd2", [P, NC, NC], F32)
        xn2 = sb("xn2", [P, 2, NC, D], F32)
        spare = sb("spare", [P, 3], F32)
        mhalf = sb("mhalf", [P, NC], F32)
        pay = sb("pay", [P, GT, ROW], U32)
        pay_last = Vw[:].bitcast(U32).rearrange("p (t w) -> p t w", t=GT)
        XR = sb("XR", [P, 2, 2, NC, P], F16)
        biasf = sb("biasf", [P, NC, D], F32)
        uall = sb("uall", [P, NC, 9], F32)
        u16 = sb("u16", [P, 2, NC, 9], F16)
        bt = sb("bt", [P, 9], F32)
        btT = sb("btT", [9, D], F32)
        bcol = sb("bcol", [P, 1], F32)
        dcol = sb("dcol", [P, 2], F32)
        mx = sb("mx", [P, GT], F32)
        dl = sb("dl", [P, GT, E], F32)
        ex = sb("ex", [P, GT, E], F32)
        ssum = sb("ssum", [P, GT], F32)
        key = sb("key", [P, GT, E], F32)
        first = sb("first", [P, GT], F32)
        oh = sb("oh", [P, 2, GT, E], F32)
        rest = sb("rest", [P, GT, E], F32)
        m2 = sb("m2", [P, GT], F32)
        den = sb("den", [P, GT], F32)
        rden = sb("rden", [P, GT], F32)
        M16 = sb("M16", [P, E, GT], F16)
        incl = sb("incl", [P, E, GT], F32)
        pos = sb("pos", [P, E, GT], F32)
        prod = sb("prod", [P, 2, GT, E], F32)
        slotf = sb("slotf", [P, 2, GT], F32)
        idx = sb("idx", [P, 2, GT], U32)
        idx_last = sb("idx_last", [P, 2, GT], U32)
        run = sb("run", [P, E], F32)
        run3 = sb("run3", [P, E], F32)
        tok = sb("tok", [P, GT], F32)
        prev = sb("prev", [P, E], F32)
        cnt = sb("cnt", [P, 3, E], F32)
        cum = sb("cum", [P, 3, 1 + E], F32)
        taken = sb("taken", [P, 1 + E], F32)
        ind = sb("ind", [P, 3, E], F32)
        red = sb("red", [P, 3], F32)
        tcol = sb("tcol", [P, 4], F32)
        twait = sb("twait", [P, NY], I32)
        rows_t = sb("rows_t", [P, COLS], F32)
        cnti = sb("cnti", [P, 2, E], I32)
        padrow = sb("padrow", [P, E], I32)

        z1w = Z1[:].rearrange("p k b d -> p (k b d)")
        uw = U[:].rearrange("p h k n -> p (h k n)").bitcast(F32)
        Gf = z1w[:, 0:9 * D].rearrange("p (r i d) -> p r i d", r=3, i=3)
        sig = z1w[:, 9 * D:9 * D + N]
        Wp = uw[:, 0:9 * D].rearrange("p (a d) -> p a d", a=9)
        fcw, wt, wd, idt = (uw[:, (9 + n) * D:(10 + n) * D] for n in range(4))
        alf = Uf[:, 1, :]
        ut = xn2[0:9].rearrange("p a k d -> p (a k d)")[:, 0:N]
        tab_width = NTILES + UNROLL + 1
        tabi = stage[:, 4 * HC * SLOT:4 * HC * SLOT + COLS * tab_width].bitcast(I32).rearrange("p (a t) -> p a t", a=COLS)

        Bw = B[:, 0:2].rearrange("p a b k n -> p (a b k n)")
        at = [0]

        def carve(words16, dt, pattern, **k):
            a = Bw[:, at[0]:at[0] + words16]
            at[0] += words16
            if dt != F16:
                a = a.bitcast(dt)
            return a.rearrange(pattern, **k)

        XS = carve(UNROLL * 2 * 2 * ROW, U32, "p (r a w) -> p r a w", r=UNROLL, a=2)
        XSh, XSf = XS.bitcast(F16), XS.bitcast(F32)
        XTf = XT[:, :, :, 0:SLOT]
        sil = stage[:, 0:2 * HC * SLOT].rearrange("p (r c s) -> p r c s", r=2, c=HC)
        hf = stage[:, 2 * HC * SLOT:4 * HC * SLOT].rearrange("p (r c s) -> p r c s", r=2, c=HC)
        Hh = carve(2 * 2 * HC * SLOT, F16, "p (r h c s) -> p r h c s", r=2, h=2, c=HC)
        Y = xn[:].rearrange("p q (r a) d -> p (q r) a d", a=2)
        assert at[0] <= 2 * 2 * NC * N

        ps = ctx.enter_context(nc.psum_tensor("ps", [P, 8, 512], F32))
        psT = ps[:, 0, :].bitcast(F16).rearrange("p (h n) -> p h n", h=2)
        psR = ps[:, 7, :]

        def u_bank(g, i):
            return (5, 6, 3, 4)[i] if isinstance(g, int) and g == NG - 1 else 5 + i % 2

        S = {}

        def s(name):
            if name not in S:
                S[name] = sem(name)
            return S[name]

        def payload(g):
            last = isinstance(g, int) and g == NG - 1
            return (pay_last, idx_last[:]) if last else (pay[:], idx[:])

        x_rows = x.rearrange("b (k p) d -> p (b k) d", p=P)
        out_rows = out[0:TOKENS, :].rearrange("(t p) d -> p t d", p=P)

        def y_free(t, u):
            return FIRST + (32 * (t // NY) if isinstance(t, int) else 32 // NY * (t - u % NY))

        def tiles_loop(eng, early, front, back, between):
            def step(t, u):
                if not isinstance(t, int) or t + 2 < NTILES:
                    early(t + 2, (u + 2) % UNROLL)
                if not isinstance(t, int) or t + 1 < NTILES:
                    front(t + 1, (u + 1) % UNROLL)
                back(t, u)

            early(1, 1)
            front(0, 0)
            peeled = 2 * UNROLL
            end = (NTILES - 2) // UNROLL * UNROLL
            for t in range(peeled):
                between(t)
                step(t, t % UNROLL)
            with eng.Fori(peeled, end, UNROLL) as t0:
                for u in range(UNROLL):
                    step(t0 + u, u)
            for t in range(end, NTILES):
                step(t, t % UNROLL)

        block = ctx.enter_context(nc.Block())

        @block.sync
        def _(sp):
            sp.dma_start(k32[:], c32).then_inc(s("in_w"), 16)
            sp.dma_start(wt, w_t).then_inc(s("in_w"), 16)
            sp.dma_start(dcol[:, 0:1], d).then_inc(s("in_w"), 16)
            sp.dma_start(fcw, fc_w).then_inc(s("in_w"), 16)
            sp.dma_start(bcol[:], fc_b).then_inc(s("in_w"), 16)
            sp.dma_start(alf, alpha.to_broadcast([P, N])).then_inc(s("in_a"), 16)
            sp.dma_start(adjT, adj_t.rearrange("(k p) n -> p k n", p=P)).then_inc(s("in_a"), 16)
            sp.dma_start(adjN, adj.rearrange("(k p) n -> p k n", p=P)).then_inc(s("in_n"), 16)
            with nc.allow_non_contiguous_dma(reason="512 numbers"):
                sp.dma_start(alfc[:], alpha.rearrange("a (k p) -> p (a k)", p=P)).then_inc(s("in_n"), 16)
            sp.dma_start(X[:, 0:GT, :], x_rows[:, 0:GT, :]).then_inc(s("in_x"), 16)
            sp.dma_start(k16[:], c16).then_inc(s("pad_st"), 16)
            sp.dma_start(wr32[:], router_t).then_inc(s("in_c"), 16)
            for g in range(1, NG):
                sp.wait_ge(s("in_x"), 16 * g)
                sp.dma_start(X[:, g * GT:(g + 1) * GT, :], x_rows[:, g * GT:(g + 1) * GT, :]).then_inc(s("in_x"), 16)
            sp.wait_ge(s("a_split"), 2)
            sp.dma_start(stage[:, 0:E * HID], w1_t).then_inc(s("in_f"), 16)
            sp.wait_ge(s("f_split"), 1)
            sp.dma_start(stage[:, 0:E * HID], w3_t).then_inc(s("in_f"), 16)
            sp.wait_ge(s("f_split"), 2)
            for c in range(HC):
                n = min(P, HID - c * P)
                sp.dma_start(stage[0:n, c * E * D:(c + 1) * E * D], w2_t[c * P:c * P + n, :]).then_inc(s("in_f"), 16)
            with sp.Fori(0, NG - 1) as g:
                sp.wait_ge(s("x2_steps"), NC * (g + 1))
                sp.dma_start(out_rows[:, bass.ds(g * GT, GT), :], X[:, bass.ds(g * GT, GT), :]).then_inc(s("out_st"), 16)

            def load_tile(col, u, u_free):
                r = sp.value_load(tabi[0:1, 0, col], min_val=0, max_val=DUMMY)
                if u_free is not None:
                    sp.wait_ge(s(f"added{u % NY}"), u_free)
                sp.dma_start(XS[:, u], slots[bass.ds(r, SLOT), :].rearrange("(p a) w -> p a w", a=2)).then_inc(s(f"xs{u}"), 16)

            def load_tiles(first, end):
                with sp.Fori(first // UNROLL, end // UNROLL) as i:
                    for u in range(UNROLL):
                        load_tile(bass.ds(i * UNROLL + u, 1), u, FIRST + 32 * (UNROLL // NY * (i - 1) + u // NY + 1))
                for t in range(end // UNROLL * UNROLL, end):
                    load_tile(slice(t, t + 1), t % UNROLL, FIRST + 32 * ((t - UNROLL) // NY + 1))

            sp.wait_ge(s("table"), 1)
            for t in range(UNROLL):
                load_tile(slice(t, t + 1), t, None)
            sp.wait_ge(s("x2_steps"), NC * NG)
            sp.dma_start(out_rows[:, (NG - 1) * GT:NG * GT, :], X[:, (NG - 1) * GT:NG * GT, :]).then_inc(s("out_last"), 16)
            load_tiles(UNROLL, STARTS[1])
            sp.wait_ge(s("pad_st"), 16)
            sp.wait_ge(s("regions"), 1)
            for e in range(E):
                row = sp.value_load(padrow[0:1, e:e + 1], min_val=0, max_val=DUMMY - SLOT)
                sp.dma_start(slots[bass.ds(row, SLOT), :], pad).then_inc(s("pad_st"), 16)
            sp.wait_ge(s("table"), 2)
            for q in range(NC):
                sp.wait_ge(s(f"moved{q}"), MOVED * (NG - 1))
            load_tiles(STARTS[1], STARTS[2])
            sp.wait_ge(s("table"), 3)
            sp.wait_ge(s("moved_last"), FIRST + NC * MOVED)
            sp.wait_ge(s("pad_st"), 16 + 16 * E)
            for name in ("added2", "added3"):
                sp.wait_ge(s(name), FIRST)
            load_tiles(STARTS[2], NTILES)
            for n in range(NY):
                sp.wait_ge(s(f"added{n}"), FIRST + 32 * ((NTILES + NY - 1 - n) // NY))

        @block.gpsimd
        def _(pool):
            tiny = lambda: nc.gpsimd.tensor_tensor(spare[:, 2:3], mhalf[:, 0:1], mhalf[:, 0:1], ALU.add).then_inc(s("tick"), 1)
            nc.gpsimd.memset(mhalf[:], -0.5).then_inc(s("mhalf"), 1)
            nc.gpsimd.memset(Uf[:, 0, :], 0.0).then_inc(s("zero_out"), 1)
            nc.gpsimd.memset(X[:, NB * NC:, :], 0.0).then_inc(s("zero_x"), 1)
            nc.gpsimd.memset(W1[:, :, :, HID:], 0.0)
            nc.gpsimd.memset(W3[:, :, :, HID:], 0.0)
            nc.gpsimd.memset(W2[:, :, :, HC - 1, :], 0.0).then_inc(s("zero_w"), 1)
            nc.gpsimd.memset(uall[:, :, 0:1], p2(SU)).then_inc(s("u0"), 1)
            pool.wait_ge(s("zero_out"), 1)
            for a in range(2):
                nc.gpsimd.dma_start(out[TOKENS + a * P:TOKENS + (a + 1) * P, :], Uf[:, 0, 0:D]).then_inc(s(f"added{a}"), 16)
            for r0, r1, name in ((0, P, "added2"), (P, P + P // 2, "added3"), (P + P // 2, SLOT, "moved_last")):
                nc.gpsimd.dma_start(slots[DUMMY + r0:DUMMY + r1, :], pad[r0:r1, :]).then_inc(s(name), 16)
            pool.wait_ge(s("mhalf"), 1)

            def ln1_rstd(b, q):
                pool.wait_ge(s("var"), b + 1)
                nc.gpsimd.tensor_tensor(rstd[:, q], var[:, q], mhalf[:], ALU.pow).then_inc(s("pow1"), 1)
                pool.wait_ge(s("pow1"), b + 1)
                nc.gpsimd.tensor_tensor(shift[:, q], negm[:, q], rstd[:, q], ALU.mult).then_inc(s("rstd"), 1)

            def ln1_lo(b, q):
                pool.wait_ge(s("xn_hi"), b + 1)
                nc.gpsimd.tensor_tensor(Xh[:, q, 1], xn[:, q], Xh[:, q, 0], ALU.subtract).then_inc(s("xn_split"), 1)

            def route(g):
                wait_apart(pool, s("route"), g + 2, tiny)

            def scatters(g, tiles, ks=(0, 1)):
                rows, places = payload(g)
                last = isinstance(g, int) and g == NG - 1
                for tt in tiles:
                    for k in ks:
                        nc.gpsimd.indirect_dma_start(
                            out=slots, out_offset=bass.IndirectOffsetOnAxis(ap=places[:, k, tt:tt + 1], axis=0),
                            in_=rows[:, tt, :], in_offset=None).then_inc(s("moved_last" if last else f"moved{tt // GB}"), 16)

            def ln2_rstd(g, q):
                pool.wait_ge(s("var2"), NC * g + q + 1)
                nc.gpsimd.tensor_tensor(rstd2[:, q], var2[:, q], mhalf[:], ALU.pow).then_inc(s("pow2"), 1)
                pool.wait_ge(s("pow2"), NC * g + q + 1)
                nc.gpsimd.tensor_tensor(shift2[:, q], negm2[:, q], rstd2[:, q], ALU.mult).then_inc(s("rstd2"), 1)

            def bias_add(b):
                pool.wait_ge(s("xn_ready"), b + 1)
                if isinstance(b, int) and b == 0:
                    pool.wait_ge(s("bias"), 1)
                nc.gpsimd.tensor_tensor(X[:, bass.ds(b * NC, NC), :], X[:, bass.ds(b * NC, NC), :], biasf[:],
                                        ALU.add).then_inc(s("x_bias"), 1)

            ln1_rstd(0, 0)
            ln1_lo(0, 0)
            ln1_rstd(1, 1)

            def body(g, tail, moves):
                if moves:
                    route(g - 2)
                for j in range(GB):
                    b = g * GB + j
                    ln1_lo(b + 1, (j + 1) % 2)
                    ln1_rstd(b + 2, j % 2)
                    if moves and j == 0:
                        scatters(g - 2, range(0, 3))
                    if moves and j == 1:
                        scatters(g - 2, range(6, 8))
                    bias_add(b)
                    if moves and j == 0:
                        scatters(g - 2, range(3, 6))
                    if moves and j == 1:
                        scatters(g - 2, range(8, 10))
                    if tail and j == 1:
                        ln2_rstds(g - 1, moves)

            def ln2_rstds(g, moves):
                for q in range(NC):
                    ln2_rstd(g, q)
                    if moves:
                        scatters(g - 1, ((10,), (11,), (12, 13), (14, 15))[q])

            body(0, False, False)
            body(1, True, False)
            with pool.Fori(2, NG) as g:
                body(g, True, True)
            route(NG - 2)
            scatters(NG - 2, range(0, 7))
            for q in range(NC):
                ln2_rstd(NG - 1, q)
                scatters(NG - 2, (7 + q,) if q < 3 else range(10, GT))

            pool.wait_ge(s("table"), 1)
            pool.wait_ge(s("out_st"), 16 * (NG - 1))

            def add_tile(t, u, col):
                before = [pool.value_load(tabi[0:1, 2 + n, col], min_val=FIRST, max_val=FIRST + 32 * NTILES) for n in range(NY)]
                for n in range(NY):
                    pool.wait_ge(s(f"added{n}"), before[n])
                pool.wait_ge(s("tick"), NG - 1 + t + (0 if isinstance(t, int) and t < 8 else 1))
                wait_apart(pool, s("y_ready"), t + 1, tiny)
                for a in range(2):
                    nc.gpsimd.indirect_dma_start(
                        out=out, out_offset=bass.IndirectOffsetOnAxis(ap=XS[:, u, a, D:D + 1], axis=0),
                        in_=Y[:, u % NY, a, :], in_offset=None, compute_op=ALU.add).then_inc(s(f"added{u % NY}"), 16)

            peeled = 4 * UNROLL
            first_move = peeled - 3 * 2 * GT // 4
            for t in range(peeled):
                if t == first_move:
                    pool.wait_ge(s("tick"), NG - 1 + t)
                    route(NG - 1)
                if t >= first_move:
                    for n in range((t - first_move) * 4 // 3, (t - first_move + 1) * 4 // 3):
                        scatters(NG - 1, (n // 2,), (n % 2,))
                if t == STARTS[1]:
                    pool.wait_ge(s("table"), 2)
                add_tile(t, t % UNROLL, slice(t, t + 1))
            pool.wait_ge(s("table"), 3)
            pool.wait_ge(s("out_last"), 16)
            with pool.Fori(peeled // UNROLL, NTILES // UNROLL) as i:
                for u in range(UNROLL):
                    add_tile(i * UNROLL + u, u, bass.ds(i * UNROLL + u, 1))
            for t in range(NTILES // UNROLL * UNROLL, NTILES):
                add_tile(t, t % UNROLL, slice(t, t + 1))

        @block.scalar
        def _(act):
            copy = lambda o, i, sc=1.0: nc.scalar.activation(o, i, ACT.Copy, scale=sc)
            act.wait_ge(s("in_a"), 32)
            nc.scalar.activation(sig, alf, ACT.Sigmoid).then_inc(s("sig"), 1)
            act.wait_ge(s("in_n"), 32)
            nc.scalar.activation(sigc[:], alfc[:], ACT.Sigmoid).then_inc(s("sig"), 1)

            def ln1_norm(b, q):
                act.wait_ge(s("rstd"), b + 1)
                for c in range(NC):
                    row = X[:, b * NC + c, :] if isinstance(b, int) else X[:, bass.ds(b * NC + c, 1), :].rearrange("p a d -> p (a d)")
                    ins = nc.scalar.activation(xn[:, q, c], row, ACT.Identity, scale=rstd[:, q, c:c + 1], bias=shift[:, q, c:c + 1])
                ins.then_inc(s("xn_ready"), 1)

            def ln1_hi(b, q):
                act.wait_ge(s("xn_ready"), b + 1)
                copy(Xh[:, q, 0], xn[:, q]).then_inc(s("xn_hi"), 1)

            act.wait_ge(s("a_full"), 1)
            copy(B[:, 0, 0], adjT).then_inc(s("a_hi"), 1)
            act.wait_ge(s("a_full"), 2)
            for k in range(NC):
                ins = nc.scalar.activation(An[:, 0, k], adjN[:, k, :], ACT.Identity, scale=sigc[:, k:k + 1])
            ins.then_inc(s("a_hi"), 1)
            ln1_norm(0, 0)
            ln1_hi(0, 0)

            def power_hi(j, i):
                act.wait_ge(s("pow_done"), (j - 1) * NC + i + 1)
                copy(B[:, j, 0, i], ps[:, 4 + i, :], p2(SA[j + 1] - SA[1] - SA[j])).then_inc(s("pow_hi"), 1)

            for i in range(NC):
                power_hi(1, i)

            def xt_evac(b, q):
                act.wait_ge(s("xt_done"), b + 1)
                copy(XT[:, q], psT).then_inc(s("xt_ready"), 1)

            def v_hi(b, q, r):
                act.wait_ge(s("v_done"), 2 * b + r + 1)
                copy(V[:, q, 0, r], ps[:, 1 + r, :], p2(SV[r + 1] - SA[r + 1])).then_inc(s("v_hi"), 1)

            def z_hi(b, j, cs):
                for c in cs:
                    act.wait_ge(s("z_done"), NC * b + c + 1)
                    z = ps[:, 3 + c % 2, 0:3 * D]
                    copy(Z2[:, 0, c, j, :], z[:, 0:D], p2(-SZ))
                    copy(Z1[:, c, j, :], z[:, D:2 * D], p2(-SZ)).then_inc(s("z_hi"), 1)

            def u_hi(g):
                for i in range(NC):
                    act.wait_ge(s("u_full"), NC * g + i + 1)
                    copy(U[:, 0, i], Uf[:, i % 2]).then_inc(s("u_hi"), 1)

            def ln2_norm(g, q):
                rows = X[:, bass.ds(g * GT, GT), :].rearrange("p (b k) d -> p b k d", k=NC)[:, :, q, :]
                act.wait_ge(s("rstd2"), NC * g + q + 1)
                if q >= 2:
                    act.wait_ge(s("xn2_lo"), NC * g + q - 1)
                for c in range(GB):
                    ins = nc.scalar.activation(xn2[:, q % 2, c], rows[:, c, :], ACT.Identity, scale=rstd2[:, q, c:c + 1],
                                               bias=shift2[:, q, c:c + 1])
                ins.then_inc(s("xn2_ready"), 1)

            def ln2_hi(g, q, moved):
                act.wait_ge(s("xn2_ready"), NC * g + q + 1)
                if moved:
                    act.wait_ge(s(f"moved{q}"), MOVED * g)
                copy(payload(g)[0].bitcast(F16)[:, q * GB:(q + 1) * GB, 0:D], xn2[:, q % 2]).then_inc(s("xn2_hi"), 1)

            def rt_evac(g, q):
                act.wait_ge(s("rt_done"), NC * g + q + 1)
                copy(XR[:, q % 2].rearrange("p h t n -> p (h t n)"), ps[:, 5 + q % 2, :].bitcast(F16)).then_inc(s("rt_ready"), 1)

            def expo(g):
                act.wait_ge(s("dl_ready"), g + 1)
                nc.scalar.activation(ex[:], dl[:], ACT.Exp, scale=p2(-SW)).then_inc(s("ex_ready"), 1)

            def weights(k):
                if k < 2:
                    act.wait_ge(s("in_f"), 16 * (k + 1))
                    src = stage[:, 0:E * HID].rearrange("p (e h) -> p e h", e=E)
                    copy((W1, W3)[k][:, 0, :, 0:HID], src, p2(SW)).then_inc(s("f_hi"), 1)
                else:
                    act.wait_ge(s("in_f"), 16 * (2 + HC))
                    act.wait_ge(s("zero_w"), 1)
                    for c in range(HC):
                        n = min(P, HID - c * P)
                        src = stage[0:n, c * E * D:(c + 1) * E * D].rearrange("p (e d) -> p e d", e=E)
                        ins = copy(W2[0:n, 0, :, c, :], src, p2(SW))
                    ins.then_inc(s("f_hi"), 1)

            def body(g, tail, moved):
                for j in range(GB):
                    b = g * GB + j
                    xt_evac(b, j % 2)
                    if tail and j == 2:
                        ln2_norm(g - 1, 2)
                    if tail and j == 2:
                        v_hi(b, j % 2, 0)
                        ln2_hi(g - 1, 2, moved)
                        v_hi(b, j % 2, 1)
                        z_hi(b - 1, j - 1, (0,))
                        ln1_norm(b + 1, (j + 1) % 2)
                        z_hi(b - 1, j - 1, (1,))
                        ln1_hi(b + 1, (j + 1) % 2)
                    else:
                        ln1_norm(b + 1, (j + 1) % 2)
                        v_hi(b, j % 2, 0)
                        ln1_hi(b + 1, (j + 1) % 2)
                        if tail and j == 3:
                            rt_evac(g - 1, 2)
                            rt_evac(g - 1, 3)
                        v_hi(b, j % 2, 1)
                    if not tail and j == 0:
                        power_hi(2, 0)
                        power_hi(2, 1)
                        weights(0)
                        power_hi(2, 2)
                        power_hi(2, 3)
                    if tail and j == 0:
                        u_hi(g - 1)
                    if j and not (tail and j == 2):
                        z_hi(b - 1, j - 1, (0, 1))
                    if tail and j == 3:
                        expo(g - 1)
                    if j:
                        z_hi(b - 1, j - 1, (2, 3))
                    if tail and j == 2:
                        ln2_norm(g - 1, 3)
                    if tail and j == 1:
                        ln2_norm(g - 1, 0)
                        ln2_hi(g - 1, 0, moved)
                        ln2_norm(g - 1, 1)
                        ln2_hi(g - 1, 1, moved)
                    if tail and j == 2:
                        rt_evac(g - 1, 0)
                        rt_evac(g - 1, 1)
                        ln2_hi(g - 1, 3, moved)
                    if not tail and j in (1, 2):
                        weights(j)
                z_hi(g * GB + 3, 3, range(NC))

            body(0, False, False)
            body(1, True, False)
            with act.Fori(2, NG) as g:
                body(g, True, True)
            u_hi(NG - 1)

            expert = [act.alloc_register(f"act_expert{u}") for u in range(UNROLL)]

            def xt(t, u):
                q = u % 2
                act.wait_ge(s("fx_done"), t + 1)
                copy(XTf[:, q], ps[:, 3, 0:SLOT].bitcast(F16).rearrange("p (h s) -> p h s", h=2)).then_inc(s("fx_ready"), 1)
                act.reg_load(expert[u], tabi[0:1, 1, t:t + 1] if isinstance(t, int) else tabi[0:1, 1, bass.ds(t, 1)])

            ln2_norm(NG - 1, 0)
            ln2_hi(NG - 1, 0, False)
            act.wait_ge(s("table"), 1)
            xt(0, 0)
            ln2_norm(NG - 1, 1)
            ln2_hi(NG - 1, 1, False)

            def between(t):
                if t < 2:
                    ln2_norm(NG - 1, t + 2)
                    ln2_hi(NG - 1, t + 2, False)
                if t == 2:
                    rt_evac(NG - 1, 0)
                    rt_evac(NG - 1, 1)
                if t == 3:
                    rt_evac(NG - 1, 2)
                    rt_evac(NG - 1, 3)
                if t == 5:
                    expo(NG - 1)

            def silu(t, q):
                for c in range(HC):
                    act.wait_ge(s(f"h_done{c}"), t + 1)
                    nc.scalar.activation(sil[:, q, c], ps[:, c, 0:SLOT], ACT.Silu,
                                         scale=p2(-SW)).then_inc(s(f"sil{c}"), 1)
                hidden_hi(t, q, range(HC))

            def hidden_hi(t, q, cs):
                for c in cs:
                    act.wait_ge(s(f"h_whole{c}"), t + 1)
                    copy(Hh[:, q, 0, c], hf[:, q, c]).then_inc(s(f"h_hi{c}"), 1)

            def y_out(t, u):
                e = act.snap(expert[u], min_val=0, max_val=E - 1)
                act.wait_ge(s("y_done"), t + 1)
                if not (isinstance(t, int) and t < NY):
                    act.wait_ge(s(f"added{u % NY}"), y_free(t, u))
                for a in range(2):
                    ins = nc.scalar.activation(Y[:, u % NY, a], ps[:, 4, a * D:(a + 1) * D], ACT.Identity,
                                               scale=XSf[:, u, a, bass.ds(e + (D + 1), 1)])
                ins.then_inc(s("y_ready"), 1)

            tiles_loop(act, xt, lambda t, u: silu(t, u % 2), y_out, between)

        @block.vector
        def _(dve):
            v = nc.vector
            tiny = lambda: v.tensor_copy(spare[:, 0:1], spare[:, 1:2])
            v.memset(spare[:, 0:2], 0.0).then_inc(s("spare"), 1)
            dve.wait_ge(s("spare"), 1)

            def ln_stats(rows, q, name, index, st, m, ne, va, out_sem):
                st_, m_, va_ = st[:, q], m[:, q], va[:, q]
                steps = Steps(dve, s(name), index, 2)
                tiny()
                for c in range(NC):
                    ins = v.bn_stats(st_[:, c, :], rows(c))
                steps.done(ins)
                steps.wait_apart(tiny)
                for c in range(NC):
                    ins = v.bn_aggr(m_[:, c, :], st_[:, c, :])
                steps.done(ins)
                steps.wait()
                v.tensor_scalar(ne[:, q], m_[:, :, 0], -1.0, None, ALU.mult)
                v.tensor_scalar(va_, m_[:, :, 1], EPS, None, ALU.add).then_inc(s(out_sem), 1)
                steps.end()

            def ln1_stats(b, q):
                ln_stats(lambda c: X[:, b * NC + c, :] if isinstance(b, int) else X[:, bass.ds(b * NC + c, 1), :].rearrange("p a d -> p (a d)"),
                         q, "ln1_st", b, stats, mv, negm, var, "var")

            w = Steps(dve, s("w_steps"), 0, 18)
            dve.wait_ge(s("in_w"), 80)
            w.done(v.tensor_scalar(dcol[:, 1:2], dcol[:, 0:1], 0.0, 1.0, ALU.max, ALU.min))
            v.tensor_scalar(idt, ident32, 1.0 - DT, None, ALU.mult)
            w.done(v.tensor_copy(Wp[:, 0], ident32))
            w.wait()
            v.tensor_scalar(wd, wt, dcol[:, 1:2], None, ALU.mult).then_inc(s("wd"), 1)
            dve.wait_ge(s("wp_done"), 1)
            v.scalar_tensor_tensor(Wp[:, 1], ps[:, 7, 0:D], DT, idt, ALU.mult, ALU.add).then_inc(s("wp"), 1)
            dve.wait_ge(s("wp_done"), 2)
            v.tensor_copy(Wp[:, 2], ps[:, 6, 0:D]).then_inc(s("wp"), 1)
            dve.wait_ge(s("wp_done"), 3)
            v.tensor_copy(Wp[:, 3:5], ps[:, 5, 0:2 * D].rearrange("p (a d) -> p a d", a=2)).then_inc(s("wp"), 1)
            a = Steps(dve, s("a_steps"), 0, 1)
            dve.wait_ge(s("sig"), 1)
            for k in range(NC):
                blk = adjT[:, k, k * P:(k + 1) * P]
                ins = v.tensor_tensor(blk, blk, ident32, ALU.subtract)
            a.done(ins)
            a.wait()
            v.scalar_tensor_tensor(adjT, adjT, DT * 0.5 * p2(SA[1]), sig.unsqueeze(1).to_broadcast([P, NC, N]),
                                   ALU.mult, ALU.mult).then_inc(s("a_full"), 1)
            dve.wait_ge(s("wp_done"), 4)
            v.tensor_copy(Wp[:, 5:9], ps[:, 4, 0:4 * D].rearrange("p (a d) -> p a d", a=4)).then_inc(s("wp"), 1)
            dve.wait_ge(s("sig"), 2)
            v.tensor_scalar(sigc[:], sigc[:], DT * 0.5 * p2(SA[1]), None, ALU.mult)
            for k in range(NC):
                blk = adjN[:, k, k * P:(k + 1) * P]
                ins = v.tensor_tensor(blk, blk, ident32, ALU.subtract)
            ins.then_inc(s("a_full"), 1)
            dve.wait_ge(s("a_hi"), 1)
            v.tensor_tensor(B[:, 0, 1], adjT, B[:, 0, 0], ALU.subtract).then_inc(s("a_split"), 1)
            dve.wait_ge(s("a_full"), 2)
            dve.wait_ge(s("a_hi"), 2)
            for k in range(NC):
                ins = v.scalar_tensor_tensor(An[:, 1, k], adjN[:, k, :], sigc[:, k:k + 1], An[:, 0, k], ALU.mult, ALU.subtract)
            ins.then_inc(s("a_split"), 1)
            dve.wait_ge(s("bw_done"), 1)
            v.tensor_tensor(bt[:], ps[:, 7, 256:265], k32[:, C_BIN:C_BIN + 9], ALU.mult).then_inc(s("bt"), 1)
            dve.wait_ge(s("in_x"), 16)
            ln1_stats(0, 0)
            ln1_stats(1, 1)
            dve.wait_ge(s("in_c"), 16)
            w.done(v.tensor_scalar(wr16[:, 0], wr32[:], p2(SW), None, ALU.mult))
            w.wait()
            v.scalar_tensor_tensor(wr16[:, 1], wr32[:], p2(SW), wr16[:, 0], ALU.mult, ALU.subtract).then_inc(s("router"), 1)
            def power_lo(j, i):
                dve.wait_ge(s("pow_hi"), (j - 1) * NC + i + 1)
                v.scalar_tensor_tensor(B[:, j, 1, i], ps[:, 4 + i, :], p2(SA[j + 1] - SA[1] - SA[j]), B[:, j, 0, i],
                                       ALU.mult, ALU.subtract).then_inc(s("pow_split"), 1)

            dve.wait_ge(s("fw_done"), 3)
            for p in range(9):
                i, r = divmod(8 - p, 3)
                ins = v.tensor_scalar(Gf[:, r, 2 - i], ps[:, 1 + p // 3, (p % 3) * D:(p % 3 + 1) * D],
                                      comb(STEPS, p) * p2(SZ - SV[r]), None, ALU.mult)
            ins.then_inc(s("g_psum"), 1)
            dve.wait_ge(s("g_psum"), 1)
            for p in range(STEPS):
                for j in range(STEPS - p):
                    i, r = divmod(j, 3)
                    ins = v.scalar_tensor_tensor(Gf[:, r, 2 - i], Wp[:, p], DT * comb(p + j, j) * p2(SZ - SV[r]),
                                                 Gf[:, r, 2 - i], ALU.mult, ALU.add)
                w.done(ins)
                if p % 2:
                    power_lo(1, p // 2)
                w.wait()
            w.done(v.tensor_copy(G16[:, 0], Gf))
            w.wait()
            v.tensor_tensor(G16[:, 1], Gf, G16[:, 0], ALU.subtract).then_inc(s("g_split"), 1)

            def u_split(a0, a1):
                w.done(v.tensor_copy(u16[:, 0, :, a0:a1], uall[:, :, a0:a1]))
                w.wait()
                v.tensor_tensor(u16[:, 1, :, a0:a1], uall[:, :, a0:a1], u16[:, 0, :, a0:a1], ALU.subtract).then_inc(s("u_split"), 1)

            def columns(n):
                dve.wait_ge(s("us_done"), n + 1)
                if n == 0:
                    dve.wait_ge(s("u0"), 1)
                    for r in range(2):
                        ins = v.tensor_scalar(uall[:, :, r + 1:r + 2], ps[:, 3, 0:8].rearrange("p (i r) -> p i r", r=2)[:, :, r:r + 1],
                                              p2(SU - SA[r + 1]), None, ALU.mult)
                    w.done(ins)
                else:
                    ins = v.tensor_scalar(uall[:, :, 3 * n:3 * n + 3], ps[:, 3, 12 * n:12 * n + 12].rearrange("p (i r) -> p i r", r=3),
                                          p2(-SA[3]), None, ALU.mult)
                    if n == 2:
                        ins.then_inc(s("columns"), 1)
                    else:
                        w.done(ins)
                if n < 2:
                    w.wait()
                    u_split(3 * n, 3 * n + 3)

            def bias_parts():
                dve.wait_ge(s("ut_done"), 1)
                v.tensor_copy(ut, ps[0:9, 4, :])
                v.tensor_copy(btT[:], ps[0:9, 5, 0:D]).then_inc(s("bias_parts"), 1)

            def bias_whole():
                dve.wait_ge(s("bias_done"), 1)
                v.tensor_copy(biasf[:], ps[:, 6, :].rearrange("p (k d) -> p k d", k=NC)).then_inc(s("bias"), 1)

            v.tensor_copy(run[:], k32[:, C_EB:C_EB + E]).then_inc(s("route"), 1)
            w.done(v.tensor_copy(tok[:], k32[:, C_TOK:C_TOK + GT]))
            w.wait()
            dve.wait_ge(s("zero_x"), 1)
            dve.wait_ge(s("zero_out"), 1)
            for name in ("added0", "added1", "moved_last"):
                dve.wait_ge(s(name), FIRST)

            def v_lo(b, q, r):
                dve.wait_ge(s("v_hi"), 2 * b + r + 1)
                v.scalar_tensor_tensor(V[:, q, 1, r], ps[:, 1 + r, :], p2(SV[r + 1] - SA[r + 1]), V[:, q, 0, r],
                                       ALU.mult, ALU.subtract).then_inc(s("v_split"), 1)

            def z_lo(b, j, cs):
                for c in cs:
                    if c == 0:
                        dve.wait_ge(s("x_bias"), b + 1)
                    dve.wait_ge(s("z_hi"), NC * b + c + 1)
                    z = ps[:, 3 + c % 2, 0:3 * D]
                    if isinstance(b, int):
                        row = X[:, b * NC + c, :]
                    else:
                        row = X[:, bass.ds(b * NC + c, 1), :].rearrange("p a d -> p (a d)")
                    v.scalar_tensor_tensor(row, z[:, 2 * D:3 * D], p2(-SZ), row, ALU.mult, ALU.add)
                    v.scalar_tensor_tensor(Z2[:, 1, c, j, :], z[:, 0:D], p2(-SZ), Z2[:, 0, c, j, :],
                                           ALU.mult, ALU.subtract).then_inc(s("z_split"), 1)

            def u_all(g):
                def lo(i):
                    dve.wait_ge(s("u_hi"), NC * g + i + 1)
                    v.tensor_tensor(U[:, 1, i], Uf[:, i % 2], U[:, 0, i], ALU.subtract).then_inc(s("u_lo"), 1)
                for i in range(NC):
                    dve.wait_ge(s("s2_done"), 2 * NC * g + i + 1)
                    if i >= 2:
                        dve.wait_ge(s("u_lo"), NC * g + i - 1)
                    v.scalar_tensor_tensor(Uf[:, i % 2], ps[:, u_bank(g, i), :], p2(-SA[3]), Z1[:, i].rearrange("p b d -> p (b d)"),
                                           ALU.mult, ALU.add).then_inc(s("u_full"), 1)
                    if i:
                        lo(i - 1)
                lo(NC - 1)

            def x2_chunk(g, q):
                st = Steps(dve, s("x2_steps"), g * NC + q, 1)
                dve.wait_ge(s("s2_done"), 2 * NC * g + NC + q + 1)
                rows = X[:, bass.ds(g * GT, GT), :].rearrange("p (b k) d -> p b k d", k=NC)[:, :, q, :]
                st.done(v.scalar_tensor_tensor(rows, ps[:, 5 + q % 2, :].rearrange("p (b d) -> p b d", b=GB), p2(-SA[3]), rows,
                                               ALU.mult, ALU.add))
                st.wait()
                row = lambda c: rows[:, c, :]
                ln_stats(row, q, "ln2_st", g * NC + q, stats2, mv2, negm2, var2, "var2")

            def ln2_lo(g, q):
                dve.wait_ge(s("xn2_hi"), NC * g + q + 1)
                rows = payload(g)[0].bitcast(F16)[:, q * GB:(q + 1) * GB, :]
                v.tensor_tensor(rows[:, :, D:2 * D], xn2[:, q % 2], rows[:, :, 0:D],
                                ALU.subtract).then_inc(s("xn2_lo"), 1)

            lg = psR[:, 0:P].rearrange("p (t e) -> p t e", e=E)
            iom = k32[:, C_IOM:C_IOM + E].unsqueeze(1).to_broadcast([P, GT, E])
            wide = lambda a: a.unsqueeze(2).to_broadcast([P, GT, E])

            def first_choice(g):
                st = Steps(dve, s("first"), g, 4)
                dve.wait_ge(s("logits"), g + 1)
                st.done(v.tensor_reduce(mx[:], lg, AX, ALU.max))
                st.wait()
                v.tensor_tensor(dl[:], lg, wide(mx[:]), ALU.subtract).then_inc(s("dl_ready"), 1)
                dve.wait_ge(s("dl_ready"), g + 1)
                st.done(v.scalar_tensor_tensor(key[:], dl[:], 0.0, iom, ALU.is_equal, ALU.mult))
                st.wait()
                st.done(v.tensor_reduce(first[:], key[:], AX, ALU.min))
                st.wait()
                st.done(v.tensor_tensor(oh[:, 0], key[:], wide(first[:]), ALU.is_equal))
                st.end()

            def second_choice(g):
                st = Steps(dve, s("second"), g, 6)
                dve.wait_ge(s("ex_ready"), g + 1)
                dve.wait_ge(s("first"), 4 * (g + 1))
                st.done(v.scalar_tensor_tensor(rest[:], oh[:, 0], -2.0, ex[:], ALU.mult, ALU.add))
                st.wait()
                st.done(v.tensor_reduce(m2[:], rest[:], AX, ALU.max))
                v.tensor_reduce(ssum[:], ex[:], AX, ALU.add)
                st.wait()
                st.done(v.tensor_tensor(key[:], rest[:], wide(m2[:]), ALU.is_equal))
                st.wait()
                st.done(v.tensor_tensor(key[:], key[:], iom, ALU.mult))
                st.wait()
                st.done(v.tensor_reduce(first[:], key[:], AX, ALU.min))
                st.wait()
                st.done(v.tensor_tensor(oh[:, 1], key[:], wide(first[:]), ALU.is_equal))
                st.wait()
                v.tensor_tensor(M16[:].rearrange("p e t -> p t e"), oh[:, 0], oh[:, 1], ALU.add).then_inc(s("mask"), 1)
                st.end()

            def gates(g):
                st = Steps(dve, s("gates"), g, 5)
                dve.wait_ge(s("mask"), g + 1)
                st.done(v.scalar_tensor_tensor(den[:], ssum[:], 1e-9, m2[:], ALU.mult, ALU.add))
                v.tensor_tensor(rest[:], M16[:].rearrange("p e t -> p t e"), ex[:], ALU.mult)
                st.wait()
                st.done(v.tensor_scalar(den[:], den[:], 1.0, p2(SW), ALU.add, ALU.mult))
                v.tensor_copy(payload(g)[0][:, :, D], tok[:])
                st.wait()
                st.done(v.reciprocal(rden[:], den[:]))
                st.done(v.tensor_scalar(tok[:], tok[:], float(GT * P), None, ALU.add))
                st.wait()
                st.done(v.tensor_tensor(payload(g)[0].bitcast(F32)[:, :, D + 1:], rest[:], wide(rden[:]), ALU.mult))
                st.end()

            def place(g):
                st = Steps(dve, s("place"), g, 6)
                dve.wait_ge(s("prefix"), g + 1)
                total = psR[:, 2 * P:3 * P]
                before = psR[:, P:2 * P].rearrange("p (e t) -> p e t", e=E)
                st.done(v.tensor_tensor_scan(incl[:].rearrange("p e t -> p (e t)"), k32[:, C_SCAN:C_SCAN + P], total, 0.0,
                                             ALU.mult, ALU.add))
                st.wait()
                st.done(v.tensor_tensor(pos[:], incl[:], total.rearrange("p (e t) -> p e t", e=E), ALU.subtract))
                st.wait()
                st.done(v.tensor_tensor(pos[:], pos[:], before, ALU.add))
                st.wait()
                st.done(v.tensor_tensor(pos[:], pos[:], run[:].unsqueeze(2).to_broadcast([P, E, GT]), ALU.add))
                st.wait()
                v.tensor_tensor(run[:], run[:], incl[:, :, GT - 1], ALU.add)
                for k in range(2):
                    ins = v.tensor_tensor(prod[:, k], oh[:, k], pos[:].rearrange("p e t -> p t e"), ALU.mult)
                st.done(ins)
                st.wait()
                st.done(v.tensor_reduce(slotf[:].rearrange("p k t -> p (k t)"), prod[:].rearrange("p k t e -> p (k t) e"),
                                        AX, ALU.add))
                st.wait()
                dve.wait_ge(s("gates"), 5 * (g + 1))
                v.tensor_copy(payload(g)[1], slotf[:]).then_inc(s("route"), 1)
                st.end()

            def weights(k):
                dve.wait_ge(s("f_hi"), k + 1)
                if k < 2:
                    src = stage[:, 0:E * HID].rearrange("p (e h) -> p e h", e=E)
                    t = (W1, W3)[k]
                    ins = v.scalar_tensor_tensor(t[:, 1, :, 0:HID], src, p2(SW), t[:, 0, :, 0:HID], ALU.mult, ALU.subtract)
                else:
                    dve.wait_ge(s("zero_w"), 1)
                    for c in range(HC):
                        n = min(P, HID - c * P)
                        src = stage[0:n, c * E * D:(c + 1) * E * D].rearrange("p (e d) -> p e d", e=E)
                        ins = v.scalar_tensor_tensor(W2[0:n, 1, :, c, :], src, p2(SW), W2[0:n, 0, :, c, :],
                                                     ALU.mult, ALU.subtract)
                ins.then_inc(s("f_split"), 1)

            def body(g, tail):
                for j in range(GB):
                    b = g * GB + j
                    q = j % 2
                    stats_last = j == 2
                    if tail and j == 2:
                        ln2_lo(g - 1, 2)
                    v_lo(b, q, 0)
                    if j == 2:
                        dve.wait_ge(s("in_x"), 16 * (min(g + 2, NG) if isinstance(g, int) else NG))
                    if not stats_last:
                        ln1_stats(b + 2, q)
                    if not tail and j == 1:
                        columns(2)
                    if stats_last:
                        v_lo(b, q, 1)
                        z_lo(b - 1, j - 1, range(NC))
                        ln1_stats(b + 2, q)
                    else:
                        v_lo(b, q, 1)
                    if not tail and j == 0:
                        columns(0)
                        power_lo(2, 0)
                        power_lo(2, 1)
                        power_lo(2, 2)
                        power_lo(2, 3)
                        weights(0)
                        columns(1)
                    if not tail and j == 1:
                        bias_parts()
                        bias_whole()
                    if tail and j == 0:
                        u_all(g - 1)
                    if j and not stats_last:
                        z_lo(b - 1, j - 1, (0,))
                    if tail and j == 3:
                        first_choice(g - 1)
                    if j and not stats_last:
                        z_lo(b - 1, j - 1, (1, 2, 3))
                    if tail and j == 2:
                        ln2_lo(g - 1, 3)
                    if tail and j == 3:
                        second_choice(g - 1)
                    if tail and j == 1:
                        x2_chunk(g - 1, 0)
                        x2_chunk(g - 1, 1)
                        x2_chunk(g - 1, 2)
                        ln2_lo(g - 1, 0)
                        x2_chunk(g - 1, 3)
                        ln2_lo(g - 1, 1)
                    if not tail and j in (1, 2):
                        weights(j)
                z_lo(g * GB + 3, 3, (0,))
                if tail:
                    gates(g - 1)
                z_lo(g * GB + 3, 3, (1, 2, 3))
                if tail:
                    v.tensor_copy(prev[:], run[:])
                    place(g - 1)

            body(0, False)
            with dve.Fori(1, NG) as g:
                body(g, True)

            tile_no = k32[:, C_TILE:C_TILE + 1]
            first_row = k32[:, C_EB:C_EB + E]
            ones = k32[:, C_ONE:C_ONE + E]
            v.memset(cum[:], 0.0)
            v.memset(taken[:], 0.0)
            v.memset(rows_t[:], 0.0).then_inc(s("tab_zero"), 1)
            dve.wait_ge(s("tab_zero"), 1)

            def tile_counts(regions, spare_rows, st):
                st.done(v.tensor_tensor(cnt[:, 0], regions, first_row, ALU.subtract))
                st.wait()
                st.done(v.tensor_scalar(cnti[:, 0], cnt[:, 0], float(spare_rows), None, ALU.add))
                st.wait()
                st.done(v.tensor_scalar(cnti[:, 1], cnti[:, 0], SLOT.bit_length() - 1, None, ALU.logical_shift_right))
                st.wait()
                st.done(v.tensor_copy(cnt[:, 1], cnti[:, 1]))
                st.wait()

            table_steps = [Steps(dve, s(f"tab{part}"), 0, 16 if part == 2 else 18) for part in range(3)]

            def table_counts(part, regions):
                st = table_steps[part]
                if part == 2:
                    v.tensor_copy(padrow[:], run[:]).then_inc(s("regions"), 1)
                tile_counts(regions, SLOT - 1 if part == 2 else 0, st)
                st.done(v.tensor_tensor(cnt[:, 0], cnt[:, 1], taken[:, 0:E], ALU.subtract))
                st.wait()
                st.done(v.tensor_tensor_scan(cum[:, part, 1:], ones, cnt[:, 0], 0.0, ALU.mult, ALU.add))
                st.wait()
                if part < 2:
                    st.done(v.tensor_scalar(cum[:, part, 1:], cum[:, part, 1:], float(STARTS[part + 1] - STARTS[part]), None,
                                            ALU.min))
                    st.wait()
                    st.done(v.tensor_tensor(cnt[:, 0], cum[:, part, 1:], cum[:, part, 0:E], ALU.subtract))
                    st.wait()
                st.done(v.tensor_tensor(cnt[:, 1], taken[:, 0:E], cnt[:, 0], ALU.add))
                st.wait()
                st.done(v.tensor_tensor(cnt[:, 2], taken[:, 1:], cnt[:, 1], ALU.subtract))
                st.wait()
                st.done(v.tensor_scalar(cnt[:, 2], cnt[:, 2], float(SLOT), float(CAP), ALU.mult, ALU.add))
                st.wait()

            def table_places(part):
                st = table_steps[part]
                st.done(v.tensor_scalar(ind[:, 0], cum[:, part, 1:], tile_no, None, ALU.is_le))
                st.wait()
                v.tensor_tensor(ind[:, 1], ind[:, 0], cnt[:, 2], ALU.mult)
                st.done(v.tensor_tensor(ind[:, 2], ind[:, 0], cnt[:, 0], ALU.mult))
                st.wait()
                st.done(v.tensor_reduce(red[:], ind[:], AX, ALU.add))
                st.wait()
                v.tensor_scalar(rows_t[:, 1:2], red[:, 0:1], float(E - 1), None, ALU.min)
                v.tensor_scalar(tcol[:, 0:1], tile_no, cum[:, part, E:], 0.0, ALU.subtract, ALU.max)
                st.done(v.tensor_tensor(tcol[:, 1:2], red[:, 1:2], k32[:, C_TILE + 1:C_TILE + 2], ALU.add))
                st.wait()
                v.scalar_tensor_tensor(tcol[:, 2:3], taken[:, 0:1], float(SLOT), tcol[:, 1:2], ALU.mult, ALU.add)
                st.done(v.scalar_tensor_tensor(tcol[:, 3:4], red[:, 2:3], float(STARTS[part]), tcol[:, 0:1], ALU.add, ALU.add))
                st.wait()
                v.tensor_scalar(rows_t[:, 0:1], tcol[:, 2:3], float(DUMMY), None, ALU.min)
                st.done(v.tensor_scalar(twait[:], k32[:, C_BACK:C_BACK + NY], tcol[:, 3:4], None, ALU.add))
                st.wait()
                st.done(v.tensor_scalar(twait[:], twait[:], NY.bit_length() - 1, 5, ALU.logical_shift_right,
                                        ALU.logical_shift_left))
                st.wait()
                v.tensor_copy(taken[:, 0:E], cnt[:, 1])
                v.tensor_scalar(rows_t[:, 2:2 + NY], twait[:], float(FIRST), None, ALU.add).then_inc(s("tab_rows"), 1)
                st.end()

            def table_copy(part):
                a, b = STARTS[part], STARTS[part + 1]
                dve.wait_ge(s("tab_psum"), part + 1)
                v.tensor_copy(tabi[0:1, :, a:b],
                              psR[0:1, 0:COLS * (b - a)].rearrange("p (a t) -> p a t", a=COLS)).then_inc(s("table"), 1)

            table_counts(0, prev[:])
            table_places(0)
            u_all(NG - 1)
            table_copy(0)
            x2_chunk(NG - 1, 0)
            x2_chunk(NG - 1, 1)
            x2_chunk(NG - 1, 2)
            ln2_lo(NG - 1, 0)
            x2_chunk(NG - 1, 3)
            ln2_lo(NG - 1, 1)

            def between(t):
                if t < 2:
                    ln2_lo(NG - 1, t + 2)
                if t == 4:
                    st = Steps(dve, s("saved"), 0, 1)
                    st.done(v.tensor_copy(run3[:], run[:]))
                    st.wait()
                    first_choice(NG - 1)
                if t == 5:
                    second_choice(NG - 1)
                if t == 6:
                    gates(NG - 1)
                if t == 8:
                    place(NG - 1)
                if t == 9:
                    table_counts(1, run3[:])
                if t == 10:
                    table_places(1)
                if t == 12:
                    table_copy(1)
                    dve.wait_ge(s("tab_rows"), 2)
                    table_counts(2, run[:])
                if t == 13:
                    table_places(2)
                if t == 15:
                    table_copy(2)

            def hidden(t, q):
                def whole(c):
                    dve.wait_ge(s(f"sil{c}"), t + 1)
                    v.scalar_tensor_tensor(hf[:, q, c], ps[:, c, SLOT:2 * SLOT], p2(-SW), sil[:, q, c],
                                           ALU.mult, ALU.mult).then_inc(s(f"h_whole{c}"), 1)

                def lo(c):
                    dve.wait_ge(s(f"h_hi{c}"), t + 1)
                    return v.tensor_tensor(Hh[:, q, 1, c], hf[:, q, c], Hh[:, q, 0, c], ALU.subtract)

                for c in range(HC):
                    whole(c)
                for c in range(HC - 1):
                    lo(c)
                lo(HC - 1).then_inc(s("h_parts"), 1)

            tiles_loop(dve, lambda t, u: None, lambda t, u: hidden(t, u % 2), lambda t, u: None, between)

        @block.tensor
        def _(pe):
            mm = nc.tensor.matmul

            def passes(out_ap, lhs, rhs, first, last):
                mm(out_ap, lhs(0), rhs(0), start=first, stop=False)
                mm(out_ap, lhs(0), rhs(1), start=False, stop=False)
                return mm(out_ap, lhs(1), rhs(0), start=False, stop=last)

            pe.wait_ge(s("in_w"), 80)
            pe.wait_ge(s("wd"), 1)
            mm(ps[:, 7, 0:D], wd, wt, start=True, stop=True).then_inc(s("wp_done"), 1)
            pe.wait_ge(s("wp"), 1)
            mm(ps[:, 6, 0:D], Wp[:, 1], Wp[:, 1], start=True, stop=True).then_inc(s("wp_done"), 1)
            pe.wait_ge(s("wp"), 2)
            mm(ps[:, 5, 0:2 * D], Wp[:, 2], Wp[:, 1:3].rearrange("p a d -> p (a d)"), start=True, stop=True).then_inc(s("wp_done"), 1)
            pe.wait_ge(s("wp"), 3)
            mm(ps[:, 4, :], Wp[:, 4], Wp[:, 1:5].rearrange("p a d -> p (a d)"), start=True, stop=True).then_inc(s("wp_done"), 1)
            pe.wait_ge(s("wp"), 4)
            for n in range(3):
                mm(ps[:, 1 + n, 0:3 * D], fcw, Wp[:, 3 * n:3 * n + 3].rearrange("p a d -> p (a d)"),
                   start=True, stop=True).then_inc(s("fw_done"), 1)
            for j in range(9):
                ins = mm(ps[:, 7, 256 + j:257 + j], Wp[:, 8 - j], bcol[:], start=True, stop=True)
            ins.then_inc(s("bw_done"), 1)
            def power(j):
                for i in range(NC):
                    if j == 1 and i == 3:
                        pe.wait_ge(s("bt"), 1)
                    if j == 2:
                        pe.wait_ge(s("pow_split"), NC)
                    for k in range(NC):
                        ins = passes(ps[:, 4 + i, :], lambda h: An[:, h, k, i * P:(i + 1) * P], lambda h: B[:, j - 1, h, k],
                                     k == 0, k == NC - 1)
                    ins.then_inc(s("pow_done"), 1)

            def columns(n):
                if n == 0:
                    pe.wait_ge(s("pow_split"), NC)
                    for i in range(NC):
                        for r in range(2):
                            for k in range(NC):
                                for h in range(2):
                                    ins = mm(ps[:, 3, 2 * i + r:2 * i + r + 1], B[:, r, h, k, i * P:(i + 1) * P], ones16[:, 0:1],
                                             start=(k == 0 and h == 0), stop=(k == NC - 1 and h == 1))
                else:
                    pe.wait_ge(s("pow_split"), 2 * NC)
                    pe.wait_ge(s("u_split"), n)
                    for i in range(NC):
                        for k in range(NC):
                            ins = passes(ps[:, 3, 12 * n + 3 * i:12 * n + 3 * i + 3], lambda h: B[:, 2, h, k, i * P:(i + 1) * P],
                                         lambda h: u16[:, h, k, 3 * n - 3:3 * n], k == 0, k == NC - 1)
                ins.then_inc(s("us_done"), 1)

            def bias_parts():
                pe.wait_ge(s("columns"), 1)
                for i in range(NC):
                    nc.tensor.transpose(ps[0:9, 4, i * P:(i + 1) * P], uall[:, i, :], ident32)
                nc.tensor.transpose(ps[0:9, 5, 0:D], bt[:], ident32).then_inc(s("ut_done"), 1)

            def bias_whole():
                pe.wait_ge(s("bias_parts"), 1)
                for i in range(NC):
                    ins = mm(ps[:, 6, i * D:(i + 1) * D], ut[:, i * P:(i + 1) * P], btT[:], start=True, stop=True)
                ins.then_inc(s("bias_done"), 1)

            pe.wait_ge(s("a_split"), 2)
            pe.wait_ge(s("pad_st"), 16)
            power(1)

            def xt(b, q):
                pe.wait_ge(s("xn_split"), b + 1)
                if not (isinstance(b, int) and b < 1):
                    pe.wait_ge(s("xt_ready"), b)
                for h in range(2):
                    for c in range(NC):
                        ins = nc.tensor.transpose(psT[:, h, c * P:(c + 1) * P], Xh[:, q, h, c, :], ident16)
                ins.then_inc(s("xt_done"), 1)

            def vv(b, q, rs=(0, 1)):
                for r in rs:
                    if isinstance(b, int) and b < 1:
                        if r == 0:
                            pe.wait_ge(s("g_psum"), 1)
                        else:
                            pe.wait_ge(s("pow_split"), NC)
                    elif r == 0:
                        pe.wait_ge(s("v_split"), 2 * b)
                    for k in range(NC):
                        ins = passes(ps[:, 1 + r, :], lambda h: Xh[:, q, h, k, :], lambda h: B[:, r, h, k], k == 0, k == NC - 1)
                    ins.then_inc(s("v_done"), 1)

            def zz(b, q, cs=range(NC)):
                pe.wait_ge(s("xt_ready"), b + 1)
                pe.wait_ge(s("v_split"), 2 * b + 2)
                for c in cs:
                    if not (isinstance(b, int) and b < 1 and c < 2):
                        pe.wait_ge(s("z_split"), NC * b + c - 1)
                    n = slice(c * P, (c + 1) * P)
                    for r in range(3):
                        ins = passes(ps[:, 3 + c % 2, 0:3 * D], lambda h: XT[:, q, h, n] if r == 0 else V[:, q, h, r - 1, n],
                                     lambda h: G16[:, h, r].rearrange("p i d -> p (i d)"), r == 0, r == 2)
                    ins.then_inc(s("z_done"), 1)

            def s2(g, second, last=lambda: None):
                shared = not (isinstance(g, int) and g == NG - 1)
                if second:
                    src = lambda h, k: U[:, h, k]
                else:
                    src = lambda h, k: Z2[:, h, k].rearrange("p b d -> p (b d)")
                    pe.wait_ge(s("z_split"), NC * GB * (g + 1))
                for i in range(NC):
                    if i == NC - 1:
                        last()
                    if second:
                        if i < 2:
                            pe.wait_ge(s("u_full"), NC * g + i + (3 if shared else 1))
                        else:
                            pe.wait_ge(s("x2_steps"), NC * g + i - 1)
                    elif i >= 2 and shared:
                        pe.wait_ge(s("u_full"), NC * g + i - 1)
                    for k in range(NC):
                        if second and i == 0:
                            pe.wait_ge(s("u_lo"), NC * g + k + 1)
                        ins = passes(ps[:, 5 + i % 2 if second else u_bank(g, i), :], lambda h: B[:, 2, h, k, i * P:(i + 1) * P], lambda h: src(h, k),
                                     k == 0, k == NC - 1)
                    ins.then_inc(s("s2_done"), 1)

            def rt(g, q):
                pe.wait_ge(s("xn2_lo"), NC * g + q + 1)
                if q < 2:
                    pe.wait_ge(s("x2_steps"), NC * g + q + 3)
                else:
                    pe.wait_ge(s("rt_ready"), NC * g + q - 1)
                bank = ps[:, 5 + q % 2, :].bitcast(F16)
                for h in range(2):
                    for t in range(GB):
                        ins = nc.tensor.transpose(bank[:, (h * GB + t) * P:(h * GB + t + 1) * P],
                                                  payload(g)[0].bitcast(F16)[:, q * GB + t, h * D:(h + 1) * D], ident16)
                ins.then_inc(s("rt_done"), 1)

            def logits(g, q):
                pe.wait_ge(s("rt_ready"), NC * g + q + 1)
                if q == 0:
                    pe.wait_ge(s("route"), g + 1)
                for t in range(GB):
                    tt = q * GB + t
                    ins = passes(psR[:, tt * E:(tt + 1) * E], lambda h: XR[:, q % 2, h, t], lambda h: wr16[:, h], True, True)
                if q == NC - 1:
                    ins.then_inc(s("logits"), 1)

            def prefix(g):
                pe.wait_ge(s("mask"), g + 1)
                m = M16[:].rearrange("p e t -> p (e t)")
                mm(psR[:, P:2 * P], tri16, m, start=True, stop=True)
                mm(psR[:, 2 * P:3 * P], ones16, m, start=True, stop=True).then_inc(s("prefix"), 1)

            def body(g, tail):
                for j in range(GB):
                    b = g * GB + j
                    xt(b, j % 2)
                    if not tail and j == 1:
                        columns(1)
                    vv(b, j % 2, (0,))
                    if tail and j == 3:
                        logits(g - 1, 0)
                        logits(g - 1, 1)
                        rt(g - 1, 2)
                        rt(g - 1, 3)
                    if not tail and j == 1:
                        columns(2)
                    vv(b, j % 2, (1,))
                    if not tail and j == 0:
                        columns(0)
                        power(2)
                    if not tail and j == 1:
                        bias_parts()
                        pe.wait_ge(s("g_split"), 1)
                        zz(0, 0, (0,))
                        bias_whole()
                        zz(0, 0, (1, 2, 3))
                    if tail and j == 0:
                        s2(g - 1, False)
                    if tail and j == 3:
                        logits(g - 1, 2)
                        logits(g - 1, 3)
                    if j and (tail or j > 1):
                        zz(b - 1, (j - 1) % 2)
                    if tail and j == 1:
                        s2(g - 1, True)
                    if tail and j == 2:
                        rt(g - 1, 0)
                        rt(g - 1, 1)
                zz(g * GB + 3, 1, (0, 1, 2))
                if tail:
                    prefix(g - 1)
                zz(g * GB + 3, 1, (3,))

            body(0, False)
            pe.wait_ge(s("router"), 1)
            with pe.Fori(1, NG) as g:
                body(g, True)
            s2(NG - 1, False)

            def table(part):
                n = STARTS[part + 1] - STARTS[part]
                pe.wait_ge(s("tab_rows"), part + 1)
                if part > 0:
                    pe.wait_ge(s("table"), part)
                for c in range(COLS):
                    ins = mm(psR[0:1, c * n:(c + 1) * n], rows_t[0:n, c:c + 1], ident32[0:n, 0:n], start=True, stop=True)
                ins.then_inc(s("tab_psum"), 1)

            table(0)

            expert = [pe.alloc_register(f"expert{u}") for u in range(UNROLL)]

            def early(t, u):
                q = u % 2
                pe.wait_ge(s(f"xs{u}"), 16 * (t // UNROLL + 1) if isinstance(t, int) else 16 // UNROLL * (t - u) + 16)
                if not (isinstance(t, int) and t < 1):
                    pe.wait_ge(s("fx_ready"), t)
                bank = ps[:, 3, 0:SLOT].bitcast(F16)
                for h in range(2):
                    for a in range(2):
                        n = (h * 2 + a) * P
                        ins = nc.tensor.transpose(bank[:, n:n + P], XSh[:, u, a, h * D:(h + 1) * D], ident16)
                ins.then_inc(s("fx_done"), 1)
                pe.reg_load(expert[u], tabi[0:1, 1, t:t + 1] if isinstance(t, int) else tabi[0:1, 1, bass.ds(t, 1)])

            s2(NG - 1, True, lambda: early(0, 0))

            def between(t):
                if t == 2:
                    rt(NG - 1, 0)
                    rt(NG - 1, 1)
                if t == 3:
                    pe.wait_ge(s("table"), 1)
                    logits(NG - 1, 0)
                    logits(NG - 1, 1)
                    rt(NG - 1, 2)
                    rt(NG - 1, 3)
                if t == 4:
                    logits(NG - 1, 2)
                    logits(NG - 1, 3)
                if t == 7:
                    prefix(NG - 1)
                if t == 12:
                    table(1)
                if t == 15:
                    table(2)

            pe.wait_ge(s("f_split"), 3)

            def front(t, u):
                q = u % 2
                e = pe.snap(expert[u], min_val=0, max_val=E - 1)
                pe.wait_ge(s("fx_ready"), t + 1)
                for c in range(HC):
                    if not (isinstance(t, int) and t < 1):
                        pe.wait_ge(s(f"h_whole{c}"), t)
                    for n, W in enumerate((W1, W3)):
                        wp = lambda h: W[:, h, bass.ds(e, 1), c * P:(c + 1) * P].rearrange("p a h -> p (a h)")
                        o = ps[:, c, n * SLOT:(n + 1) * SLOT]
                        hi, lo = wp(0), wp(1)
                        mm(o, hi, XTf[:, q, 0], start=True, stop=False)
                        mm(o, hi, XTf[:, q, 1], start=False, stop=False)
                        ins = mm(o, lo, XTf[:, q, 0], start=False, stop=True)
                    ins.then_inc(s(f"h_done{c}"), 1)

            def back(t, u):
                q = u % 2
                e = pe.snap(expert[u], min_val=0, max_val=E - 1)
                pe.wait_ge(s("h_parts"), t + 1)
                if not (isinstance(t, int) and t < 1):
                    pe.wait_ge(s("y_ready"), t)
                for a in range(2):
                    o = ps[:, 4, a * D:(a + 1) * D]
                    for c in range(HC):
                        wp = lambda h: W2[:, h, bass.ds(e, 1), c, :].rearrange("p a d -> p (a d)")
                        ins = passes(o, lambda h: Hh[:, q, h, c, a * P:(a + 1) * P], wp, c == 0, c == HC - 1)
                ins.then_inc(s("y_done"), 1)

            tiles_loop(pe, early, front, back, between)


def kernel(x, adj, L0_gnn_alpha_train, L0_gnn_w, L0_gnn_d, L0_gnn_fc_in_w, L0_gnn_fc_in_b, L0_ffn_router_w,
           L0_ffn_w1, L0_ffn_w2, L0_ffn_w3):
    import concourse.bacc as _bacc
    from concourse.bass_utils import run_bass_kernel_spmd as _run

    f = np.ascontiguousarray
    c32, c16, pad = shape_constants()
    w1, w2, w3 = np.asarray(L0_ffn_w1), np.asarray(L0_ffn_w2), np.asarray(L0_ffn_w3)
    arrays = {
        "in_x": f(np.asarray(x)),
        "in_adj": f(np.asarray(adj)),
        "in_adj_t": f(np.asarray(adj).T),
        "in_alpha": f(np.asarray(L0_gnn_alpha_train).reshape(1, N)),
        "in_w_t": f(np.asarray(L0_gnn_w).T),
        "in_d": f(np.asarray(L0_gnn_d).reshape(D, 1)),
        "in_fc_w": f(np.asarray(L0_gnn_fc_in_w)),
        "in_fc_b": f(np.asarray(L0_gnn_fc_in_b).reshape(D, 1)),
        "in_router_t": f(np.asarray(L0_ffn_router_w).T),
        "in_w1_t": f(w1.transpose(2, 0, 1).reshape(D, E * HID)),
        "in_w3_t": f(w3.transpose(2, 0, 1).reshape(D, E * HID)),
        "in_w2_t": f(w2.transpose(2, 0, 1).reshape(HID, E * D)),
        "in_c32": c32,
        "in_c16": c16,
        "in_pad": pad,
    }
    nc = _bacc.Bacc("TRN2", target_bir_lowering=False, num_devices=1)
    args = [nc.dram_tensor(n, a.shape, mybir.dt.from_np(a.dtype), kind="ExternalInput").ap() for n, a in arrays.items()]
    out = nc.dram_tensor("out_rows", (TOKENS + SLOT, D), F32, kind="ExternalOutput").ap()
    gnn_moe_kernel(nc, *args, out)
    r = _run(nc, [arrays], core_ids=[0])
    return np.asarray(r.results[0]["out_rows"])[0:TOKENS].reshape(NB, N, D)
```
